# Optimizing a Trainium2 kernel written in Bass

```python
import numpy as np
import jax
import jax.numpy as jnp

def _softmax(x, axis=-1):
    return jax.nn.softmax(x, axis=axis)

def _gelu(x):
    return jax.nn.gelu(x, approximate=True)

def _silu(x):
    return jax.nn.silu(x)

def _sigmoid(x):
    return jax.nn.sigmoid(x)

def _layernorm(x, axis=-1, eps=1e-05):
    m = jnp.mean(x, axis=axis, keepdims=True)
    v = jnp.var(x, axis=axis, keepdims=True)
    return (x - m) / jnp.sqrt(v + eps)

def _scatter_add(tgt, idx, src, axis=0):
    return tgt.at[idx].add(src)

def _segment_sum(src, seg, n):
    return jax.ops.segment_sum(src, seg, n)
kernel_name = 'mk_gnn_ffn_d4_gnn_r16_fa0994'

def setup_inputs(seed: int=0):
    np.random.seed(seed)
    _w = jnp.asarray

    def _rec_inputs():
        import jax
        import jax.numpy as jnp
        _gk = jax.random.key(seed)
        x = -0.0003713 + 1 * jax.random.normal(jax.random.fold_in(_gk, 1), (3125, 256), jnp.float32)
        src = jax.random.randint(jax.random.fold_in(_gk, 2), (50000,), 0, 3125, jnp.int32)
        dst = jnp.minimum((3125 * jax.random.uniform(jax.random.fold_in(_gk, 3), (50000,)) ** 2.0).astype(jnp.int32), 49999)
        _o = jnp.argsort(dst, stable=True)
        src = src[_o]
        dst = dst[_o]
        edge_weight = jax.random.uniform(jax.random.fold_in(_gk, 14), (50000,), jnp.float32, 0.0, 0.999994)
        return (x, src, dst, edge_weight)
    x, src, dst, edge_weight = _rec_inputs()

    def _L0_gnn_setup():
        import jax, jax.numpy as jnp
        import numpy as np
        N_NODES = 3125
        N_EDGES = 50000
        D = 256
        L = 3
        key = jax.random.key(seed)
        k1, k2, k3, k4, k5 = jax.random.split(key, 5)
        features = jax.random.normal(k1, (N_NODES, D), dtype=jnp.float32)
        scale = 1.0 / np.sqrt(D)
        W_self = jax.random.normal(k2, (L, D, D), dtype=jnp.float32) * scale
        W_neigh = jax.random.normal(k3, (L, D, D), dtype=jnp.float32) * scale
        bias = jnp.zeros((L, D), dtype=jnp.float32)
        src = jax.random.randint(k4, (N_EDGES,), 0, N_NODES, dtype=jnp.int32)
        dst = jax.random.randint(k5, (N_EDGES,), 0, N_NODES, dtype=jnp.int32)
        return {'features': features, 'W_self': W_self, 'W_neigh': W_neigh, 'bias': bias, 'src': src, 'dst': dst}
    _L0_gnn_all = _L0_gnn_setup()
    _L0_gnn_in = {k: v for k, v in _L0_gnn_all.items() if k in ('W_self', 'W_neigh', 'bias')}
    del _L0_gnn_all

    def _L0_ffn_setup():
        import jax, jax.numpy as jnp
        import numpy as np
        D_MODEL = 256
        EXPERT_DIM = 512
        NUM_EXPERTS = 8
        TOP_K = 2
        SEQ_LEN = 128
        BATCH = 2
        key = jax.random.key(seed)
        ks = jax.random.split(key, 8)
        s = 0.02
        x = jax.random.normal(ks[0], (SEQ_LEN, BATCH, D_MODEL), dtype=jnp.float32)
        Wg = jax.random.normal(ks[1], (D_MODEL, NUM_EXPERTS), dtype=jnp.float32) * s
        bg = jax.random.normal(ks[2], (NUM_EXPERTS,), dtype=jnp.float32) * s
        bias = jnp.zeros((NUM_EXPERTS,), dtype=jnp.float32)
        W1 = jax.random.normal(ks[3], (NUM_EXPERTS, D_MODEL, EXPERT_DIM), dtype=jnp.float32) * s
        b1 = jax.random.normal(ks[4], (NUM_EXPERTS, EXPERT_DIM), dtype=jnp.float32) * s
        W2 = jax.random.normal(ks[5], (NUM_EXPERTS, EXPERT_DIM, D_MODEL), dtype=jnp.float32) * s
        b2 = jax.random.normal(ks[6], (NUM_EXPERTS, D_MODEL), dtype=jnp.float32) * s
        return {'x': x, 'Wg': Wg, 'bg': bg, 'bias': bias, 'W1': W1, 'b1': b1, 'W2': W2, 'b2': b2}
    _L0_ffn_all = _L0_ffn_setup()
    _L0_ffn_in = {k: v for k, v in _L0_ffn_all.items() if k in ('Wg', 'bg', 'bias', 'W1', 'b1', 'W2', 'b2')}
    del _L0_ffn_all

    def _L1_gnn_setup():
        import jax, jax.numpy as jnp
        import numpy as np
        NEG_SLOPE = 0.01

        def _leaky(x):
            return jnp.where(x >= 0, x, NEG_SLOPE * x)

        def _gcn(x, W, b, src, dst, w, n):
            h = x @ W
            agg = jax.ops.segment_sum(w[:, None] * h[src], dst, num_segments=n)
            return agg + b
        key = jax.random.key(seed)
        ks = jax.random.split(key, 10)
        N, E, IN, HID, OUT, B = (6250, 18750, 256, 256, 256, 128)
        features = jax.random.normal(ks[0], (N, IN), dtype=jnp.float32)
        values = jax.random.uniform(ks[1], (E,), dtype=jnp.float32)
        s = 1.0 / np.sqrt(IN)
        W1 = jax.random.normal(ks[2], (IN, HID), dtype=jnp.float32) * s
        b1 = jnp.zeros((HID,), dtype=jnp.float32)
        W2 = jax.random.normal(ks[3], (HID + IN, OUT), dtype=jnp.float32) * (1.0 / np.sqrt(HID + IN))
        b2 = jnp.zeros((OUT,), dtype=jnp.float32)
        Wl = jax.random.normal(ks[4], (HID + OUT, IN), dtype=jnp.float32) * (1.0 / np.sqrt(HID + OUT))
        bl = jnp.zeros((IN,), dtype=jnp.float32)
        adjs = jax.random.randint(ks[5], (2, E), 0, N, dtype=jnp.int64)
        batch = jnp.sort(jax.random.randint(ks[6], (N,), 0, B, dtype=jnp.int64))
        root_idx = jax.random.randint(ks[7], (B,), 0, N, dtype=jnp.int64)
        return {'features': features, 'values': values, 'W1': W1, 'b1': b1, 'W2': W2, 'b2': b2, 'Wl': Wl, 'bl': bl, 'adjs': adjs, 'batch': batch, 'root_idx': root_idx}
    _L1_gnn_all = _L1_gnn_setup()
    _L1_gnn_in = {k: v for k, v in _L1_gnn_all.items() if k in ('W1', 'b1', 'W2', 'b2', 'Wl', 'bl', 'root_idx')}
    del _L1_gnn_all

    def _L1_ffn_setup():
        import jax, jax.numpy as jnp
        import numpy as np
        E, D, H, TOP_K = (6, 256, 256, 2)
        ROUTER_H = D // 2
        key = jax.random.key(seed)
        ks = jax.random.split(key, 12)
        s = 1.0 / np.sqrt(D)
        sh = 1.0 / np.sqrt(H)
        sr = 1.0 / np.sqrt(ROUTER_H)
        return {'features': jax.random.normal(ks[0], (8, 256, D), dtype=jnp.float32), 'router_w1': jax.random.uniform(ks[1], (D, ROUTER_H), jnp.float32, -s, s), 'router_b1': jnp.zeros((ROUTER_H,), jnp.float32), 'router_w2': jax.random.uniform(ks[2], (ROUTER_H, E), jnp.float32, -sr, sr), 'router_b2': jnp.zeros((E,), jnp.float32), 'expert_w1': jax.random.uniform(ks[3], (E, D, H), jnp.float32, -s, s), 'expert_b1': jnp.zeros((E, H), jnp.float32), 'expert_w2': jax.random.uniform(ks[4], (E, H, H), jnp.float32, -sh, sh), 'expert_b2': jnp.zeros((E, H), jnp.float32), 'expert_w3': jax.random.uniform(ks[5], (E, H, D), jnp.float32, -sh, sh), 'expert_b3': jnp.zeros((E, D), jnp.float32)}
    _L1_ffn_all = _L1_ffn_setup()
    _L1_ffn_in = {k: v for k, v in _L1_ffn_all.items() if k in ('router_w1', 'router_b1', 'router_w2', 'router_b2', 'expert_w1', 'expert_b1', 'expert_w2', 'expert_b2', 'expert_w3', 'expert_b3')}
    del _L1_ffn_all

    def _L2_gnn_setup():
        import jax, jax.numpy as jnp
        import numpy as np
        N_NODES = 3125
        N_EDGES = 50000
        IN_F = 256
        HEADS = 4
        OUT_F = 64
        NEG_SLOPE = 0.2
        key = jax.random.key(seed)
        k1, k2, k3, k4, k5 = jax.random.split(key, 5)
        x = jax.random.normal(k1, (N_NODES, IN_F), dtype=jnp.float32)
        edge_index = jax.random.randint(k2, (2, N_EDGES), 0, N_NODES, dtype=jnp.int64)
        W = jax.random.normal(k3, (IN_F, HEADS * OUT_F), dtype=jnp.float32) * (1.0 / np.sqrt(IN_F))
        att_src = jax.random.normal(k4, (1, HEADS, OUT_F), dtype=jnp.float32) * (1.0 / np.sqrt(OUT_F))
        att_dst = jax.random.normal(k5, (1, HEADS, OUT_F), dtype=jnp.float32) * (1.0 / np.sqrt(OUT_F))
        bias = jnp.zeros((HEADS * OUT_F,), dtype=jnp.float32)
        return {'x': x, 'edge_index': edge_index, 'W': W, 'att_src': att_src, 'att_dst': att_dst, 'bias': bias}
    _L2_gnn_all = _L2_gnn_setup()
    _L2_gnn_in = {k: v for k, v in _L2_gnn_all.items() if k in ('W', 'att_src', 'att_dst', 'bias')}
    del _L2_gnn_all

    def _L2_ffn_setup():
        import jax, jax.numpy as jnp
        import numpy as np
        B, K, D = (512, 16, 256)
        E = 32
        H = int(D * 0.25)
        key = jax.random.key(seed)
        ks = jax.random.split(key, 7)
        d_rs = D ** (-0.5)
        h_rs = H ** (-0.5)
        x = jax.random.normal(ks[0], (B, K, D), dtype=jnp.float32)
        router_w = jax.random.uniform(ks[1], (E, D), jnp.float32, -d_rs, d_rs)
        router_b = jax.random.uniform(ks[2], (E,), jnp.float32, -d_rs, d_rs)
        W1 = jax.random.uniform(ks[3], (E, D, H), jnp.float32, -h_rs, h_rs)
        b1 = jax.random.uniform(ks[4], (E, H), jnp.float32, -h_rs, h_rs)
        W2 = jax.random.uniform(ks[5], (E, H, D), jnp.float32, -d_rs, d_rs)
        b2 = jax.random.uniform(ks[6], (E, D), jnp.float32, -d_rs, d_rs)
        return {'x': x, 'router_w': router_w, 'router_b': router_b, 'W1': W1, 'b1': b1, 'W2': W2, 'b2': b2}
    _L2_ffn_all = _L2_ffn_setup()
    _L2_ffn_in = {k: v for k, v in _L2_ffn_all.items() if k in ('router_w', 'router_b', 'W1', 'b1', 'W2', 'b2')}
    del _L2_ffn_all

    def _L3_gnn_setup():
        import jax, jax.numpy as jnp
        import numpy as np
        N_NODES = 625
        N_EDGES = 20000
        D = 256
        key = jax.random.key(seed)
        k1, k2, k3, k4, k5 = jax.random.split(key, 5)
        x = jax.random.normal(k1, (N_NODES, D), dtype=jnp.float32)
        src = jax.random.randint(k2, (N_EDGES,), 0, N_NODES, dtype=jnp.int32)
        dst = jax.random.randint(k3, (N_EDGES,), 0, N_NODES, dtype=jnp.int32)
        s = 1.0 / np.sqrt(D)
        theta_w = jax.random.uniform(k4, (D, D), jnp.float32, -s, s)
        theta_b = jnp.zeros((D,), jnp.float32)
        phi_w = jax.random.uniform(k5, (D, D), jnp.float32, -s, s)
        phi_b = jnp.zeros((D,), jnp.float32)
        return {'x': x, 'src': src, 'dst': dst, 'theta_w': theta_w, 'theta_b': theta_b, 'phi_w': phi_w, 'phi_b': phi_b}
    _L3_gnn_all = _L3_gnn_setup()
    _L3_gnn_in = {k: v for k, v in _L3_gnn_all.items() if k in ('theta_w', 'theta_b', 'phi_w', 'phi_b')}
    del _L3_gnn_all

    def _L3_ffn_setup():
        import jax, jax.numpy as jnp
        import numpy as np
        B, A = (256, 8)
        IN, OUT = (256, 256)
        SH1, SH2 = (256, 128)
        EH1, EH2 = (128, 64)
        E, TOPK = (4, 2)

        def _shared_mlp(x, W1, b1, W2, b2, W3, b3):
            h = jax.nn.relu(x @ W1 + b1)
            h = jax.nn.relu(h @ W2 + b2)
            return h @ W3 + b3

        def _experts_mlp(x, eW1, eb1, eW2, eb2, eW3, eb3):
            h = jax.nn.relu(jnp.einsum('baf,efh->ebah', x, eW1) + eb1[:, None, None, :])
            h = jax.nn.relu(jnp.einsum('ebah,ehg->ebag', h, eW2) + eb2[:, None, None, :])
            o = jnp.einsum('ebag,ego->ebao', h, eW3) + eb3[:, None, None, :]
            return jnp.moveaxis(o, 0, -1)
        key = jax.random.key(seed)
        ks = jax.random.split(key, 16)
        s = 0.05
        return {'x': jax.random.normal(ks[0], (B, A, IN), jnp.float32), 'sW1': jax.random.normal(ks[1], (IN, SH1), jnp.float32) * s, 'sb1': jnp.zeros((SH1,), jnp.float32), 'sW2': jax.random.normal(ks[2], (SH1, SH2), jnp.float32) * s, 'sb2': jnp.zeros((SH2,), jnp.float32), 'sW3': jax.random.normal(ks[3], (SH2, OUT), jnp.float32) * s, 'sb3': jnp.zeros((OUT,), jnp.float32), 'eW1': jax.random.normal(ks[4], (E, IN, EH1), jnp.float32) * s, 'eb1': jnp.zeros((E, EH1), jnp.float32), 'eW2': jax.random.normal(ks[5], (E, EH1, EH2), jnp.float32) * s, 'eb2': jnp.zeros((E, EH2), jnp.float32), 'eW3': jax.random.normal(ks[6], (E, EH2, OUT), jnp.float32) * s, 'eb3': jnp.zeros((E, OUT), jnp.float32), 'gW': jax.random.normal(ks[7], (IN, E), jnp.float32) * s, 'gb': jnp.zeros((E,), jnp.float32)}
    _L3_ffn_all = _L3_ffn_setup()
    _L3_ffn_in = {k: v for k, v in _L3_ffn_all.items() if k in ('sW1', 'sb1', 'sW2', 'sb2', 'sW3', 'sb3', 'eW1', 'eb1', 'eW2', 'eb2', 'eW3', 'eb3', 'gW', 'gb')}
    del _L3_ffn_all
    return {'x': x, 'src': src, 'dst': dst, 'edge_weight': edge_weight, 'L0_gnn_W_self': _L0_gnn_in['W_self'], 'L0_gnn_W_neigh': _L0_gnn_in['W_neigh'], 'L0_gnn_bias': _L0_gnn_in['bias'], 'L0_ffn_Wg': _L0_ffn_in['Wg'], 'L0_ffn_bg': _L0_ffn_in['bg'], 'L0_ffn_bias': _L0_ffn_in['bias'], 'L0_ffn_W1': _L0_ffn_in['W1'], 'L0_ffn_b1': _L0_ffn_in['b1'], 'L0_ffn_W2': _L0_ffn_in['W2'], 'L0_ffn_b2': _L0_ffn_in['b2'], 'L1_gnn_W1': _L1_gnn_in['W1'], 'L1_gnn_b1': _L1_gnn_in['b1'], 'L1_gnn_W2': _L1_gnn_in['W2'], 'L1_gnn_b2': _L1_gnn_in['b2'], 'L1_gnn_Wl': _L1_gnn_in['Wl'], 'L1_gnn_bl': _L1_gnn_in['bl'], 'L1_gnn_root_idx': _L1_gnn_in['root_idx'], 'L1_ffn_router_w1': _L1_ffn_in['router_w1'], 'L1_ffn_router_b1': _L1_ffn_in['router_b1'], 'L1_ffn_router_w2': _L1_ffn_in['router_w2'], 'L1_ffn_router_b2': _L1_ffn_in['router_b2'], 'L1_ffn_expert_w1': _L1_ffn_in['expert_w1'], 'L1_ffn_expert_b1': _L1_ffn_in['expert_b1'], 'L1_ffn_expert_w2': _L1_ffn_in['expert_w2'], 'L1_ffn_expert_b2': _L1_ffn_in['expert_b2'], 'L1_ffn_expert_w3': _L1_ffn_in['expert_w3'], 'L1_ffn_expert_b3': _L1_ffn_in['expert_b3'], 'L2_gnn_W': _L2_gnn_in['W'], 'L2_gnn_att_src': _L2_gnn_in['att_src'], 'L2_gnn_att_dst': _L2_gnn_in['att_dst'], 'L2_gnn_bias': _L2_gnn_in['bias'], 'L2_ffn_router_w': _L2_ffn_in['router_w'], 'L2_ffn_router_b': _L2_ffn_in['router_b'], 'L2_ffn_W1': _L2_ffn_in['W1'], 'L2_ffn_b1': _L2_ffn_in['b1'], 'L2_ffn_W2': _L2_ffn_in['W2'], 'L2_ffn_b2': _L2_ffn_in['b2'], 'L3_gnn_theta_w': _L3_gnn_in['theta_w'], 'L3_gnn_theta_b': _L3_gnn_in['theta_b'], 'L3_gnn_phi_w': _L3_gnn_in['phi_w'], 'L3_gnn_phi_b': _L3_gnn_in['phi_b'], 'L3_ffn_sW1': _L3_ffn_in['sW1'], 'L3_ffn_sb1': _L3_ffn_in['sb1'], 'L3_ffn_sW2': _L3_ffn_in['sW2'], 'L3_ffn_sb2': _L3_ffn_in['sb2'], 'L3_ffn_sW3': _L3_ffn_in['sW3'], 'L3_ffn_sb3': _L3_ffn_in['sb3'], 'L3_ffn_eW1': _L3_ffn_in['eW1'], 'L3_ffn_eb1': _L3_ffn_in['eb1'], 'L3_ffn_eW2': _L3_ffn_in['eW2'], 'L3_ffn_eb2': _L3_ffn_in['eb2'], 'L3_ffn_eW3': _L3_ffn_in['eW3'], 'L3_ffn_eb3': _L3_ffn_in['eb3'], 'L3_ffn_gW': _L3_ffn_in['gW'], 'L3_ffn_gb': _L3_ffn_in['gb']}

def reference(x, src, dst, edge_weight, L0_gnn_W_self, L0_gnn_W_neigh, L0_gnn_bias, L0_ffn_Wg, L0_ffn_bg, L0_ffn_bias, L0_ffn_W1, L0_ffn_b1, L0_ffn_W2, L0_ffn_b2, L1_gnn_W1, L1_gnn_b1, L1_gnn_W2, L1_gnn_b2, L1_gnn_Wl, L1_gnn_bl, L1_gnn_root_idx, L1_ffn_router_w1, L1_ffn_router_b1, L1_ffn_router_w2, L1_ffn_router_b2, L1_ffn_expert_w1, L1_ffn_expert_b1, L1_ffn_expert_w2, L1_ffn_expert_b2, L1_ffn_expert_w3, L1_ffn_expert_b3, L2_gnn_W, L2_gnn_att_src, L2_gnn_att_dst, L2_gnn_bias, L2_ffn_router_w, L2_ffn_router_b, L2_ffn_W1, L2_ffn_b1, L2_ffn_W2, L2_ffn_b2, L3_gnn_theta_w, L3_gnn_theta_b, L3_gnn_phi_w, L3_gnn_phi_b, L3_ffn_sW1, L3_ffn_sb1, L3_ffn_sW2, L3_ffn_sb2, L3_ffn_sW3, L3_ffn_sb3, L3_ffn_eW1, L3_ffn_eb1, L3_ffn_eW2, L3_ffn_eb2, L3_ffn_eW3, L3_ffn_eb3, L3_ffn_gW, L3_ffn_gb):
    import jax
    import jax.numpy as jnp

    def _L0_gnn_ref(features, W_self, W_neigh, bias, src, dst):
        import jax, jax.numpy as jnp
        import numpy as np
        N_NODES = 3125
        N_EDGES = 50000
        D = 256
        L = 3
        "3-layer GraphSAGE encoder (DGL SAGEConv, mean aggregator), eval mode.\n\n            Per layer: h_neigh = mean over in-neighbors of h (messages src -> dst);\n                       out = h @ W_self + h_neigh @ W_neigh + bias; relu except last.\n            feat_drop / wrapper dropout are identity in eval mode. The wrapper's relu\n            after layers 0,1 is idempotent with SAGEConv's internal relu.\n            "
        n = features.shape[0]
        ones = jnp.ones(src.shape[0], dtype=features.dtype)
        deg = jax.ops.segment_sum(ones, dst, num_segments=n)
        inv_deg = jnp.where(deg > 0, 1.0 / jnp.maximum(deg, 1.0), 0.0)[:, None]
        h = features
        for l in range(L):
            agg = jax.ops.segment_sum(h[src], dst, num_segments=n) * inv_deg
            h = h @ W_self[l] + agg @ W_neigh[l] + bias[l]
            if l < L - 1:
                h = jax.nn.relu(h)
        return h

    def _L0_ffn_ref(x, Wg, bg, bias, W1, b1, W2, b2):
        import jax, jax.numpy as jnp
        import numpy as np
        D_MODEL = 256
        EXPERT_DIM = 512
        NUM_EXPERTS = 8
        TOP_K = 2
        SEQ_LEN = 128
        BATCH = 2
        x_flat = x.reshape(-1, D_MODEL)
        gate_logits = x_flat @ Wg + bg + bias
        topk_vals, topk_idx = jax.lax.top_k(gate_logits, TOP_K)
        topk_w = jax.nn.softmax(topk_vals, axis=-1)
        combine = (jax.nn.one_hot(topk_idx, NUM_EXPERTS, dtype=x.dtype) * topk_w[..., None]).sum(axis=1)
        h = jax.nn.relu(jnp.einsum('td,edh->teh', x_flat, W1) + b1)
        y = jnp.einsum('teh,ehd->ted', h, W2) + b2
        out = jnp.einsum('ted,te->td', y, combine)
        return out.reshape(x.shape)

    def _L1_gnn_ref(features, values, W1, b1, W2, b2, Wl, bl, adjs, batch, root_idx):
        import jax, jax.numpy as jnp
        import numpy as np
        NEG_SLOPE = 0.01

        def _leaky(x):
            return jnp.where(x >= 0, x, NEG_SLOPE * x)

        def _gcn(x, W, b, src, dst, w, n):
            h = x @ W
            agg = jax.ops.segment_sum(w[:, None] * h[src], dst, num_segments=n)
            return agg + b
        N = features.shape[0]
        src, dst = (adjs[0], adjs[1])
        f1 = features
        h = _gcn(f1, W1, b1, src, dst, values, N)
        f2 = h
        root1 = f1[root_idx[batch]]
        x = _leaky(jnp.concatenate([h, root1], axis=1))
        x = _gcn(x, W2, b2, src, dst, values, N)
        x = _leaky(x)
        root2 = f2[root_idx[batch]]
        x = jnp.concatenate([x, root2], axis=1)
        return _leaky(x @ Wl + bl)

    def _L1_ffn_ref(features, router_w1, router_b1, router_w2, router_b2, expert_w1, expert_b1, expert_w2, expert_b2, expert_w3, expert_b3):
        import jax, jax.numpy as jnp
        import numpy as np
        E, D, H, TOP_K = (6, 256, 256, 2)
        ROUTER_H = D // 2
        rh = jax.nn.relu(features @ router_w1 + router_b1)
        expert_logits = jax.nn.softmax(rh @ router_w2 + router_b2, axis=-1)
        top_w, top_i = jax.lax.top_k(expert_logits, TOP_K)
        routing_weights = jax.nn.softmax(top_w, axis=-1)
        h1 = jax.nn.relu(jnp.einsum('bsd,edh->bseh', features, expert_w1) + expert_b1)
        h2 = jax.nn.relu(jnp.einsum('bseh,ehf->bsef', h1, expert_w2) + expert_b2)
        expert_out = jnp.einsum('bsef,efo->bseo', h2, expert_w3) + expert_b3
        sel = jnp.take_along_axis(expert_out, top_i[:, :, :, None], axis=2)
        combined = jnp.sum(sel * routing_weights[..., None], axis=2)
        return combined

    def _L2_gnn_ref(x, edge_index, W, att_src, att_dst, bias):
        import jax, jax.numpy as jnp
        import numpy as np
        N_NODES = 3125
        N_EDGES = 50000
        IN_F = 256
        HEADS = 4
        OUT_F = 64
        NEG_SLOPE = 0.2
        N = x.shape[0]
        h = (x @ W).reshape(N, HEADS, OUT_F)
        a_src = jnp.sum(h * att_src, axis=-1)
        a_dst = jnp.sum(h * att_dst, axis=-1)
        loop = jnp.arange(N, dtype=edge_index.dtype)
        src = jnp.concatenate([edge_index[0], loop])
        dst = jnp.concatenate([edge_index[1], loop])
        e = jax.nn.leaky_relu(a_src[src] + a_dst[dst], negative_slope=NEG_SLOPE)
        e_max = jax.lax.stop_gradient(jax.ops.segment_max(e, dst, num_segments=N))
        e_max = jnp.where(jnp.isfinite(e_max), e_max, 0.0)
        ex = jnp.exp(e - e_max[dst])
        denom = jax.ops.segment_sum(ex, dst, num_segments=N)
        alpha = ex / denom[dst]
        msg = h[src] * alpha[..., None]
        out = jax.ops.segment_sum(msg, dst, num_segments=N)
        return out.reshape(N, HEADS * OUT_F) + bias

    def _L2_ffn_ref(x, router_w, router_b, W1, b1, W2, b2):
        import jax, jax.numpy as jnp
        import numpy as np
        B, K, D = (512, 16, 256)
        E = 32
        H = int(D * 0.25)
        xf = x.reshape(-1, D)
        logits = xf @ router_w.T + router_b
        idx = jnp.argmax(logits, axis=-1)
        w1t = jnp.take(W1, idx, axis=0)
        h = jnp.einsum('nd,ndh->nh', xf, w1t) + jnp.take(b1, idx, axis=0)
        h = jax.nn.relu(h)
        w2t = jnp.take(W2, idx, axis=0)
        out = jnp.einsum('nh,nhd->nd', h, w2t) + jnp.take(b2, idx, axis=0)
        out = jax.nn.relu(out)
        return out.reshape(x.shape)

    def _L3_gnn_ref(x, src, dst, theta_w, theta_b, phi_w, phi_b):
        import jax, jax.numpy as jnp
        import numpy as np
        N_NODES = 625
        N_EDGES = 20000
        D = 256
        x_src = x[src]
        x_dst = x[dst]
        theta_x = (x_dst - x_src) @ theta_w.T + theta_b
        phi_x = x_src @ phi_w.T + phi_b
        e = jax.nn.relu(theta_x + phi_x)
        out = jax.ops.segment_max(e, dst, num_segments=x.shape[0])
        return jnp.where(jnp.isfinite(out), out, 0.0)

    def _L3_ffn_ref(x, sW1, sb1, sW2, sb2, sW3, sb3, eW1, eb1, eW2, eb2, eW3, eb3, gW, gb):
        import jax, jax.numpy as jnp
        import numpy as np
        B, A = (256, 8)
        IN, OUT = (256, 256)
        SH1, SH2 = (256, 128)
        EH1, EH2 = (128, 64)
        E, TOPK = (4, 2)

        def _shared_mlp(x, W1, b1, W2, b2, W3, b3):
            h = jax.nn.relu(x @ W1 + b1)
            h = jax.nn.relu(h @ W2 + b2)
            return h @ W3 + b3

        def _experts_mlp(x, eW1, eb1, eW2, eb2, eW3, eb3):
            h = jax.nn.relu(jnp.einsum('baf,efh->ebah', x, eW1) + eb1[:, None, None, :])
            h = jax.nn.relu(jnp.einsum('ebah,ehg->ebag', h, eW2) + eb2[:, None, None, :])
            o = jnp.einsum('ebag,ego->ebao', h, eW3) + eb3[:, None, None, :]
            return jnp.moveaxis(o, 0, -1)
        all_out = _experts_mlp(x, eW1, eb1, eW2, eb2, eW3, eb3)
        shared = _shared_mlp(x, sW1, sb1, sW2, sb2, sW3, sb3)
        gates = jax.nn.softmax(x @ gW + gb, axis=-1)
        topv, topi = jax.lax.top_k(gates, TOPK)
        topw = jax.nn.softmax(topv, axis=-1)
        sel = jnp.take_along_axis(all_out, topi[:, :, None, :], axis=-1)
        gated = jnp.sum(sel * topw[:, :, None, :], axis=-1)
        return shared + gated
    edge_index = jnp.stack([src, dst])
    batch0 = jnp.zeros((3125,), jnp.int32)
    x = x + _L0_gnn_ref(_layernorm(x, axis=-1), L0_gnn_W_self, L0_gnn_W_neigh, L0_gnn_bias, src, dst)
    x = x + _L0_ffn_ref(_layernorm(x, axis=-1)[None], L0_ffn_Wg, L0_ffn_bg, L0_ffn_bias, L0_ffn_W1, L0_ffn_b1, L0_ffn_W2, L0_ffn_b2)[0]
    x = x + _L1_gnn_ref(_layernorm(x, axis=-1), edge_weight, L1_gnn_W1, L1_gnn_b1, L1_gnn_W2, L1_gnn_b2, L1_gnn_Wl, L1_gnn_bl, edge_index, batch0, L1_gnn_root_idx)
    x = x + _L1_ffn_ref(_layernorm(x, axis=-1)[None], L1_ffn_router_w1, L1_ffn_router_b1, L1_ffn_router_w2, L1_ffn_router_b2, L1_ffn_expert_w1, L1_ffn_expert_b1, L1_ffn_expert_w2, L1_ffn_expert_b2, L1_ffn_expert_w3, L1_ffn_expert_b3)[0]
    x = x + _L2_gnn_ref(_layernorm(x, axis=-1), edge_index, L2_gnn_W, L2_gnn_att_src, L2_gnn_att_dst, L2_gnn_bias)
    x = x + _L2_ffn_ref(_layernorm(x, axis=-1)[None], L2_ffn_router_w, L2_ffn_router_b, L2_ffn_W1, L2_ffn_b1, L2_ffn_W2, L2_ffn_b2)[0]
    x = x + _L3_gnn_ref(_layernorm(x, axis=-1), src, dst, L3_gnn_theta_w, L3_gnn_theta_b, L3_gnn_phi_w, L3_gnn_phi_b)
    x = x + _L3_ffn_ref(_layernorm(x, axis=-1)[None], L3_ffn_sW1, L3_ffn_sb1, L3_ffn_sW2, L3_ffn_sb2, L3_ffn_sW3, L3_ffn_sb3, L3_ffn_eW1, L3_ffn_eb1, L3_ffn_eW2, L3_ffn_eb2, L3_ffn_eW3, L3_ffn_eb3, L3_ffn_gW, L3_ffn_gb)[0]
    return x

_drawn_inputs = setup_inputs


def setup_inputs(seed=0):
    import zlib

    import numpy as np

    out = dict(_drawn_inputs(seed))
    spreads = {'L0_gnn_bias': (0.0, 0.1),
     'L0_ffn_bias': (0.0, 0.461),
     'L1_gnn_b1': (0.0, 0.403),
     'L1_gnn_b2': (0.0, 0.8),
     'L1_gnn_bl': (0.0, 0.8),
     'L1_ffn_router_b1': (0.0, 0.8),
     'L1_ffn_router_b2': (0.0, 0.8),
     'L1_ffn_expert_b1': (0.0, 0.8),
     'L1_ffn_expert_b2': (0.0, 0.8),
     'L1_ffn_expert_b3': (0.0, 0.8),
     'L2_gnn_bias': (0.0, 0.757),
     'L3_gnn_theta_b': (0.0, 0.8),
     'L3_gnn_phi_b': (0.0, 0.8),
     'L3_ffn_sb1': (0.0, 0.8),
     'L3_ffn_sb2': (0.0, 2.0),
     'L3_ffn_sb3': (0.0, 2.0),
     'L3_ffn_eb1': (0.0, 0.8),
     'L3_ffn_eb2': (0.0, 2.0),
     'L3_ffn_eb3': (0.0, 2.0),
     'L3_ffn_gb': (0.0, 0.8)}
    factors = {'L0_ffn_Wg': 2.798,
     'L0_ffn_bg': 8.0,
     'L0_ffn_b1': 8.0,
     'L0_ffn_b2': 4.848,
     'L1_ffn_router_w1': 6.151,
     'L1_ffn_router_w2': 6.104,
     'L1_ffn_expert_w1': 8.0,
     'L1_ffn_expert_w2': 8.0,
     'L1_ffn_expert_w3': 6.792,
     'L2_gnn_att_src': 8.0,
     'L2_gnn_att_dst': 28.736,
     'L2_ffn_router_w': 4.129,
     'L2_ffn_router_b': 8.0,
     'L2_ffn_W1': 5.067,
     'L2_ffn_b1': 8.0,
     'L2_ffn_W2': 3.794,
     'L2_ffn_b2': 8.0,
     'L3_ffn_sW1': 4.77,
     'L3_ffn_sW2': 4.182,
     'L3_ffn_sW3': 3.762,
     'L3_ffn_eW1': 8.0,
     'L3_ffn_eW2': 8.0,
     'L3_ffn_eW3': 8.0,
     'L3_ffn_gW': 8.0}
    for name, (base, spread) in spreads.items():
        noise = np.random.default_rng([zlib.crc32(name.encode()), seed]).standard_normal(out[name].shape)
        drawn = base * np.exp(spread * noise) if base else spread * noise
        out[name] = jnp.asarray(drawn.astype(out[name].dtype))
    for name, factor in factors.items():
        out[name] = (out[name] * factor).astype(out[name].dtype)
    return out
```

```python
import concourse.bass as bass
import numpy as np
from concourse import mybir
from contextlib import ExitStack

F32, I32, U32, BF16 = mybir.dt.float32, mybir.dt.int32, mybir.dt.uint32, mybir.dt.bfloat16
ALU = mybir.AluOpType
ACT = mybir.ActivationFunctionType
AX = mybir.AxisListType.X

N, E, D = 3125, 50000, 256
NB, BLOCKS = 125, 25
TE = 128
GT = 4
GROUPS = -(-E // (TE * GT))
TILES = GROUPS * GT
RG = 7
ROUNDS = GROUPS // RG
RT = RG * GT
GW = 260
HEADS, HD = 4, 64
NOWHERE = 4000
LOWEST = -(2.0 ** 125)


class Signals:

    def __init__(self, ctx, nc, part):
        self.ctx, self.nc, self.part, self.by_name = ctx, nc, part, {}

    def __call__(self, name):
        if name not in self.by_name:
            self.by_name[name] = self.ctx.enter_context(self.nc.semaphore(f"{self.part}_{name}"))
        return self.by_name[name]


class Memory:
    pass


def clear(nc, signals):
    with nc.Block() as block:
        @block.gpsimd
        def _(pool):
            for s in signals.by_name.values():
                pool.sem_clear(s)


def chunks(ap, p=128):
    return ap.rearrange("(k p) m -> p k m", p=p)


def edge_tables(nc, m, a, parts):
    ctx = ExitStack()
    with ctx:
        S = Signals(ctx, nc, "edges")
        wide = 4 * TE
        m.weights.reset()
        take = m.weights.take
        cut = lambda ap: ap.rearrange("p (c j) -> p c j", j=TE)
        dst_i, nxt_i, src_i = (cut(take(wide).bitcast(I32)) for _ in range(3))
        rows = take(4 * wide).rearrange("p (n c j) -> p n c j", n=4, j=TE)
        nxt_f = cut(take(wide))
        bar = cut(take(wide // 2).bitcast(BF16))
        below = take(wide)
        bar0 = ctx.enter_context(nc.sbuf_tensor("bar0", [1, 2], BF16))
        cnt = ctx.enter_context(nc.sbuf_tensor("cnt", [128, 24], F32))
        ptr_i = ctx.enter_context(nc.sbuf_tensor("ptr_i", [1, 24], I32))
        glo_i = ctx.enter_context(nc.sbuf_tensor("glo_i", [1, 24], I32))
        glo_f = ctx.enter_context(nc.sbuf_tensor("glo_f", [1, 24], F32))
        steps = ctx.enter_context(nc.sbuf_tensor("steps", [1, GROUPS], F32))
        dl = ctx.enter_context(nc.sbuf_tensor("dl", [1, GROUPS], F32))
        DST, SRC, WGT, LAST = range(4)

        def in_rows(eng, tile, dram, shift, signal):
            for c in range(3):
                at = shift + c * 128 * TE
                eng.dma_start(tile[:, c, :], dram[at:at + 128 * TE].rearrange("(p j) -> p j", j=TE)).then_inc(signal, 16)
            at = shift + 3 * 128 * TE
            full = (E - at) // TE
            eng.dma_start(tile[0:full, 3, :], dram[at:at + full * TE].rearrange("(p j) -> p j", j=TE)).then_inc(signal, 16)
            at += full * TE
            eng.dma_start(tile[full:full + 1, 3, 0:E - at], dram[at:E].rearrange("(p j) -> p j", p=1)).then_inc(signal, 16)

        block = ctx.enter_context(nc.Block())

        @block.gpsimd
        def _(pool):
            pool.memset(m.ident[:, :], 0.0).then_inc(S("ident0"), 1)
            pool.wait_ge(S("ident0"), 1)
            pool.affine_select(out=m.ident[:, :], in_=m.ident[:, :], compare_op=ALU.not_equal, fill=1.0, base=0,
                               pattern=[[-1, 128]], channel_multiplier=1).then_inc(S("ident"), 1)
            pool.iota(m.iota[:, :], pattern=[[1, 128]], base=0, channel_multiplier=0,
                      allow_small_or_imprecise_dtypes=True).then_inc(S("iota"), 1)
            pool.memset(m.zeros[:, :], 0.0).then_inc(S("iota"), 1)
            pool.memset(m.spread[:, :], 0.0).then_inc(S("spread0"), 1)
            pool.wait_ge(S("spread0"), 1)
            sp = m.spread[:, :].rearrange("e (f h) -> e f h", h=64)
            pool.affine_select(out=sp, in_=sp, compare_op=ALU.not_equal, fill=1.0, base=0,
                               pattern=[[-1, 32], [0, 64]], channel_multiplier=1).then_inc(S("iota"), 1)

        @block.sync
        def _(sp):
            sp.wait_ge(S("filled"), 4)
            in_rows(sp, dst_i, a["dst"], 0, S("dst_in"))
            in_rows(sp, nxt_i, a["dst"], 1, S("nxt_in"))
            in_rows(sp, src_i, a["src"], 0, S("src_in"))
            in_rows(sp, rows[:, WGT], a["edge_weight"], 0, S("wgt_in"))
            sp.wait_ge(S("bar"), 2)
            sp.dma_start(m.bars[0:1].rearrange("(p j) -> p j", p=1), bar0[0:1, 0:1]).then_inc(S("bars_out"), 16)
            for c in range(3):
                at = 1 + c * 128 * TE
                sp.dma_start(m.bars[at:at + 128 * TE].rearrange("(p j) -> p j", j=TE), bar[:, c, :]).then_inc(S("bars_out"), 16)
            at = 1 + 3 * 128 * TE
            sp.dma_start(m.bars[at:at + 8 * TE].rearrange("(p j) -> p j", j=TE), bar[0:8, 3, :]).then_inc(S("bars_out"), 16)
            sp.wait_ge(S("bars_out"), 80)

        @block.vector
        def _(dve):
            nc.vector.memset(dst_i[:, :, :], NOWHERE).then_inc(S("filled"), 1)
            nc.vector.memset(nxt_i[:, :, :], NOWHERE).then_inc(S("filled"), 1)
            nc.vector.memset(src_i[:, :, :], 0).then_inc(S("filled"), 1)
            nc.vector.memset(rows[:, WGT], 0.0).then_inc(S("filled"), 1)
            nc.vector.memset(m.lg[:, :], LOWEST).then_inc(S("filled_more"), 1)
            nc.vector.memset(m.pr[:, :], -1.0).then_inc(S("filled_more"), 1)
            nc.vector.memset(bar0[:, :], LOWEST).then_inc(S("bar"), 1)
            nc.vector.memset(m.ones[:, :], 1.0).then_inc(S("ones"), 1)
            nc.vector.memset(m.glo[:, :], 0).then_inc(S("glo0"), 1)
            nc.vector.memset(m.fr[:, :], 0).then_inc(S("glo0"), 1)
            nc.vector.memset(dl[:, :], 0.0).then_inc(S("glo0"), 1)
            dve.wait_ge(S("dst_in"), 80)
            nc.vector.tensor_copy(rows[:, DST], dst_i[:, :, :]).then_inc(S("dst_f"), 1)
            dve.wait_ge(S("nxt_in"), 80)
            nc.vector.tensor_copy(nxt_f[:, :, :], nxt_i[:, :, :]).then_inc(S("nxt_f"), 1)
            dve.wait_ge(S("src_in"), 80)
            nc.vector.tensor_copy(rows[:, SRC], src_i[:, :, :]).then_inc(S("src_f"), 1)
            dve.wait_ge(S("dst_f"), 1)
            dve.wait_ge(S("nxt_f"), 1)
            nc.vector.tensor_tensor(rows[:, LAST], rows[:, DST], nxt_f[:, :, :], ALU.not_equal).then_inc(S("last_f"), 1)
            dve.wait_ge(S("last_f"), 1)
            nc.vector.tensor_scalar(bar[:, :, :], rows[:, LAST], LOWEST, None, ALU.mult).then_inc(S("bar"), 1)
            for b in range(1, BLOCKS):
                if b > 1:
                    dve.wait_ge(S("cnt"), b - 1)
                nc.vector.tensor_scalar(below[:, :], rows[:, DST].rearrange("p c j -> p (c j)"), float(NB * b), 0.0,
                                        ALU.is_lt, ALU.add, accum_out=cnt[:, b - 1:b]).then_inc(S("cnt"), 1)
            dve.wait_ge(S("ptr"), 1)
            nc.vector.tensor_copy(ptr_i[:, :], m.bank[0][0:1, 0:24]).then_inc(S("ptr_i"), 1)
            dve.wait_ge(S("ptr_i"), 1)
            nc.vector.tensor_scalar(glo_i[:, :], ptr_i[:, :], 9, None, ALU.arith_shift_right).then_inc(S("glo_i"), 1)
            dve.wait_ge(S("glo_i"), 1)
            dve.wait_ge(S("glo0"), 3)
            nc.vector.tensor_copy(m.glo[:, 1:25], glo_i[:, :]).then_inc(S("glo"), 1)
            nc.vector.memset(m.glo[:, 25:26], GROUPS - 1).then_inc(S("glo"), 1)
            nc.vector.tensor_copy(glo_f[:, :], glo_i[:, :]).then_inc(S("glo_f"), 1)
            dve.wait_ge(S("glo_f"), 1)
            dve.wait_ge(S("iota"), 3)
            for b in range(24):
                nc.vector.scalar_tensor_tensor(dl[:, :], m.iota[0:1, 0:GROUPS], glo_f[:, b:b + 1], dl[:, :],
                                               ALU.is_ge, ALU.add).then_inc(S("dl"), 1)
                dve.wait_ge(S("dl"), b + 1)
            nc.vector.scalar_tensor_tensor(steps[:, :], m.iota[0:1, 0:GROUPS], 1.0, dl[:, :],
                                           ALU.add, ALU.add).then_inc(S("steps"), 1)
            dve.wait_ge(S("steps"), 1)
            nc.vector.tensor_copy(m.fr[:, RG:GROUPS], steps[:, 0:GROUPS - RG]).then_inc(S("fr"), 1)
            for n, out in enumerate([m.dst_c, m.src_c, m.w_c, m.last_c]):
                dve.wait_ge(S("columns"), n + 1)
                nc.vector.tensor_copy(out[:, :], m.bank[1 + n][:, 0:TILES]).then_inc(S("columns_out"), 1)

        @block.tensor
        def _(pe):
            pe.wait_ge(S("ident"), 1)
            pe.wait_ge(S("ones"), 1)
            pe.wait_ge(S("cnt"), 24)
            nc.tensor.matmul(m.bank[0][0:1, 0:24], m.ones[:, :], cnt[:, :], start=True, stop=True).then_inc(S("ptr"), 1)
            for n, (signal, count) in enumerate([("dst_f", 1), ("src_f", 1), ("wgt_in", 80), ("last_f", 1)]):
                pe.wait_ge(S(signal), count)
                for c in range(4):
                    t = nc.tensor.transpose(m.bank[1 + n][:, c * 128:(c + 1) * 128], rows[:, n, c, :], m.ident[:, :])
                t.then_inc(S("columns"), 1)
    clear(nc, S)


class Chain:

    def __init__(self, eng, signal, t, steps):
        self.eng, self.counter, self.t, self.steps, self.done = eng, signal, t, steps, 0

    def link(self, ins):
        self.done += 1
        ins.then_inc(self.counter, 1)
        self.eng.wait_ge(self.counter, self.t * self.steps + self.done)

    def end(self):
        assert self.done == self.steps, (self.done, self.steps)


def norm_dve(nc, m, S, dve, t, rows, name="norm"):
    c = Chain(dve, S(name + "_steps"), t, 4)
    dve.sem_inc(S("turn"), 1)
    c.link(nc.vector.bn_stats(m.st[:, :], rows))
    dve.sem_inc(S("turn"), 1)
    c.link(nc.vector.bn_aggr(m.mv[:, :], m.st[:, :]))
    c.link(nc.vector.tensor_scalar(m.ve[:, :], m.mv[:, 1:2], 1e-5, None, ALU.add))
    dve.wait_ge(S(name + "_sd"), t + 1)
    c.link(nc.vector.reciprocal(m.rs[:, :], m.sd[:, :]))
    c.end()
    nc.vector.tensor_scalar(m.xn[:, :], rows, m.mv[:, 0:1], m.rs[:, :], ALU.subtract, ALU.mult)\
        .then_inc(S(name + "_xn"), 1)


def norm_act(nc, m, S, act, t, name="norm"):
    act.wait_ge(S(name + "_steps"), t * 4 + 3)
    nc.scalar.activation(m.sd[:, :], m.ve[:, :], ACT.Sqrt).then_inc(S(name + "_sd"), 1)


def turn_pe(nc, m, S, pe, t, name="norm"):
    pe.wait_ge(S(name + "_xn"), t + 1)
    nc.tensor.transpose(m.bank[3][:, 0:NB], m.xn[:, 0:128], m.ident[0:NB, 0:NB])
    nc.tensor.transpose(m.bank[3][:, NB:2 * NB], m.xn[:, 128:256], m.ident[0:NB, 0:NB]).then_inc(S(name + "_turned"), 1)


def turn_act(nc, m, S, act, t, name="norm"):
    act.wait_ge(S(name + "_turned"), t + 1)
    nc.scalar.copy(m.xt[:, :, :], m.bank[3][:, 0:2 * NB].rearrange("p (k n) -> p k n", k=2)).then_inc(S(name + "_xt"), 1)


def product(nc, out, xt, w, signal):
    k = w.shape[1]
    for j in range(k):
        last = nc.tensor.matmul(out, xt[:, j, :], w[:, j, :], start=(j == 0), stop=(j == k - 1))
    last.then_inc(signal, 1)


def first_store(act, m, S):
    act.dma_start(m.primer[0:1, 0:1], m.ident[0:1, 0:1]).then_inc(S("stored"), 16)


def store_act(nc, m, S, act, t, psum, width, table, signal, per_block=1):
    act.wait_ge(S(signal), t + 1)
    act.wait_ge(S("stored"), t * 16 * per_block + 16)
    nc.scalar.copy(m.stage[:, 0:width], psum).then_inc(S("stage"), 1)
    act.wait_ge(S("stage"), t + 2)
    act.dma_start(table[bass.ds(t * NB, NB), :], m.stage[:, 0:width]).then_inc(S("stored"), 16)


def router_steps(experts, softmax, top):
    return 1 + (5 if softmax else 0) + (9 if top == 2 else 3) + (2 if experts < 8 else 0)


def router_dve(nc, m, S, dve, t, logits, bias, experts, softmax, top):
    c = Chain(dve, S("router_steps"), t, router_steps(experts, softmax, top))
    wide = max(experts, 8)
    if experts < 8:
        c.link(nc.vector.memset(m.lg[:, experts:8], LOWEST))
        c.link(nc.vector.memset(m.pr[:, experts:8], -1.0))
    dve.wait_ge(S("logits"), t + 1)
    c.link(nc.vector.tensor_tensor(m.lg[:, 0:experts], logits, bias, ALU.add))
    pick = m.lg
    if softmax:
        dve.sem_inc(S("turn"), 1)
        c.link(nc.vector.max(m.v8[:, :], m.lg[:, 0:wide]))
        c.link(nc.vector.tensor_scalar(m.neg[:, :], m.v8[:, 0:1], -1.0, None, ALU.mult))
        dve.wait_ge(S("router_exp"), t + 1)
        c.link(nc.vector.tensor_reduce(m.sm[:, :], m.ex[:, 0:experts], AX, ALU.add))
        c.link(nc.vector.reciprocal(m.sr[:, :], m.sm[:, :]))
        c.link(nc.vector.tensor_scalar(m.pr[:, 0:experts], m.ex[:, 0:experts], m.sr[:, :], None, ALU.mult))
        pick = m.pr
    dve.sem_inc(S("turn"), 1)
    c.link(nc.vector.max(m.v8[:, :], pick[:, 0:wide]))
    dve.sem_inc(S("turn"), 1)
    c.link(nc.vector.max_index(m.i8[:, :], m.v8[:, :], pick[:, 0:wide]))
    c.link(nc.vector.tensor_copy(m.i8f[:, :], m.i8[:, :]))
    if top == 1:
        c.end()
        nc.vector.tensor_scalar(m.c[:, 0:experts], m.iota[0:NB, 0:experts], m.i8f[:, 0:1], None, ALU.is_equal)\
            .then_inc(S("weights"), 1)
        return
    c.link(nc.vector.tensor_tensor(m.d12[:, :], m.v8[:, 1:2], m.v8[:, 0:1], ALU.subtract))
    dve.wait_ge(S("router_exp2"), t + 1)
    c.link(nc.vector.tensor_scalar(m.sm2[:, :], m.e2[:, :], 1.0, None, ALU.add))
    c.link(nc.vector.reciprocal(m.w12[:, 0:1], m.sm2[:, :]))
    c.link(nc.vector.tensor_tensor(m.w12[:, 1:2], m.e2[:, :], m.w12[:, 0:1], ALU.mult))
    c.link(nc.vector.tensor_scalar(m.c1[:, 0:experts], m.iota[0:NB, 0:experts], m.i8f[:, 0:1], m.w12[:, 0:1],
                                   ALU.is_equal, ALU.mult))
    c.link(nc.vector.tensor_scalar(m.c2[:, 0:experts], m.iota[0:NB, 0:experts], m.i8f[:, 1:2], m.w12[:, 1:2],
                                   ALU.is_equal, ALU.mult))
    c.end()
    nc.vector.tensor_tensor(m.c[:, 0:experts], m.c1[:, 0:experts], m.c2[:, 0:experts], ALU.add).then_inc(S("weights"), 1)


def router_act(nc, m, S, act, t, experts, softmax, top, turn=True):
    steps = router_steps(experts, softmax, top)
    fill = 2 if experts < 8 else 0
    if softmax:
        act.wait_ge(S("router_steps"), t * steps + fill + 3)
        nc.scalar.activation(m.ex[:, 0:experts], m.lg[:, 0:experts], ACT.Exp, bias=m.neg[:, :]).then_inc(S("router_exp"), 1)
    if top == 2:
        act.wait_ge(S("router_steps"), t * steps + fill + (10 if softmax else 5))
        nc.scalar.activation(m.e2[:, :], m.d12[:, :], ACT.Exp).then_inc(S("router_exp2"), 1)


def router_turned_act(nc, m, S, act, t, experts):
    act.wait_ge(S("weights_turned"), t + 1)
    nc.scalar.copy(m.ct[0:experts, :], m.bank[3][0:experts, 256:256 + NB]).then_inc(S("ct"), 1)


def router_pe(nc, m, S, pe, t, experts):
    pe.wait_ge(S("weights"), t + 1)
    nc.tensor.transpose(m.bank[3][0:experts, 256:256 + NB], m.c[:, 0:experts], m.ident[0:NB, 0:NB])\
        .then_inc(S("weights_turned"), 1)


class Experts:

    def __init__(self, count, layers, out, out_chunks, out_units):
        self.count, self.layers, self.out, self.out_chunks, self.out_units = count, layers, out, out_chunks, out_units
        depth = len(layers)
        self.jobs, self.hidden = [], {}
        for step in range(count + depth):
            for layer in range(depth + 1):
                e = step - layer
                if 0 <= e < count:
                    self.jobs.append((e, layer))
                    if layer < depth:
                        self.hidden[e, layer] = len(self.hidden)

    def pe(self, nc, m, S, pe, t, before_outputs):
        n, depth = len(self.hidden), len(self.layers)
        for e, layer in self.jobs:
            if (e, layer) == (0, depth):
                before_outputs()
            if layer < depth:
                i = self.hidden[e, layer]
                if layer == 0:
                    source = m.xt
                else:
                    pe.wait_ge(S("hidden"), t * n + self.hidden[e, layer - 1] + 1)
                    source = m.ht[:, self.hidden[e, layer - 1] % 4]
                if i >= 4:
                    pe.wait_ge(S("hidden"), t * n + i - 3)
                k_in, c_out, units, weights, _ = self.layers[layer]
                for c in range(c_out):
                    for k in range(k_in):
                        last = nc.tensor.matmul(m.hid[i % 4][0:units, c * NB:(c + 1) * NB], weights(e, k, c),
                                                source[:, k, :], start=(k == 0), stop=(k == k_in - 1))
                last.then_inc(S("hidden_sums"), 1)
            else:
                i = self.hidden[e, depth - 1]
                pe.wait_ge(S("hidden"), t * n + i + 1)
                o = 1 + e
                if o >= 2:
                    pe.wait_ge(S("added"), t * (1 + self.count) + o - 1)
                u = self.out_units
                for k in range(self.out_chunks):
                    last = nc.tensor.matmul(m.bank[6 + o % 2][0:NB, 0:D], m.ht[0:u, i % 4, k, :], self.out(e, k),
                                            start=(k == 0), stop=(k == self.out_chunks - 1))
                last.then_inc(S("outputs"), 1)

    def act(self, nc, m, S, act, t, before_outputs):
        n = len(self.hidden)
        ahead = sum(layer < len(self.layers) for _, layer in self.jobs[:self.jobs.index((0, len(self.layers)))])
        for (e, layer), i in sorted(self.hidden.items(), key=lambda kv: kv[1]):
            if i == ahead:
                before_outputs()
            act.wait_ge(S("hidden_sums"), t * n + i + 1)
            _, c_out, units, _, bias = self.layers[layer]
            for c in range(c_out):
                last = nc.scalar.activation(m.ht[0:units, i % 4, c, :], m.hid[i % 4][0:units, c * NB:(c + 1) * NB],
                                            ACT.Relu, bias=bias(e, c))
            last.then_inc(S("hidden"), 1)

    def dve(self, nc, m, S, dve, t, rows):
        total = 1 + self.count
        for o in range(total):
            dve.wait_ge(S("outputs"), t * total + o + 1)
            if o == 0:
                ins = nc.vector.tensor_tensor(rows, m.bank[6][0:NB, 0:D], rows, ALU.add)
            else:
                ins = nc.vector.scalar_tensor_tensor(rows, m.bank[6 + o % 2][0:NB, 0:D], m.c[:, o - 1:o], rows,
                                                     ALU.mult, ALU.add)
            ins.then_inc(S("added"), 1)
            dve.wait_ge(S("added"), t * total + o + 1)


def edge_pass(nc, m, name, table, width, kind, pe_tile, act_tile, dve_tile, weight=None, sp_loads=None, stores=0):
    ctx = ExitStack()
    with ctx:
        S = Signals(ctx, nc, name)
        scans = kind == "max"
        halves = [(0, width)] if width <= 128 else [(0, 128), (128, 256)]
        columns = {"sum": D, "degrees": GW, "max": width, "attention": GW}[kind]
        arrived, before = m.arrived, m.arrived_count
        m.arrived_count += 16 * ROUNDS
        bars_in = [S(f"bars_{k}") for k in range(RG)] if scans else []
        onehot = S("onehot")
        block = ctx.enter_context(nc.Block())

        def visits(eng, d):
            first = eng.value_load(m.glo[0:1, bass.ds(d, 1)], min_val=0, max_val=GROUPS - 1)
            last = eng.value_load(m.glo[0:1, bass.ds(d + 1, 1)], min_val=0, max_val=GROUPS - 1)
            return first, last + 1

        def slot_of(g):
            return nc.s_assert_within(g % RG, 0, RG - 1, skip_runtime_bounds_check_because="a remainder")

        @block.gpsimd
        def _(pool):
            if kind == "degrees":
                pool.memset(m.rows[:, :].rearrange("p (t w) -> p t w", w=GW)[:, :, D:GW], 1.0).then_inc(S("ones"), 1)
            with pool.Fori(0, ROUNDS) as i:
                for k in range(RG):
                    free = pool.value_load(m.fr[0:1, bass.ds(i * RG + k, 1)], min_val=0, max_val=GROUPS + BLOCKS)
                    pool.wait_ge(S("summed"), free * GT + 4)
                    pool.sem_inc(S("turn"), 1)
                    pool.tensor_copy(m.idx[:, k * GT:(k + 1) * GT], m.src_c[:, bass.ds((i * RG + k) * GT, GT)])\
                        .then_inc(S("idx"), 1)
                    pool.wait_ge(S("idx"), i * RG + (k + 1))
                    pool.sem_inc(S("turn"), 1)
                    for s in range(GT):
                        n = k * GT + s
                        pool.indirect_dma_start(
                            out=m.rows[:, n * GW:n * GW + table.shape[1]], out_offset=None, in_=table,
                            in_offset=bass.IndirectOffsetOnAxis(ap=m.idx[:, n:n + 1], axis=0)).then_inc(arrived[n], 16)

        @block.sync
        def _(sp):
            if sp_loads:
                sp_loads(sp, S)
            with sp.Fori(0, ROUNDS) as i:
                for k in range(RG):
                    if scans:
                        free = sp.value_load(m.fr[0:1, bass.ds(i * RG + k, 1)], min_val=0, max_val=GROUPS + BLOCKS)
                        sp.wait_ge(S("summed"), free * GT + 4)
                        sp.sem_inc(S("turn_sp"), 1)
                        at = (i * RG + k) * (GT * TE)
                        sp.dma_start(m.bar[:, k * GT * TE:(k + 1) * GT * TE], m.bars[bass.ds(at, GT * TE)].partition_broadcast(128))\
                            .then_inc(bars_in[k], 16)
                        sp.wait_ge(bars_in[k], i * 16 + 16)
                        sp.sem_inc(S("turn_sp"), 1)
                    for s in range(GT):
                        sp.wait_ge(arrived[k * GT + s], i * 16 + (before + 16))
                        sp.sem_inc(S("tiles_in"), 1)
            if stores:
                sp.wait_ge(S("stored"), 16 * BLOCKS * stores + 16)
            if sp_loads:
                sp.wait_ge(S("loaded"), 16 * sp_loads.count)

        @block.vector
        def _(dve):
            nc.vector.tensor_scalar(m.dloc[:, :], m.dst_c[:, :], float(NB), None, ALU.add).then_inc(S("relative"), 1)
            if scans:
                nc.vector.memset(m.run[:, GT - 1], 0.0).then_inc(S("run0"), 1)
                dve.wait_ge(S("run0"), 1)
            with dve.Fori(0, BLOCKS) as d:
                first, last = visits(dve, d)
                dve.wait_ge(S("relative"), d + 1)
                nc.vector.tensor_scalar(m.dloc[:, :], m.dloc[:, :], -float(NB), None, ALU.add).then_inc(S("relative"), 1)
                dve.wait_ge(S("relative"), d + 2)
                dve.sem_inc(S("turn"), 1)
                with dve.Fori(first, last) as g:
                    v = g + d

                    def one_hot(s):
                        dve.wait_ge(S("summed"), v * GT + (s + 1))
                        edge = bass.ds(g * GT + s, 1)
                        if weight is None:
                            nc.vector.tensor_scalar(m.sel[:, s, :], m.iota[:, 0:NB], m.dloc[:, edge], None, ALU.is_equal)\
                                .then_inc(onehot, 1)
                        else:
                            nc.vector.tensor_scalar(m.sel[:, s, :], m.iota[:, 0:NB], m.dloc[:, edge], weight[:, edge],
                                                    ALU.is_equal, ALU.mult).then_inc(onehot, 1)

                    if kind in ("sum", "degrees"):
                        for s in range(GT):
                            one_hot(s)
                    elif kind == "max":
                        slot = slot_of(g)
                        for s in range(GT):
                            one_hot(s)
                            n = v * GT + s
                            dve.wait_ge(S("turned"), n + 5)
                            dve.wait_ge(S("scanned"), n + 2)
                            dve.wait_ge(S("back"), n + 1)
                            for h, (lo, hi) in enumerate(halves):
                                w = hi - lo
                                ins = nc.vector.tensor_tensor_scan(
                                    m.run[0:w, s, h, :], m.bar[0:w, bass.ds((slot * GT + s) * TE, TE)],
                                    m.bank[1 + s % 2][0:w, h * TE:(h + 1) * TE], m.run[0:w, (s - 1) % GT, h, TE - 1:TE],
                                    ALU.add, ALU.max)
                            ins.then_inc(S("scanned"), 1)
                    else:
                        slot = slot_of(g)

                        def logit(s):
                            n = v * GT + s
                            tile = m.rows[:, bass.ds((slot * GT + s) * GW + D, HEADS)]
                            dve.wait_ge(S("tiles_in"), g * GT + (s + 1))
                            dve.wait_ge(S("dst_values"), n + 5)
                            own = m.bank[4 + s % 2]
                            nc.vector.tensor_tensor(m.e0[:, s, :], tile, own[:, 0:HEADS], ALU.add).then_inc(S("logit_steps"), 1)
                            dve.wait_ge(S("logit_steps"), n * 2 + 1)
                            nc.vector.scalar_tensor_tensor(m.e1[:, s, :], m.e0[:, s, :], 0.2, m.e0[:, s, :], ALU.mult, ALU.max)\
                                .then_inc(S("logit_steps"), 1)
                            dve.wait_ge(S("logit_steps"), n * 2 + 2)
                            dve.wait_ge(S("weighted"), n + 1)
                            nc.vector.tensor_tensor(m.e3[:, s, :], m.e1[:, s, :], own[:, HEADS:2 * HEADS], ALU.subtract)\
                                .then_inc(S("logit"), 1)

                        def message(s):
                            n = v * GT + s
                            dve.wait_ge(S("weighted"), n + 5)
                            tile = m.rows[:, bass.ds((slot * GT + s) * GW, D)].rearrange("p (h f) -> p h f", h=HEADS)
                            nc.vector.tensor_tensor(m.msg[:, s, 0:D].rearrange("p (h f) -> p h f", h=HEADS), tile,
                                                    m.msg[:, s, D:GW].unsqueeze(2).to_broadcast([128, HEADS, HD]), ALU.mult)\
                                .then_inc(S("message"), 1)

                        one_hot(0)
                        one_hot(1)
                        for s in range(GT + 1):
                            if s + 2 < GT:
                                one_hot(s + 2)
                            if s < GT:
                                logit(s)
                            if s > 0:
                                message(s - 1)
                dve_tile(dve, S, d)

        @block.scalar
        def _(act):
            if stores:
                first_store(act, m, S)
            with act.Fori(0, BLOCKS) as d:
                if kind in ("max", "attention"):
                    first, last = visits(act, d)
                    act.sem_inc(S("turn_act"), 1)
                    with act.Fori(first, last) as g:
                        v = g + d
                        slot = slot_of(g) if kind == "max" else None
                        for s in range(GT + 1):
                            n = v * GT + s
                            if kind == "max" and s < GT:
                                act.wait_ge(S("tiles_in"), g * GT + (s + 1))
                                act.wait_ge(S("turned"), n + 1)
                                nc.scalar.copy(m.gt[:, s, 0:width], m.rows[:, bass.ds((slot * GT + s) * GW, width)])\
                                    .then_inc(S("tile_copied"), 1)
                            if kind == "max" and s > 0:
                                act.wait_ge(S("back"), n + 4)
                                act.wait_ge(S("summed"), n)
                                nc.scalar.copy(m.runt[:, s - 1, 0:width], m.bank[4 + (s - 1) % 2][:, 0:width])\
                                    .then_inc(S("copied"), 1)
                            if kind == "attention" and s < GT:
                                act.wait_ge(S("sel_turned"), n + 1)
                                act.wait_ge(S("dst_values"), n + 1)
                                nc.scalar.copy(m.selt[:, s, :], m.bank[1 + s % 2][0:NB, 0:TE]).then_inc(S("selt"), 1)
                            if kind == "attention" and s > 0:
                                act.wait_ge(S("logit"), n + 2)
                                act.wait_ge(S("summed"), n)
                                nc.scalar.activation(m.msg[:, s - 1, D:GW], m.e3[:, s - 1, :], ACT.Exp)\
                                    .then_inc(S("weighted"), 1)
                act_tile(act, S, d)

        @block.tensor
        def _(pe):
            pe.sem_inc(S("summed"), 4)
            for name in ("acc_read", "stage", "done", "y"):
                pe.sem_inc(S(name), 1)
            if kind == "max":
                pe.sem_inc(S("scanned"), 2)
                pe.sem_inc(S("turned"), 4)
                pe.sem_inc(S("back"), 4)
                pe.sem_inc(S("copied"), 2)
            if kind == "attention":
                pe.sem_inc(S("selt"), 2)
                pe.sem_inc(S("dst_values"), 4)
                pe.sem_inc(S("logit"), 2)
                pe.sem_inc(S("weighted"), 4)
            if kind == "degrees":
                pe.wait_ge(S("ones"), 1)
            with pe.Fori(0, BLOCKS) as d:
                first, last = visits(pe, d)
                pe.wait_ge(S("acc_read"), d + 1)
                nc.tensor.matmul(m.acc[:, 0:columns], m.zeros[:, 0:NB], m.zeros[:, 0:columns], start=True, stop=False)
                with pe.Fori(first, last) as g:
                    v = g + d
                    slot = slot_of(g)

                    def gathered(s, lo, hi):
                        return m.rows[:, bass.ds((slot * GT + s) * GW + lo, hi - lo)]

                    def add(s, rows):
                        pe.wait_ge(onehot, v * GT + (s + 1))
                        nc.tensor.matmul(m.acc[:, 0:columns], m.sel[:, s, :], rows, start=False, stop=False).then_inc(S("summed"), 1)

                    if kind in ("sum", "degrees"):
                        for s in range(GT):
                            pe.wait_ge(S("tiles_in"), g * GT + (s + 1))
                            add(s, gathered(s, 0, columns))
                    elif kind == "max":
                        def turn(s):
                            n = v * GT + s
                            pe.wait_ge(S("tile_copied"), n + 1)
                            pe.wait_ge(S("scanned"), n + 1)
                            for h, (lo, hi) in enumerate(halves):
                                ins = nc.tensor.transpose(m.bank[1 + s % 2][0:hi - lo, h * TE:(h + 1) * TE],
                                                          m.gt[:, s, lo:hi], m.ident[:, :])
                            ins.then_inc(S("turned"), 1)

                        def turn_back(s):
                            n = v * GT + s
                            pe.wait_ge(S("scanned"), n + 3)
                            pe.wait_ge(S("copied"), n + 1)
                            pe.sem_inc(S("turn_pe"), 1)
                            for h, (lo, hi) in enumerate(halves):
                                ins = nc.tensor.transpose(m.bank[4 + s % 2][:, lo:hi],
                                                          m.run[0:hi - lo, s, h, :], m.ident[0:hi - lo, 0:hi - lo])
                            ins.then_inc(S("back"), 1)

                        for step in range(GT + 2):
                            if step < GT:
                                turn(step)
                            if 1 <= step <= GT:
                                turn_back(step - 1)
                            if step >= 2:
                                pe.wait_ge(S("copied"), v * GT + step - 2 + 3)
                                add(step - 2, m.runt[:, step - 2, 0:width])
                    else:
                        def turn_selection(s):
                            n = v * GT + s
                            pe.wait_ge(onehot, n + 1)
                            pe.wait_ge(S("selt"), n + 1)
                            nc.tensor.transpose(m.bank[1 + s % 2][0:NB, 0:TE], m.sel[:, s, :], m.ident[:, :])\
                                .then_inc(S("sel_turned"), 1)

                        def dst_values(s):
                            n = v * GT + s
                            pe.wait_ge(S("selt"), n + 3)
                            pe.wait_ge(S("logit"), n + 1)
                            nc.tensor.matmul(m.bank[4 + s % 2][:, 0:2 * HEADS], m.selt[:, s, :],
                                             m.own[:, bass.ds(d * 2 * HEADS, 2 * HEADS)], start=True, stop=True)\
                                .then_inc(S("dst_values"), 1)

                        for step in range(GT + 3):
                            if step < GT:
                                turn_selection(step)
                            if 1 <= step <= GT:
                                dst_values(step - 1)
                            if step >= 3:
                                pe.wait_ge(S("message"), v * GT + step - 3 + 1)
                                add(step - 3, m.msg[:, step - 3, :])
                nc.tensor.matmul(m.acc[:, 0:columns], m.zeros[:, 0:NB], m.zeros[:, 0:columns], start=False, stop=True)\
                    .then_inc(S("block_summed"), 1)
                pe_tile(pe, S, d)
    clear(nc, S)


def load(sp, S, count, pairs):
    for out, in_ in pairs:
        sp.dma_start(out, in_).then_inc(S("loaded"), 16)


class Loads:

    def __init__(self, pairs):
        self.pairs, self.count = pairs, len(pairs)

    def __call__(self, sp, S):
        for out, in_ in self.pairs:
            sp.dma_start(out, in_, allow_slow_non_contiguous=True).then_inc(S("loaded"), 16)


def across(ap, p=NB):
    return ap.partition_broadcast(p)


def first_block(nc, m, table, w_table, w_self, bias, loads):
    ctx = ExitStack()
    with ctx:
        S = Signals(ctx, nc, "first")
        block = ctx.enter_context(nc.Block())

        @block.sync
        def _(sp):
            loads(sp, S)
            sp.wait_ge(S("loaded"), 16 * loads.count)
            sp.sem_inc(S("weights_in"), 1)
            sp.wait_ge(S("stored"), 16 * BLOCKS + 16)

        @block.vector
        def _(dve):
            dve.wait_ge(S("weights_in"), 1)
            with dve.Fori(0, BLOCKS) as t:
                dve.wait_ge(S("done"), t + 1)
                norm_dve(nc, m, S, dve, t, m.x[:, bass.ds(t * D, D)])
                own_part_dve(nc, m, S, dve, t, bias)

        @block.scalar
        def _(act):
            first_store(act, m, S)
            with act.Fori(0, BLOCKS) as t:
                norm_act(nc, m, S, act, t)
                turn_act(nc, m, S, act, t)
                store_act(nc, m, S, act, t, m.bank[6][0:NB, 0:D], D, table, "table_rows")

        @block.tensor
        def _(pe):
            pe.sem_inc(S("stage"), 1)
            pe.sem_inc(S("done"), 1)
            pe.wait_ge(S("weights_in"), 1)
            with pe.Fori(0, BLOCKS) as t:
                turn_pe(nc, m, S, pe, t)
                table_and_own_pe(nc, m, S, pe, t, w_table, w_self)
    clear(nc, S)


def table_and_own_pe(nc, m, S, pe, t, w_table, w_self):
    pe.wait_ge(S("norm_xt"), t + 1)
    product(nc, m.bank[6][0:NB, 0:D], m.xt, w_table, S("table_rows"))
    product(nc, m.bank[7][0:NB, 0:D], m.xt, w_self, S("own_rows"))


def own_part_dve(nc, m, S, dve, t, bias):
    dve.wait_ge(S("own_rows"), t + 1)
    dve.wait_ge(S("stage"), t + 2)
    nc.vector.tensor_tensor(m.y[:, bass.ds(t * D, D)], m.bank[7][0:NB, 0:D], bias, ALU.add).then_inc(S("done"), 1)


def sage_pass(nc, m, name, table, next_table, w_table, w_self, bias, degrees, loads):
    def dve_tile(dve, S, d):
        dve.wait_ge(S("block_summed"), d + 1)
        dve.wait_ge(S("done"), d + 1)
        if degrees:
            c = Chain(dve, S("degree_steps"), d, 4)
            at = bass.ds(d, 1)
            c.link(nc.vector.tensor_scalar(m.has[:, at], m.acc[:, D:D + 1], 1.0, None, ALU.min))
            c.link(nc.vector.tensor_scalar(m.deg[:, :], m.acc[:, D:D + 1], 1.0, None, ALU.max))
            c.link(nc.vector.reciprocal(m.rdeg[:, :], m.deg[:, :]))
            c.link(nc.vector.tensor_tensor(m.inv[:, at], m.has[:, at], m.rdeg[:, :], ALU.mult))
            c.end()
        nc.vector.scalar_tensor_tensor(m.h[:, :], m.acc[:, 0:D], m.inv[:, bass.ds(d, 1)], m.y[:, bass.ds(d * D, D)],
                                       ALU.mult, ALU.add).then_inc(S("acc_read"), 1)
        own_part_dve(nc, m, S, dve, d, bias)

    def act_tile(act, S, d):
        act.wait_ge(S("acc_read"), d + 2)
        nc.scalar.activation(m.xn[:, :], m.h[:, :], ACT.Relu).then_inc(S("norm_xn"), 1)
        turn_act(nc, m, S, act, d)
        store_act(nc, m, S, act, d, m.bank[6][0:NB, 0:D], D, next_table, "table_rows")

    def pe_tile(pe, S, d):
        turn_pe(nc, m, S, pe, d)
        table_and_own_pe(nc, m, S, pe, d, w_table, w_self)

    edge_pass(nc, m, name, table, D, "degrees" if degrees else "sum", pe_tile, act_tile, dve_tile, sp_loads=loads, stores=1)


def root_row(nc, m, name, table, root_idx, w, leaky, bias, out, loads):
    ctx = ExitStack()
    with ctx:
        S = Signals(ctx, nc, name)
        row, turned = m.scratch[:, 0:D], m.scratch[:, D:D + 256].rearrange("p (k n) -> p k n", k=2)
        soft = m.scratch[:, 2 * D:3 * D]
        rows_before = m.root_count
        m.root_count += 16
        block = ctx.enter_context(nc.Block())

        @block.sync
        def _(sp):
            loads(sp, S)
            sp.dma_start(m.root_in[:, :], root_idx[0:1].partition_broadcast(128)).then_inc(S("root_in"), 16)
            sp.wait_ge(S("loaded"), 16 * loads.count)
            sp.wait_ge(S("root_in"), 16)

        @block.vector
        def _(dve):
            dve.wait_ge(S("root_in"), 16)
            nc.vector.tensor_scalar(m.root[:, :], m.root_in[:, :], N - 1, None, ALU.min).then_inc(S("root"), 1)
            dve.wait_ge(m.root_arrived, rows_before + 16)
            nc.vector.scalar_tensor_tensor(soft, row, 0.01 if leaky else 1.0, row, ALU.mult, ALU.max).then_inc(S("soft"), 1)
            dve.wait_ge(S("sums"), 1)
            if bias is None:
                nc.vector.tensor_copy(out, m.bank[6][0:NB, 0:D]).then_inc(S("out"), 1)
            else:
                nc.vector.tensor_tensor(out, m.bank[6][0:NB, 0:D], bias, ALU.add).then_inc(S("out"), 1)

        @block.gpsimd
        def _(pool):
            pool.wait_ge(S("root"), 1)
            pool.indirect_dma_start(out=row, out_offset=None, in_=table,
                                    in_offset=bass.IndirectOffsetOnAxis(ap=m.root[:, 0:1], axis=0)).then_inc(m.root_arrived, 16)
            pool.wait_ge(m.root_arrived, rows_before + 16)

        @block.scalar
        def _(act):
            act.wait_ge(S("turned"), 1)
            nc.scalar.copy(turned, m.bank[3][:, 0:256].rearrange("p (k n) -> p k n", k=2)).then_inc(S("turned_in"), 1)

        @block.tensor
        def _(pe):
            pe.wait_ge(S("soft"), 1)
            nc.tensor.transpose(m.bank[3][:, 0:128], soft[:, 0:128], m.ident[:, :])
            nc.tensor.transpose(m.bank[3][:, 128:256], soft[:, 128:256], m.ident[:, :]).then_inc(S("turned"), 1)
            pe.wait_ge(S("turned_in"), 1)
            pe.wait_ge(S("loaded"), 16 * loads.count)
            product(nc, m.bank[6][0:NB, 0:D], turned[:, :, 0:NB], w, S("sums"))
    clear(nc, S)


def loaded(eng, S, loads):
    eng.wait_ge(S("loaded"), 16 * loads.count)


def experts_pe(nc, m, S, pe, t, experts, biases):
    def before_outputs():
        router_pe(nc, m, S, pe, t, experts.count)
        pe.wait_ge(S("ct"), t + 1)
        nc.tensor.matmul(m.bank[6][0:NB, 0:D], m.ct[0:experts.count, :], biases, start=True, stop=True)\
            .then_inc(S("outputs"), 1)
    experts.pe(nc, m, S, pe, t, before_outputs)


def table_act(nc, m, S, act, t, table, rows, signal, ahead=0):
    act.wait_ge(S(signal), t + (1 + ahead))
    act.dma_start(table[bass.ds(t * NB, NB), :], rows).then_inc(S("stored"), 16)


def sage_experts_pass(nc, m, a, table, next_table, norm_table):
    take, vec = m.weights.take, m.vectors.take
    m.weights.reset()
    m.vectors.reset(keep=m.sage_vectors)
    w1 = take(8 * 2 * 512).rearrange("p (e k f) -> p e k f", e=8, k=2)
    w2 = take(8 * 4 * D).rearrange("p (e k f) -> p e k f", e=8, k=4)
    wg = vec(16).rearrange("p (k e) -> p k e", k=2)
    b1 = vec(32).rearrange("p (e c) -> p e c", e=8)
    b2 = vec(D)[0:8]
    bg, bg2, rb = vec(8)[0:NB], vec(8)[0:NB], vec(8)[0:NB]
    w_next = take(2 * D).rearrange("p (k f) -> p k f", k=2)
    loads = Loads([(wg, chunks(a["L0_ffn_Wg"])), (bg, across(a["L0_ffn_bg"])), (bg2, across(a["L0_ffn_bias"])),
                   (b2, a["L0_ffn_b2"]), (w_next, chunks(a["L1_gnn_W1"]))] +
                  [(b1[:, e], a["L0_ffn_b1"][e].rearrange("(c p) -> p c", p=128)) for e in range(8)] +
                  [(w1[:, e], chunks(a["L0_ffn_W1"][e])) for e in range(8)] +
                  [(w2[:, e], chunks(a["L0_ffn_W2"][e])) for e in range(8)])
    experts = Experts(8, [(2, 4, 128, lambda e, k, c: w1[:, e, k, c * 128:(c + 1) * 128], lambda e, c: b1[:, e, c:c + 1])],
                      lambda e, k: w2[:, e, k, :], 4, 128)

    def dve_tile(dve, S, d):
        loaded(dve, S, loads)
        rows = m.x[:, bass.ds(d * D, D)]
        dve.wait_ge(S("block_summed"), d + 1)
        dve.wait_ge(S("stage"), d + 1)
        dve.wait_ge(S("stored"), d * 32 + 16)
        c = Chain(dve, S("entry_steps"), d, 2)
        nc.vector.scalar_tensor_tensor(m.h[:, :], m.acc[:, 0:D], m.inv[:, bass.ds(d, 1)], m.y[:, bass.ds(d * D, D)],
                                       ALU.mult, ALU.add).then_inc(S("acc_read"), 1)
        dve.wait_ge(S("acc_read"), d + 2)
        c.link(nc.vector.tensor_tensor(rows, rows, m.h[:, :], ALU.add))
        c.link(nc.vector.tensor_tensor(rb, bg, bg2, ALU.add))
        c.end()
        norm_dve(nc, m, S, dve, d, rows)
        router_dve(nc, m, S, dve, d, m.bank[6][0:NB, 0:8], rb, 8, False, 2)
        experts.dve(nc, m, S, dve, d, rows)
        norm_dve(nc, m, S, dve, d, rows, "next")

    def act_tile(act, S, d):
        norm_act(nc, m, S, act, d)
        turn_act(nc, m, S, act, d)
        router_act(nc, m, S, act, d, 8, False, 2, turn=False)
        loaded(act, S, loads)
        experts.act(nc, m, S, act, d, lambda: router_turned_act(nc, m, S, act, d, 8))
        norm_act(nc, m, S, act, d, "next")
        turn_act(nc, m, S, act, d, "next")
        table_act(nc, m, S, act, d, norm_table, m.xn[:, :], "next_xn")
        store_act(nc, m, S, act, d, m.bank[6][0:NB, 0:D], D, next_table, "table_rows", per_block=2)

    def pe_tile(pe, S, d):
        loaded(pe, S, loads)
        turn_pe(nc, m, S, pe, d)
        pe.wait_ge(S("norm_xt"), d + 1)
        product(nc, m.bank[6][0:NB, 0:8], m.xt, wg, S("logits"))
        experts_pe(nc, m, S, pe, d, experts, b2)
        turn_pe(nc, m, S, pe, d, "next")
        pe.wait_ge(S("next_xt"), d + 1)
        product(nc, m.bank[6][0:NB, 0:D], m.xt, w_next, S("table_rows"))

    edge_pass(nc, m, "sage2", table, D, "sum", pe_tile, act_tile, dve_tile, sp_loads=loads, stores=2)


def conv_pass(nc, m, a, table, next_table, conv_table):
    take, vec = m.weights.take, m.vectors.take
    m.weights.reset()
    m.vectors.reset(keep=m.root_vectors)
    w2 = take(2 * D).rearrange("p (k f) -> p k f", k=2)
    b1 = vec(D)[0:NB]
    loads = Loads([(w2, chunks(a["L1_gnn_W2"][0:D])), (b1, across(a["L1_gnn_b1"]))])

    def dve_tile(dve, S, d):
        loaded(dve, S, loads)
        dve.wait_ge(S("block_summed"), d + 1)
        dve.wait_ge(S("stored"), d * 32 + 16)
        nc.vector.tensor_tensor(m.h[:, :], m.acc[:, 0:D], b1, ALU.add).then_inc(S("acc_read"), 1)
        dve.wait_ge(S("acc_read"), d + 2)
        nc.vector.scalar_tensor_tensor(m.xn[:, :], m.h[:, :], 0.01, m.h[:, :], ALU.mult, ALU.max).then_inc(S("norm_xn"), 1)
        dve.wait_ge(S("table_sums"), d + 1)
        nc.vector.tensor_tensor(m.stage[:, 0:D], m.bank[6][0:NB, 0:D], m.root_out[0:NB], ALU.add).then_inc(S("table_rows"), 1)

    def act_tile(act, S, d):
        table_act(nc, m, S, act, d, conv_table, m.h[:, :], "acc_read", ahead=1)
        turn_act(nc, m, S, act, d)
        table_act(nc, m, S, act, d, next_table, m.stage[:, 0:D], "table_rows")

    def pe_tile(pe, S, d):
        loaded(pe, S, loads)
        turn_pe(nc, m, S, pe, d)
        pe.wait_ge(S("norm_xt"), d + 1)
        product(nc, m.bank[6][0:NB, 0:D], m.xt, w2, S("table_sums"))

    edge_pass(nc, m, "conv1", table, D, "sum", pe_tile, act_tile, dve_tile, weight=m.w_c, sp_loads=loads, stores=2)


def conv_experts_pass(nc, m, a, table, next_table, logit_table):
    take, vec = m.weights.take, m.vectors.take
    m.weights.reset()
    m.vectors.reset(keep=m.root_vectors)
    square = lambda: take(6 * 2 * D).rearrange("p (e k f) -> p e k f", e=6, k=2)
    wl = take(2 * D).rearrange("p (k f) -> p k f", k=2)
    e1, e2, e3 = square(), square(), square()
    r1 = take(2 * 128).rearrange("p (k f) -> p k f", k=2)
    w_next = take(2 * D).rearrange("p (k f) -> p k f", k=2)
    r2, rb1, rb2 = vec(6), vec(1), vec(6)[0:NB]
    conv_b = vec(D)[0:NB]
    bias1 = vec(12).rearrange("p (e c) -> p e c", e=6)
    bias2 = vec(12).rearrange("p (e c) -> p e c", e=6)
    bias3 = vec(D)[0:6]
    att_s, att_d = vec(D)[0:NB], vec(D)[0:NB]
    loads = Loads([(wl, chunks(a["L1_gnn_Wl"][0:D])), (r1, chunks(a["L1_ffn_router_w1"])), (w_next, chunks(a["L2_gnn_W"])),
                   (r2, a["L1_ffn_router_w2"]), (rb1, a["L1_ffn_router_b1"].rearrange("(p c) -> p c", c=1)),
                   (rb2, across(a["L1_ffn_router_b2"])), (conv_b, across(a["L1_gnn_b2"])), (bias3, a["L1_ffn_expert_b3"]),
                   (att_s, across(a["L2_gnn_att_src"].rearrange("a h f -> (a h f)"))),
                   (att_d, across(a["L2_gnn_att_dst"].rearrange("a h f -> (a h f)")))] +
                  [(b[:, e], a[n][e].rearrange("(c p) -> p c", p=128)) for e in range(6)
                   for b, n in ((bias1, "L1_ffn_expert_b1"), (bias2, "L1_ffn_expert_b2"))] +
                  [(w[:, e], chunks(a[n][e])) for e in range(6)
                   for w, n in ((e1, "L1_ffn_expert_w1"), (e2, "L1_ffn_expert_w2"), (e3, "L1_ffn_expert_w3"))])
    layer = lambda w, b: (2, 2, 128, lambda e, k, c: w[:, e, k, c * 128:(c + 1) * 128], lambda e, c: b[:, e, c:c + 1])
    experts = Experts(6, [layer(e1, bias1), layer(e2, bias2)], lambda e, k: e3[:, e, k, :], 2, 128)
    heads = lambda ap: ap.rearrange("p (h f) -> p h f", h=HEADS)

    def dve_tile(dve, S, d):
        loaded(dve, S, loads)
        rows = m.x[:, bass.ds(d * D, D)]
        dve.wait_ge(S("block_summed"), d + 1)
        dve.wait_ge(S("stored"), d * 32 + 16)
        nc.vector.tensor_tensor(m.h[:, :], m.acc[:, 0:D], conv_b, ALU.add).then_inc(S("acc_read"), 1)
        dve.wait_ge(S("acc_read"), d + 2)
        nc.vector.scalar_tensor_tensor(m.xn[:, :], m.h[:, :], 0.01, m.h[:, :], ALU.mult, ALU.max).then_inc(S("conv_xn"), 1)
        c = Chain(dve, S("entry_steps"), d, 3)
        dve.wait_ge(S("conv_rows"), d + 1)
        c.link(nc.vector.tensor_tensor(m.h[:, :], m.bank[6][0:NB, 0:D], m.root_out[0:NB], ALU.add))
        c.link(nc.vector.scalar_tensor_tensor(m.h2[:, :], m.h[:, :], 0.01, m.h[:, :], ALU.mult, ALU.max))
        c.link(nc.vector.tensor_tensor(rows, rows, m.h2[:, :], ALU.add))
        c.end()
        norm_dve(nc, m, S, dve, d, rows)
        router_dve(nc, m, S, dve, d, m.bank[6][0:NB, 0:6], rb2, 6, True, 2)
        experts.dve(nc, m, S, dve, d, rows)
        norm_dve(nc, m, S, dve, d, rows, "next")
        dve.wait_ge(S("stage"), d + 2)
        q = Chain(dve, S("logit_parts"), d, 4)
        own = m.bank[6][0:NB, 0:D]
        q.link(nc.vector.tensor_tensor(m.h[:, :], own, att_s, ALU.mult))
        q.link(nc.vector.tensor_reduce(m.as_[:, bass.ds(d * HEADS, HEADS)], heads(m.h[:, :]), AX, ALU.add))
        q.link(nc.vector.tensor_tensor(m.h2[:, :], own, att_d, ALU.mult))
        q.link(nc.vector.tensor_reduce(m.own[0:NB, bass.ds(d * 2 * HEADS, HEADS)], heads(m.h2[:, :]), AX, ALU.add))
        q.end()
        dve.sem_inc(S("turn"), 1)
        nc.vector.tensor_copy(m.stage[:, D:GW], m.as_[:, bass.ds(d * HEADS, HEADS)]).then_inc(S("stage_logits"), 1)
        nc.vector.tensor_copy(m.y[:, bass.ds(d * D, D)], own).then_inc(S("own_rows"), 1)

    def act_tile(act, S, d):
        turn_act(nc, m, S, act, d, "conv")
        norm_act(nc, m, S, act, d)
        turn_act(nc, m, S, act, d)
        loaded(act, S, loads)
        act.wait_ge(S("router_hidden"), d + 1)
        nc.scalar.activation(m.rt[:, :], m.bank[7][:, 0:NB], ACT.Relu, bias=rb1).then_inc(S("rt"), 1)
        router_act(nc, m, S, act, d, 6, True, 2, turn=False)
        experts.act(nc, m, S, act, d, lambda: router_turned_act(nc, m, S, act, d, 6))
        norm_act(nc, m, S, act, d, "next")
        turn_act(nc, m, S, act, d, "next")
        act.wait_ge(S("table_rows"), d + 1)
        nc.scalar.copy(m.stage[:, 0:D], m.bank[6][0:NB, 0:D]).then_inc(S("stage"), 1)
        act.wait_ge(S("stage"), d + 2)
        table_act(nc, m, S, act, d, next_table, m.stage[:, :], "own_rows")
        table_act(nc, m, S, act, d, logit_table, m.stage[:, D:GW], "own_rows")

    def pe_tile(pe, S, d):
        loaded(pe, S, loads)
        turn_pe(nc, m, S, pe, d, "conv")
        pe.wait_ge(S("conv_xt"), d + 1)
        product(nc, m.bank[6][0:NB, 0:D], m.xt, wl, S("conv_rows"))
        turn_pe(nc, m, S, pe, d)
        pe.wait_ge(S("norm_xt"), d + 1)
        for k in range(2):
            last = nc.tensor.matmul(m.bank[7][:, 0:NB], r1[:, k, :], m.xt[:, k, :], start=(k == 0), stop=(k == 1))
        last.then_inc(S("router_hidden"), 1)
        pe.wait_ge(S("rt"), d + 1)
        nc.tensor.matmul(m.bank[6][0:NB, 0:6], m.rt[:, :], r2, start=True, stop=True).then_inc(S("logits"), 1)
        experts_pe(nc, m, S, pe, d, experts, bias3)
        turn_pe(nc, m, S, pe, d, "next")
        pe.wait_ge(S("next_xt"), d + 1)
        product(nc, m.bank[6][0:NB, 0:D], m.xt, w_next, S("table_rows"))

    edge_pass(nc, m, "conv2", table, D, "sum", pe_tile, act_tile, dve_tile, weight=m.w_c, sp_loads=loads, stores=2)


def peak_pass(nc, m, logit_table):
    def dve_tile(dve, S, d):
        at = bass.ds(d, 1)
        as_, ad = m.as_[:, bass.ds(d * HEADS, HEADS)], m.own[0:NB, bass.ds(d * 2 * HEADS, HEADS)]
        dve.wait_ge(S("block_summed"), d + 1)
        nc.vector.tensor_tensor(m.p0[:, :], m.acc[:, 0:HEADS], ad, ALU.add).then_inc(S("acc_read"), 1)
        dve.wait_ge(S("acc_read"), d + 2)
        c = Chain(dve, S("peak_steps"), d, 6)
        c.link(nc.vector.scalar_tensor_tensor(m.p1[:, :], m.p0[:, :], 0.2, m.p0[:, :], ALU.mult, ALU.max))
        c.link(nc.vector.tensor_scalar(m.none[:, :], m.has[:, at], -1.0, -LOWEST, ALU.add, ALU.mult))
        c.link(nc.vector.tensor_scalar(m.p2[:, :], m.p1[:, :], m.has[:, at], m.none[:, :], ALU.mult, ALU.add))
        c.link(nc.vector.tensor_tensor(m.p0[:, :], as_, ad, ALU.add))
        c.link(nc.vector.scalar_tensor_tensor(m.p1[:, :], m.p0[:, :], 0.2, m.p0[:, :], ALU.mult, ALU.max))
        largest = m.own[0:NB, bass.ds(d * 2 * HEADS + HEADS, HEADS)]
        c.link(nc.vector.tensor_tensor(largest, m.p1[:, :], m.p2[:, :], ALU.max))
        c.end()
        nc.vector.tensor_tensor(m.as_[:, bass.ds(d * HEADS, HEADS)], m.p1[:, :], largest, ALU.subtract)\
            .then_inc(S("own_logit"), 1)
        dve.wait_ge(S("own_logit"), d + 1)

    nothing = lambda eng, S, d: None
    edge_pass(nc, m, "peak", logit_table, HEADS, "max", nothing, nothing, dve_tile, weight=m.last_c)


def attention_experts_pass(nc, m, a, table, next_table):
    take, vec = m.weights.take, m.vectors.take
    m.weights.reset()
    m.vectors.reset()
    w1 = take(2 * 2048).rearrange("p (k f) -> p k f", k=2)
    w2 = take(16 * D).rearrange("p (q f) -> p q f", q=16)
    wr = take(64).rearrange("p (k f) -> p k f", k=2)
    theta, phi, diff = (take(2 * D).rearrange("p (k f) -> p k f", k=2) for _ in range(3))
    gat_b, tb, pb = vec(D)[0:NB], vec(D)[0:NB], vec(D)[0:NB]
    rb = vec(32)[0:NB]
    b1 = vec(16)
    b2 = vec(D)[0:32]
    loads = Loads([(wr, chunks(a["L2_ffn_router_w"])), (theta, chunks(a["L3_gnn_theta_w"])), (phi, chunks(a["L3_gnn_phi_w"])),
                   (gat_b, across(a["L2_gnn_bias"])), (tb, across(a["L3_gnn_theta_b"])), (pb, across(a["L3_gnn_phi_b"])),
                   (rb, across(a["L2_ffn_router_b"])), (b2, a["L2_ffn_b2"]),
                   (b1, a["L2_ffn_b1"].rearrange("(q e) h -> (e h) q", e=2)),
                   (w2, a["L2_ffn_W2"].rearrange("(q e) h f -> (e h) q f", e=2))] +
                  [(w1[:, k, :].rearrange("p (e h) -> p e h", h=64), a["L2_ffn_W1"][:, k * 128:(k + 1) * 128, :].rearrange("e p h -> p e h"))
                   for k in range(2)])
    heads = lambda ap: ap.rearrange("p (h f) -> p h f", h=HEADS)
    wide = lambda ap: ap.unsqueeze(2).to_broadcast([NB, HEADS, HD])
    mask_bank = [m.bank[7], m.bank[3]]

    def dve_tile(dve, S, d):
        loaded(dve, S, loads)
        rows, y = m.x[:, bass.ds(d * D, D)], m.y[:, bass.ds(d * D, D)]
        dve.wait_ge(S("block_summed"), d + 1)
        dve.wait_ge(S("stage"), d + 1)
        dve.wait_ge(S("own_weight"), d + 1)
        c = Chain(dve, S("entry_steps"), d, 9)
        c.link(nc.vector.tensor_tensor(diff, phi, theta, ALU.subtract))
        c.link(nc.vector.tensor_tensor(m.h[:, :], tb, pb, ALU.add))
        c.link(nc.vector.tensor_tensor(heads(m.h2[:, :]), heads(y), wide(m.p1[:, :]), ALU.mult))
        c.link(nc.vector.tensor_tensor(m.p2[:, :], m.acc[:, D:GW], m.p1[:, :], ALU.add))
        c.link(nc.vector.reciprocal(m.p0[:, :], m.p2[:, :]))
        c.link(nc.vector.tensor_tensor(m.h2[:, :], m.acc[:, 0:D], m.h2[:, :], ALU.add))
        c.link(nc.vector.tensor_tensor(heads(m.xn[:, :]), heads(m.h2[:, :]), wide(m.p0[:, :]), ALU.mult))
        c.link(nc.vector.tensor_tensor(m.h2[:, :], m.xn[:, :], gat_b, ALU.add))
        c.link(nc.vector.tensor_tensor(rows, rows, m.h2[:, :], ALU.add))
        c.end()
        dve.sem_inc(S("acc_read"), 1)
        norm_dve(nc, m, S, dve, d, rows)
        router_dve(nc, m, S, dve, d, m.bank[6][0:NB, 0:32], rb, 32, False, 1)
        for b in range(4):
            dve.wait_ge(S("masks"), d * 4 + b + 1)
            dve.wait_ge(S("hidden"), d * 4 + b + 1)
            ht = m.ht[:, b].rearrange("p c n -> p (c n)")
            nc.vector.tensor_tensor(ht, ht, mask_bank[b % 2][:, 0:4 * NB], ALU.mult).then_inc(S("masked"), 1)
        dve.wait_ge(S("outputs"), d + 1)
        nc.vector.scalar_tensor_tensor(rows, m.bank[6][0:NB, 0:D], 0.0, rows, ALU.max, ALU.add).then_inc(S("added"), 1)
        dve.wait_ge(S("added"), d + 1)
        norm_dve(nc, m, S, dve, d, rows, "next")
        dve.wait_ge(S("own_rows"), d + 1)
        nc.vector.tensor_tensor(y, m.bank[7][0:NB, 0:D], m.h[:, :], ALU.add).then_inc(S("y"), 1)

    def act_tile(act, S, d):
        act.wait_ge(S("y"), d + 1)
        nc.scalar.activation(m.p1[:, :], m.as_[:, bass.ds(d * HEADS, HEADS)], ACT.Exp).then_inc(S("own_weight"), 1)
        norm_act(nc, m, S, act, d)
        turn_act(nc, m, S, act, d)
        loaded(act, S, loads)
        for b in range(4):
            if b == 3:
                act.wait_ge(S("weights_turned"), d + 1)
                nc.scalar.copy(m.ct[0:32, :], m.bank[3][0:32, 256:256 + NB]).then_inc(S("ct"), 1)
                nc.scalar.copy(m.ctb[:, :], m.bank[3][0:32, 256:256 + NB]).then_inc(S("ct"), 1)
            act.wait_ge(S("hidden_sums"), d * 4 + b + 1)
            for c in range(4):
                last = nc.scalar.activation(m.ht[:, b, c, :], m.hid[b][:, c * NB:(c + 1) * NB], ACT.Relu,
                                            bias=b1[:, 4 * b + c:4 * b + c + 1])
            last.then_inc(S("hidden"), 1)
        norm_act(nc, m, S, act, d, "next")
        turn_act(nc, m, S, act, d, "next")
        store_act(nc, m, S, act, d, m.bank[6][0:NB, 0:D], D, next_table, "table_rows")

    def pe_tile(pe, S, d):
        loaded(pe, S, loads)
        turn_pe(nc, m, S, pe, d)
        pe.wait_ge(S("norm_xt"), d + 1)
        product(nc, m.bank[6][0:NB, 0:32], m.xt, wr, S("logits"))
        for b in range(4):
            for c in range(4):
                q = 4 * b + c
                for k in range(2):
                    last = nc.tensor.matmul(m.hid[b][:, c * NB:(c + 1) * NB], w1[:, k, q * 128:(q + 1) * 128],
                                            m.xt[:, k, :], start=(k == 0), stop=(k == 1))
            last.then_inc(S("hidden_sums"), 1)
        router_pe(nc, m, S, pe, d, 32)
        pe.wait_ge(S("ct"), 2 * d + 2)

        def masks(b):
            if b >= 2:
                pe.wait_ge(S("masked"), d * 4 + b - 1)
            for c in range(4):
                q = 4 * b + c
                last = nc.tensor.matmul(mask_bank[b % 2][:, c * NB:(c + 1) * NB], m.spread[:, q * 128:(q + 1) * 128],
                                        m.ctb[:, :], start=True, stop=True)
            last.then_inc(S("masks"), 1)

        masks(0)
        masks(1)
        nc.tensor.matmul(m.bank[6][0:NB, 0:D], m.ct[0:32, :], b2, start=True, stop=False)
        for b in range(4):
            pe.wait_ge(S("masked"), d * 4 + b + 1)
            if b + 2 < 4:
                masks(b + 2)
            for c in range(4):
                last = nc.tensor.matmul(m.bank[6][0:NB, 0:D], m.ht[:, b, c, :], w2[:, 4 * b + c, :],
                                        start=False, stop=(4 * b + c == 15))
        last.then_inc(S("outputs"), 1)
        turn_pe(nc, m, S, pe, d, "next")
        pe.wait_ge(S("next_xt"), d + 1)
        product(nc, m.bank[6][0:NB, 0:D], m.xt, diff, S("table_rows"))
        product(nc, m.bank[7][0:NB, 0:D], m.xt, theta, S("own_rows"))

    edge_pass(nc, m, "attend", table, GW, "attention", pe_tile, act_tile, dve_tile, sp_loads=loads, stores=1)


def edge_conv_experts_pass(nc, m, a, table, out):
    take, vec = m.weights.take, m.vectors.take
    m.weights.reset()
    m.vectors.reset()
    s1 = take(2 * D).rearrange("p (k f) -> p k f", k=2)
    s2 = take(2 * 128).rearrange("p (k f) -> p k f", k=2)
    s3 = take(D)
    e1 = take(4 * 2 * 128).rearrange("p (e k f) -> p e k f", e=4, k=2)
    e2 = take(4 * 64).rearrange("p (e f) -> p e f", e=4)
    e3 = take(4 * D)[0:64].rearrange("p (e f) -> p e f", e=4)
    wg = vec(8).rearrange("p (k e) -> p k e", k=2)
    sb1, sb2 = vec(2), vec(1)
    sb3 = vec(D)[0:NB]
    eb1, eb2 = vec(4), vec(4)[0:64]
    eb3 = vec(D)[0:4]
    gb = vec(4)[0:NB]
    column = lambda v: v.rearrange("(c p) -> p c", p=128)
    loads = Loads([(s1, chunks(a["L3_ffn_sW1"])), (s2, chunks(a["L3_ffn_sW2"])), (s3, a["L3_ffn_sW3"]),
                   (wg, chunks(a["L3_ffn_gW"])), (sb1, column(a["L3_ffn_sb1"])), (sb2, column(a["L3_ffn_sb2"])),
                   (sb3, across(a["L3_ffn_sb3"])), (eb1, a["L3_ffn_eb1"].rearrange("e p -> p e")),
                   (eb2, a["L3_ffn_eb2"].rearrange("e p -> p e")), (eb3, a["L3_ffn_eb3"]), (gb, across(a["L3_ffn_gb"])),
                   (e2, a["L3_ffn_eW2"].rearrange("e p f -> p e f")), (e3, a["L3_ffn_eW3"].rearrange("e p f -> p e f"))] +
                  [(e1[:, e], chunks(a["L3_ffn_eW1"][e])) for e in range(4)])
    experts = Experts(4, [(2, 1, 128, lambda e, k, c: e1[:, e, k, :], lambda e, c: eb1[:, e:e + 1]),
                          (1, 1, 64, lambda e, k, c: e2[:, e, :], lambda e, c: eb2[:, e:e + 1])],
                      lambda e, k: e3[:, e, :], 1, 64)
    shared = m.shared

    def dve_tile(dve, S, d):
        loaded(dve, S, loads)
        rows = m.x[:, bass.ds(d * D, D)]
        dve.wait_ge(S("block_summed"), d + 1)
        nc.vector.tensor_tensor(m.h[:, :], m.acc[:, 0:D], m.y[:, bass.ds(d * D, D)], ALU.add).then_inc(S("acc_read"), 1)
        dve.wait_ge(S("acc_read"), d + 2)
        c = Chain(dve, S("entry_steps"), d, 2)
        c.link(nc.vector.tensor_scalar(m.h2[:, :], m.h[:, :], 0.0, m.has[:, bass.ds(d, 1)], ALU.max, ALU.mult))
        c.link(nc.vector.tensor_tensor(rows, rows, m.h2[:, :], ALU.add))
        c.end()
        norm_dve(nc, m, S, dve, d, rows)
        router_dve(nc, m, S, dve, d, m.bank[6][0:NB, 0:4], gb, 4, True, 2)
        experts.dve(nc, m, S, dve, d, rows)
        nc.vector.tensor_tensor(rows, rows, sb3, ALU.add).then_inc(S("rows"), 1)

    def act_tile(act, S, d):
        norm_act(nc, m, S, act, d)
        turn_act(nc, m, S, act, d)
        loaded(act, S, loads)
        act.wait_ge(S("shared_sums"), 2 * d + 1)
        for c in range(2):
            last = nc.scalar.activation(shared[:, c, :], m.bank[7][:, c * NB:(c + 1) * NB], ACT.Relu, bias=sb1[:, c:c + 1])
        last.then_inc(S("shared"), 1)
        act.wait_ge(S("shared_sums"), 2 * d + 2)
        nc.scalar.activation(shared[:, 2, :], m.bank[7][:, 256:256 + NB], ACT.Relu, bias=sb2).then_inc(S("shared"), 1)
        router_act(nc, m, S, act, d, 4, True, 2, turn=False)
        experts.act(nc, m, S, act, d, lambda: router_turned_act(nc, m, S, act, d, 4))
        act.wait_ge(S("rows"), d + 1)
        act.dma_start(out[bass.ds(d * NB, NB), :], m.x[:, bass.ds(d * D, D)]).then_inc(S("stored"), 16)

    def pe_tile(pe, S, d):
        loaded(pe, S, loads)
        turn_pe(nc, m, S, pe, d)
        pe.wait_ge(S("norm_xt"), d + 1)
        product(nc, m.bank[6][0:NB, 0:4], m.xt, wg, S("logits"))
        for c in range(2):
            for k in range(2):
                last = nc.tensor.matmul(m.bank[7][:, c * NB:(c + 1) * NB], s1[:, k, c * 128:(c + 1) * 128], m.xt[:, k, :],
                                        start=(k == 0), stop=(k == 1))
        last.then_inc(S("shared_sums"), 1)
        pe.wait_ge(S("shared"), 2 * d + 1)
        for k in range(2):
            last = nc.tensor.matmul(m.bank[7][:, 256:256 + NB], s2[:, k, :], shared[:, k, :], start=(k == 0), stop=(k == 1))
        last.then_inc(S("shared_sums"), 1)

        def before_outputs():
            router_pe(nc, m, S, pe, d, 4)
            pe.wait_ge(S("ct"), d + 1)
            nc.tensor.matmul(m.bank[6][0:NB, 0:D], m.ct[0:4, :], eb3, start=True, stop=False)
            pe.wait_ge(S("shared"), 2 * d + 2)
            nc.tensor.matmul(m.bank[6][0:NB, 0:D], shared[:, 2, :], s3, start=False, stop=True).then_inc(S("outputs"), 1)
        experts.pe(nc, m, S, pe, d, before_outputs)

    edge_pass(nc, m, "peaks", table, D, "max", pe_tile, act_tile, dve_tile, weight=m.last_c, sp_loads=loads, stores=1)


class Arena:

    def __init__(self, tensor, size):
        self.tensor, self.size, self.used = tensor, size, 0

    def reset(self, keep=0):
        self.used = keep

    def take(self, columns):
        at, self.used = self.used, self.used + columns
        assert self.used <= self.size, (self.used, self.size)
        return self.tensor[:, at:at + columns]


def build(nc, a, out, stop=99):
    m = Memory()
    ctx = ExitStack()
    with ctx:
        def sb(name, shape, dt=F32):
            return ctx.enter_context(nc.sbuf_tensor(name, shape, dt))

        def small(names, widths):
            return [sb(n, [NB, w]) for n, w in zip(names.split(), widths)]

        m.arrived = [ctx.enter_context(nc.semaphore(f"rows_arrived_{k}")) for k in range(RT)]
        m.root_arrived = ctx.enter_context(nc.semaphore("root_arrived"))
        m.arrived_count = m.root_count = 0
        m.x = sb("x", [NB, BLOCKS * D])
        m.y = sb("y", [NB, BLOCKS * D])
        m.rows = sb("rows", [128, RT * GW])
        m.sel = sb("sel", [128, GT, NB])
        m.dst_c, m.w_c, m.last_c, m.dloc = (sb(n, [128, TILES]) for n in ("dst_c", "w_c", "last_c", "dloc"))
        m.src_c = sb("src_c", [128, TILES], I32)
        m.idx = sb("idx", [128, RT], I32)
        m.ident = sb("ident", [128, 128])
        m.iota = sb("iota", [128, 128])
        m.ones = sb("ones", [128, 1])
        m.zeros = sb("zeros", [1, 512], BF16)
        m.spread = sb("spread", [32, 2048], BF16)
        m.glo = sb("glo", [1, 26], I32)
        m.fr = sb("fr", [1, GROUPS], I32)
        m.xn, m.h, m.h2 = small("xn h h2", [D, D, D])
        m.stage = sb("stage", [NB, GW])
        m.xt = sb("xt", [128, 2, NB])
        m.ht = sb("ht", [128, 4, 4, NB])
        m.rt = sb("rt", [128, NB])
        m.shared = sb("shared", [128, 3, NB])
        m.st, m.mv, m.ve, m.sd, m.rs = small("st mv ve sd rs", [6, 2, 1, 1, 1])
        m.has, m.inv, m.deg, m.rdeg, m.none = small("has inv deg rdeg none", [BLOCKS, BLOCKS, 1, 1, 1])
        m.p0, m.p1, m.p2, m.as_ = small("p0 p1 p2 as_", [HEADS, HEADS, HEADS, BLOCKS * HEADS])
        m.lg, m.ex, m.pr, m.v8, m.i8f, m.neg = small("lg ex pr v8 i8f neg", [32, 8, 8, 8, 8, 1])
        m.sm, m.sr, m.d12, m.e2, m.sm2, m.w12 = small("sm sr d12 e2 sm2 w12", [1, 1, 1, 1, 1, 2])
        m.c1, m.c2, m.c = small("c1 c2 c", [8, 8, 32])
        m.i8 = sb("i8", [NB, 8], U32)
        m.own = sb("own", [NB, BLOCKS * 2 * HEADS])
        m.ct = sb("ct", [32, NB])
        m.ctb = sb("ctb", [32, NB], BF16)
        m.root_in = sb("root_in", [128, 1], I32)
        m.root = sb("root", [128, 1], I32)
        m.scratch = sb("scratch", [128, RT * TE // 2 + 3 * GT * D])
        at = RT * TE // 2
        m.bar = m.scratch[:, 0:at].bitcast(BF16)
        cut = lambda n, w: m.scratch[:, at + n * GT * D:at + n * GT * D + GT * w].rearrange("p (s f) -> p s f", s=GT)
        m.gt, m.runt = cut(0, D), cut(1, D)
        m.run = m.scratch[:, at + 2 * GT * D:at + 3 * GT * D].rearrange("p (s h e) -> p s h e", s=GT, h=2)
        m.msg = m.scratch[:, 0:GT * GW].rearrange("p (s f) -> p s f", s=GT)
        m.selt = m.scratch[0:NB, 1100:1100 + GT * TE].rearrange("p (s f) -> p s f", s=GT)
        m.e0, m.e1, m.e3 = (m.scratch[:, 1700 + 16 * n:1716 + 16 * n].rearrange("p (s f) -> p s f", s=GT) for n in range(3))
        m.weights_t = sb("weights_t", [128, 8 * 2 * 512 + 8 * 4 * D + 2 * D])
        m.weights = Arena(m.weights_t, 8 * 2 * 512 + 8 * 4 * D + 2 * D)
        m.vectors_t = sb("vectors_t", [128, 1400])
        m.vectors = Arena(m.vectors_t, 1400)
        m.root_vectors = D
        m.root_out = m.vectors_t[:, 0:D]
        m.sage_vectors = 0
        m.bank = [ctx.enter_context(nc.psum_tensor(f"bank{i}", [128, 512], F32)) for i in range(8)]
        m.acc = m.bank[0][0:NB, :]
        m.hid = [m.bank[4], m.bank[5], m.bank[1], m.bank[2]]
        m.bars = nc.dram_tensor("bars", (1 + TILES * TE,), BF16).ap()
        dram = lambda name, width: nc.dram_tensor(name, (N, width), F32).ap()
        tables = [dram(f"table_{i}", D) for i in range(6)]
        norm_table, conv_table, attention_table, logit_table = (
            dram("norm_table", D), dram("conv_table", D), dram("attention_table", GW), dram("logit_table", HEADS))

        m.primer = dram("primer", 1)

        edge_tables(nc, m, a, None)
        m.weights.reset()
        m.vectors.reset()
        sage_w = m.weights.take(6 * 2 * D).rearrange("p (i k f) -> p i k f", i=6, k=2)
        sage_b = m.vectors.take(3 * D)[0:NB].rearrange("p (i f) -> p i f", i=3)
        loads = Loads([(m.x[:, :].rearrange("p (t f) -> p t f", f=D), a["x"].rearrange("(t p) f -> p t f", p=NB))] +
                      [(sage_w[:, i], chunks(a["L0_gnn_W_neigh"][i])) for i in range(3)] +
                      [(sage_w[:, 3 + i], chunks(a["L0_gnn_W_self"][i])) for i in range(3)] +
                      [(sage_b[:, i], across(a["L0_gnn_bias"][i])) for i in range(3)])
        first_block(nc, m, tables[0], sage_w[:, 0], sage_w[:, 3], sage_b[:, 0], loads)
        sage_pass(nc, m, "sage0", tables[0], tables[1], sage_w[:, 1], sage_w[:, 4], sage_b[:, 1], True, None)
        sage_pass(nc, m, "sage1", tables[1], tables[2], sage_w[:, 2], sage_w[:, 5], sage_b[:, 2], False, None)
        if stop > 1:
            sage_experts_pass(nc, m, a, tables[2], tables[3], norm_table)
        if stop > 2:
            m.weights.reset()
            m.vectors.reset(keep=m.root_vectors)
            w = m.weights.take(2 * D).rearrange("p (k f) -> p k f", k=2)
            root_row(nc, m, "root1", norm_table, a["L1_gnn_root_idx"], w, True, None, m.root_out[0:NB],
                     Loads([(w, chunks(a["L1_gnn_W2"][D:2 * D]))]))
            conv_pass(nc, m, a, tables[3], tables[4], conv_table)
            m.weights.reset()
            m.vectors.reset(keep=m.root_vectors)
            w = m.weights.take(2 * D).rearrange("p (k f) -> p k f", k=2)
            b = m.vectors.take(D)[0:NB]
            root_row(nc, m, "root2", conv_table, a["L1_gnn_root_idx"], w, False, b, m.root_out[0:NB],
                     Loads([(w, chunks(a["L1_gnn_Wl"][D:2 * D])), (b, across(a["L1_gnn_bl"]))]))
            conv_experts_pass(nc, m, a, tables[4], attention_table, logit_table)
        if stop > 3:
            peak_pass(nc, m, logit_table)
            attention_experts_pass(nc, m, a, attention_table, tables[5])
        if stop > 4:
            edge_conv_experts_pass(nc, m, a, tables[5], out)
        else:
            with nc.Block() as block:
                with nc.semaphore("debug") as dbg:
                    @block.sync
                    def _(sp):
                        sp.dma_start(out.rearrange("(t p) f -> p t f", p=NB), m.x[:, :].rearrange("p (t f) -> p t f", f=D)).then_inc(dbg, 16)
                        sp.wait_ge(dbg, 16)


TURNED = ("L2_ffn_router_w", "L3_gnn_theta_w", "L3_gnn_phi_w")
STOP = 99


def kernel(**inputs):
    import numpy as _np
    import concourse.bacc as _bacc
    from concourse.bass_utils import run_bass_kernel_spmd as _run

    nc = _bacc.Bacc("TRN2", target_bir_lowering=False, num_devices=1)
    arrays, a = {}, {}
    for name, value in inputs.items():
        v = _np.asarray(value)
        v = _np.ascontiguousarray(v.T if name in TURNED else v)
        arrays[f"in_{name}"] = v
        a[name] = nc.dram_tensor(f"in_{name}", v.shape, mybir.dt.from_np(v.dtype), kind="ExternalInput").ap()
    out = nc.dram_tensor("out_0_dram", (N, D), F32, kind="ExternalOutput").ap()
    build(nc, a, out, STOP)
    return _run(nc, [arrays], core_ids=[0]).results[0]["out_0_dram"]
```

```python
import concourse.bass as bass
import numpy as np
from concourse import mybir
from contextlib import ExitStack

F32, I32, U32, BF16 = mybir.dt.float32, mybir.dt.int32, mybir.dt.uint32, mybir.dt.bfloat16
ALU = mybir.AluOpType
ACT = mybir.ActivationFunctionType
AX = mybir.AxisListType.X

N, E, D = 3125, 50000, 256
NB, BLOCKS = 125, 25
TE = 128
GT = 4
GROUPS = -(-E // (TE * GT))
TILES = GROUPS * GT
RG = 7
ROUNDS = GROUPS // RG
RT = RG * GT
GW = 260
HEADS, HD = 4, 64
PARTS = 4
NOWHERE = 4000
LOWEST = -(2.0 ** 125)


class Signals:

    def __init__(self, ctx, nc, part):
        self.ctx, self.nc, self.part, self.by_name = ctx, nc, part, {}

    def __call__(self, name):
        if name not in self.by_name:
            self.by_name[name] = self.ctx.enter_context(self.nc.semaphore(f"{self.part}_{name}"))
        return self.by_name[name]


class Memory:
    pass


def clear(nc, signals):
    with nc.Block() as block:
        @block.gpsimd
        def _(pool):
            for s in signals.by_name.values():
                pool.sem_clear(s)


def chunks(ap, p=128):
    return ap.rearrange("(k p) m -> p k m", p=p)


def edge_tables(nc, m, a, parts):
    ctx = ExitStack()
    with ctx:
        S = Signals(ctx, nc, "edges")
        wide = 4 * TE
        m.weights.reset()
        take = m.weights.take
        cut = lambda ap: ap.rearrange("p (c j) -> p c j", j=TE)
        dst_i, nxt_i, src_i = (cut(take(wide).bitcast(I32)) for _ in range(3))
        rows = take(4 * wide).rearrange("p (n c j) -> p n c j", n=4, j=TE)
        nxt_f = cut(take(wide))
        bar = cut(take(wide // 2).bitcast(BF16))
        below = take(wide)
        bar0 = ctx.enter_context(nc.sbuf_tensor("bar0", [1, 2], BF16))
        cnt = ctx.enter_context(nc.sbuf_tensor("cnt", [128, 24], F32))
        ptr_i = ctx.enter_context(nc.sbuf_tensor("ptr_i", [1, 24], I32))
        glo_i = ctx.enter_context(nc.sbuf_tensor("glo_i", [1, 24], I32))
        glo_f = ctx.enter_context(nc.sbuf_tensor("glo_f", [1, 24], F32))
        steps = ctx.enter_context(nc.sbuf_tensor("steps", [1, GROUPS], F32))
        dl = ctx.enter_context(nc.sbuf_tensor("dl", [1, GROUPS], F32))
        more, firsts = (ctx.enter_context(nc.sbuf_tensor(n, [1, BLOCKS], I32)) for n in ("more", "firsts"))
        DST, SRC, WGT, LAST = range(4)

        def in_rows(eng, tile, dram, shift, signal):
            for c in range(3):
                at = shift + c * 128 * TE
                eng.dma_start(tile[:, c, :], dram[at:at + 128 * TE].rearrange("(p j) -> p j", j=TE)).then_inc(signal, 16)
            at = shift + 3 * 128 * TE
            full = (E - at) // TE
            eng.dma_start(tile[0:full, 3, :], dram[at:at + full * TE].rearrange("(p j) -> p j", j=TE)).then_inc(signal, 16)
            at += full * TE
            eng.dma_start(tile[full:full + 1, 3, 0:E - at], dram[at:E].rearrange("(p j) -> p j", p=1)).then_inc(signal, 16)

        block = ctx.enter_context(nc.Block())

        @block.gpsimd
        def _(pool):
            pool.memset(m.ident[:, :], 0.0).then_inc(S("ident0"), 1)
            pool.wait_ge(S("ident0"), 1)
            pool.affine_select(out=m.ident[:, :], in_=m.ident[:, :], compare_op=ALU.not_equal, fill=1.0, base=0,
                               pattern=[[-1, 128]], channel_multiplier=1).then_inc(S("ident"), 1)
            pool.iota(m.iota[:, :], pattern=[[1, 128]], base=0, channel_multiplier=0,
                      allow_small_or_imprecise_dtypes=True).then_inc(S("iota"), 1)
            pool.memset(m.zeros[:, :], 0.0).then_inc(S("iota"), 1)
            pool.memset(m.spread[:, :], 0.0).then_inc(S("spread0"), 1)
            pool.wait_ge(S("spread0"), 1)
            sp = m.spread[:, :].rearrange("e (f h) -> e f h", h=64)
            pool.affine_select(out=sp, in_=sp, compare_op=ALU.not_equal, fill=1.0, base=0,
                               pattern=[[-1, 32], [0, 64]], channel_multiplier=1).then_inc(S("iota"), 1)

        @block.sync
        def _(sp):
            sp.wait_ge(S("filled"), 4)
            in_rows(sp, dst_i, a["dst"], 0, S("dst_in"))
            in_rows(sp, nxt_i, a["dst"], 1, S("nxt_in"))
            in_rows(sp, src_i, a["src"], 0, S("src_in"))
            in_rows(sp, rows[:, WGT], a["edge_weight"], 0, S("wgt_in"))
            sp.wait_ge(S("bar"), 2)
            sp.dma_start(m.bars[0:1].rearrange("(p j) -> p j", p=1), bar0[0:1, 0:1]).then_inc(S("bars_out"), 16)
            for c in range(3):
                at = 1 + c * 128 * TE
                sp.dma_start(m.bars[at:at + 128 * TE].rearrange("(p j) -> p j", j=TE), bar[:, c, :]).then_inc(S("bars_out"), 16)
            at = 1 + 3 * 128 * TE
            sp.dma_start(m.bars[at:at + 8 * TE].rearrange("(p j) -> p j", j=TE), bar[0:8, 3, :]).then_inc(S("bars_out"), 16)
            sp.wait_ge(S("bars_out"), 80)

        @block.vector
        def _(dve):
            nc.vector.memset(dst_i[:, :, :], NOWHERE).then_inc(S("filled"), 1)
            nc.vector.memset(nxt_i[:, :, :], NOWHERE).then_inc(S("filled"), 1)
            nc.vector.memset(src_i[:, :, :], 0).then_inc(S("filled"), 1)
            nc.vector.memset(rows[:, WGT], 0.0).then_inc(S("filled"), 1)
            nc.vector.memset(m.lg[:, :], LOWEST).then_inc(S("filled_more"), 1)
            nc.vector.memset(m.pr[:, :], -1.0).then_inc(S("filled_more"), 1)
            nc.vector.memset(bar0[:, :], LOWEST).then_inc(S("bar"), 1)
            nc.vector.memset(m.ones[:, :], 1.0).then_inc(S("ones"), 1)
            nc.vector.memset(m.glo[:, :], 0).then_inc(S("glo0"), 1)
            nc.vector.memset(m.fr[:, :], 0).then_inc(S("glo0"), 1)
            nc.vector.memset(dl[:, :], 0.0).then_inc(S("glo0"), 1)
            dve.wait_ge(S("dst_in"), 80)
            nc.vector.tensor_copy(rows[:, DST], dst_i[:, :, :]).then_inc(S("dst_f"), 1)
            dve.wait_ge(S("nxt_in"), 80)
            nc.vector.tensor_copy(nxt_f[:, :, :], nxt_i[:, :, :]).then_inc(S("nxt_f"), 1)
            dve.wait_ge(S("src_in"), 80)
            nc.vector.tensor_copy(rows[:, SRC], src_i[:, :, :]).then_inc(S("src_f"), 1)
            dve.wait_ge(S("dst_f"), 1)
            dve.wait_ge(S("nxt_f"), 1)
            nc.vector.tensor_tensor(rows[:, LAST], rows[:, DST], nxt_f[:, :, :], ALU.not_equal).then_inc(S("last_f"), 1)
            dve.wait_ge(S("last_f"), 1)
            nc.vector.tensor_scalar(bar[:, :, :], rows[:, LAST], LOWEST, None, ALU.mult).then_inc(S("bar"), 1)
            for b in range(1, BLOCKS):
                if b > 1:
                    dve.wait_ge(S("cnt"), b - 1)
                nc.vector.tensor_scalar(below[:, :], rows[:, DST].rearrange("p c j -> p (c j)"), float(NB * b), 0.0,
                                        ALU.is_lt, ALU.add, accum_out=cnt[:, b - 1:b]).then_inc(S("cnt"), 1)
            dve.wait_ge(S("ptr"), 1)
            nc.vector.tensor_copy(ptr_i[:, :], m.bank[0][0:1, 0:24]).then_inc(S("ptr_i"), 1)
            dve.wait_ge(S("ptr_i"), 1)
            nc.vector.tensor_scalar(glo_i[:, :], ptr_i[:, :], 9, None, ALU.arith_shift_right).then_inc(S("glo_i"), 1)
            dve.wait_ge(S("glo_i"), 1)
            dve.wait_ge(S("glo0"), 3)
            nc.vector.tensor_copy(m.glo[:, 1:25], glo_i[:, :]).then_inc(S("glo"), 1)
            nc.vector.memset(m.glo[:, 25:26], GROUPS - 1).then_inc(S("glo"), 1)
            nc.vector.tensor_copy(glo_f[:, :], glo_i[:, :]).then_inc(S("glo_f"), 1)
            dve.wait_ge(S("glo_f"), 1)
            dve.wait_ge(S("iota"), 3)
            for b in range(24):
                nc.vector.scalar_tensor_tensor(dl[:, :], m.iota[0:1, 0:GROUPS], glo_f[:, b:b + 1], dl[:, :],
                                               ALU.is_ge, ALU.add).then_inc(S("dl"), 1)
                dve.wait_ge(S("dl"), b + 1)
            nc.vector.scalar_tensor_tensor(steps[:, :], m.iota[0:1, 0:GROUPS], 1.0, dl[:, :],
                                           ALU.add, ALU.add).then_inc(S("steps"), 1)
            dve.wait_ge(S("steps"), 1)
            nc.vector.memset(m.packed[:, :], 0).then_inc(S("glo"), 1)
            dve.wait_ge(S("glo"), 3)
            nc.vector.tensor_tensor(more[:, :], m.glo[:, 1:26], m.glo[:, 0:25], ALU.subtract).then_inc(S("packed"), 1)
            nc.vector.tensor_scalar(firsts[:, :], m.glo[:, 0:25], 128, 1, ALU.mult, ALU.add).then_inc(S("packed"), 1)
            dve.wait_ge(S("packed"), 2)
            nc.vector.tensor_tensor(m.packed[:, 0:25], firsts[:, :], more[:, :], ALU.add).then_inc(S("packed"), 1)
            nc.vector.tensor_copy(m.fr[:, RG:GROUPS], steps[:, 0:GROUPS - RG]).then_inc(S("fr"), 1)
            for n, out in enumerate([m.dst_c, m.src_c, m.w_c, m.last_c]):
                dve.wait_ge(S("columns"), n + 1)
                nc.vector.tensor_copy(out[:, :], m.bank[1 + n][:, 0:TILES]).then_inc(S("columns_out"), 1)

        @block.tensor
        def _(pe):
            pe.wait_ge(S("ident"), 1)
            pe.wait_ge(S("ones"), 1)
            pe.wait_ge(S("cnt"), 24)
            nc.tensor.matmul(m.bank[0][0:1, 0:24], m.ones[:, :], cnt[:, :], start=True, stop=True).then_inc(S("ptr"), 1)
            for n, (signal, count) in enumerate([("dst_f", 1), ("src_f", 1), ("wgt_in", 80), ("last_f", 1)]):
                pe.wait_ge(S(signal), count)
                for c in range(4):
                    t = nc.tensor.transpose(m.bank[1 + n][:, c * 128:(c + 1) * 128], rows[:, n, c, :], m.ident[:, :])
                t.then_inc(S("columns"), 1)
    clear(nc, S)


class Chain:

    def __init__(self, eng, signal, t, steps):
        self.eng, self.counter, self.t, self.steps, self.done = eng, signal, t, steps, 0

    def link(self, ins):
        self.done += 1
        ins.then_inc(self.counter, 1)
        self.eng.wait_ge(self.counter, self.t * self.steps + self.done)

    def end(self):
        assert self.done == self.steps, (self.done, self.steps)


def norm_dve(nc, m, S, dve, t, rows, name="norm", stored=None):
    c = Chain(dve, S(name + "_steps"), t, 4)
    dve.sem_inc(S("turn"), 1)
    c.link(nc.vector.bn_stats(m.st[:, :], rows))
    dve.sem_inc(S("turn"), 1)
    c.link(nc.vector.bn_aggr(m.mv[:, :], m.st[:, :]))
    c.link(nc.vector.tensor_scalar(m.ve[:, :], m.mv[:, 1:2], 1e-5, None, ALU.add))
    dve.wait_ge(S(name + "_sd"), t + 1)
    c.link(nc.vector.reciprocal(m.rs[:, :], m.sd[:, :]))
    c.end()
    if stored is not None:
        dve.wait_ge(S("stored"), stored)
    nc.vector.tensor_scalar(m.xn[:, :], rows, m.mv[:, 0:1], m.rs[:, :], ALU.subtract, ALU.mult)\
        .then_inc(S(name + "_xn"), 1)


def norm_act(nc, m, S, act, t, name="norm"):
    act.wait_ge(S(name + "_steps"), t * 4 + 3)
    nc.scalar.activation(m.sd[:, :], m.ve[:, :], ACT.Sqrt).then_inc(S(name + "_sd"), 1)


def turn_pe(nc, m, S, pe, t, name="norm"):
    pe.wait_ge(S(name + "_xn"), t + 1)
    nc.tensor.transpose(m.bank[3][:, 0:NB], m.xn[:, 0:128], m.ident[0:NB, 0:NB])
    nc.tensor.transpose(m.bank[3][:, NB:2 * NB], m.xn[:, 128:256], m.ident[0:NB, 0:NB]).then_inc(S(name + "_turned"), 1)


def turn_act(nc, m, S, act, t, name="norm"):
    act.wait_ge(S(name + "_turned"), t + 1)
    nc.scalar.copy(m.xt[:, :, :], m.bank[3][:, 0:2 * NB].rearrange("p (k n) -> p k n", k=2)).then_inc(S(name + "_xt"), 1)


def product(nc, out, xt, w, signal):
    k = w.shape[1]
    for j in range(k):
        last = nc.tensor.matmul(out, xt[:, j, :], w[:, j, :], start=(j == 0), stop=(j == k - 1))
    last.then_inc(signal, 1)


def first_store(act, m, S):
    act.dma_start(m.primer[0:1, 0:1], m.ident[0:1, 0:1]).then_inc(S("stored"), 16)


def store_act(nc, m, S, act, t, psum, width, table, signal, per_block=1):
    act.wait_ge(S(signal), t + 1)
    act.wait_ge(S("stored"), t * 16 * per_block + 16)
    nc.scalar.copy(m.stage[:, 0:width], psum).then_inc(S("stage"), 1)
    act.wait_ge(S("stage"), t + 2)
    act.dma_start(table[bass.ds(t * NB, NB), :], m.stage[:, 0:width]).then_inc(S("stored"), 16)


def router_steps(experts, softmax, top):
    return 1 + (5 if softmax else 0) + (9 if top == 2 else 3) + (2 if experts < 8 else 0)


def router_dve(nc, m, S, dve, t, logits, bias, experts, softmax, top):
    c = Chain(dve, S("router_steps"), t, router_steps(experts, softmax, top))
    wide = max(experts, 8)
    if experts < 8:
        c.link(nc.vector.memset(m.lg[:, experts:8], LOWEST))
        c.link(nc.vector.memset(m.pr[:, experts:8], -1.0))
    dve.wait_ge(S("logits"), t + 1)
    c.link(nc.vector.tensor_tensor(m.lg[:, 0:experts], logits, bias, ALU.add))
    pick = m.lg
    if softmax:
        dve.sem_inc(S("turn"), 1)
        c.link(nc.vector.max(m.v8[:, :], m.lg[:, 0:wide]))
        c.link(nc.vector.tensor_scalar(m.neg[:, :], m.v8[:, 0:1], -1.0, None, ALU.mult))
        dve.wait_ge(S("router_exp"), t + 1)
        c.link(nc.vector.tensor_reduce(m.sm[:, :], m.ex[:, 0:experts], AX, ALU.add))
        c.link(nc.vector.reciprocal(m.sr[:, :], m.sm[:, :]))
        c.link(nc.vector.tensor_scalar(m.pr[:, 0:experts], m.ex[:, 0:experts], m.sr[:, :], None, ALU.mult))
        pick = m.pr
    dve.sem_inc(S("turn"), 1)
    c.link(nc.vector.max(m.v8[:, :], pick[:, 0:wide]))
    dve.sem_inc(S("turn"), 1)
    c.link(nc.vector.max_index(m.i8[:, :], m.v8[:, :], pick[:, 0:wide]))
    c.link(nc.vector.tensor_copy(m.i8f[:, :], m.i8[:, :]))
    if top == 1:
        c.end()
        nc.vector.tensor_scalar(m.c[:, 0:experts], m.iota[0:NB, 0:experts], m.i8f[:, 0:1], None, ALU.is_equal)\
            .then_inc(S("weights"), 1)
        return
    c.link(nc.vector.tensor_tensor(m.d12[:, :], m.v8[:, 1:2], m.v8[:, 0:1], ALU.subtract))
    dve.wait_ge(S("router_exp2"), t + 1)
    c.link(nc.vector.tensor_scalar(m.sm2[:, :], m.e2[:, :], 1.0, None, ALU.add))
    c.link(nc.vector.reciprocal(m.w12[:, 0:1], m.sm2[:, :]))
    c.link(nc.vector.tensor_tensor(m.w12[:, 1:2], m.e2[:, :], m.w12[:, 0:1], ALU.mult))
    c.link(nc.vector.tensor_scalar(m.c1[:, 0:experts], m.iota[0:NB, 0:experts], m.i8f[:, 0:1], m.w12[:, 0:1],
                                   ALU.is_equal, ALU.mult))
    c.link(nc.vector.tensor_scalar(m.c2[:, 0:experts], m.iota[0:NB, 0:experts], m.i8f[:, 1:2], m.w12[:, 1:2],
                                   ALU.is_equal, ALU.mult))
    c.end()
    nc.vector.tensor_tensor(m.c[:, 0:experts], m.c1[:, 0:experts], m.c2[:, 0:experts], ALU.add).then_inc(S("weights"), 1)


def router_act(nc, m, S, act, t, experts, softmax, top, turn=True):
    steps = router_steps(experts, softmax, top)
    fill = 2 if experts < 8 else 0
    if softmax:
        act.wait_ge(S("router_steps"), t * steps + fill + 3)
        nc.scalar.activation(m.ex[:, 0:experts], m.lg[:, 0:experts], ACT.Exp, bias=m.neg[:, :]).then_inc(S("router_exp"), 1)
    if top == 2:
        act.wait_ge(S("router_steps"), t * steps + fill + (10 if softmax else 5))
        nc.scalar.activation(m.e2[:, :], m.d12[:, :], ACT.Exp).then_inc(S("router_exp2"), 1)


def router_turned_act(nc, m, S, act, t, experts):
    act.wait_ge(S("weights_turned"), t + 1)
    nc.scalar.copy(m.ct[0:experts, :], m.bank[3][0:experts, 256:256 + NB]).then_inc(S("ct"), 1)


def router_pe(nc, m, S, pe, t, experts):
    pe.wait_ge(S("weights"), t + 1)
    nc.tensor.transpose(m.bank[3][0:experts, 256:256 + NB], m.c[:, 0:experts], m.ident[0:NB, 0:NB])\
        .then_inc(S("weights_turned"), 1)


class Experts:

    def __init__(self, count, layers, out, out_chunks, out_units):
        self.count, self.layers, self.out, self.out_chunks, self.out_units = count, layers, out, out_chunks, out_units
        depth = len(layers)
        self.jobs, self.hidden = [], {}
        for step in range(count + depth):
            for layer in range(depth + 1):
                e = step - layer
                if 0 <= e < count:
                    self.jobs.append((e, layer))
                    if layer < depth:
                        self.hidden[e, layer] = len(self.hidden)

    def pe(self, nc, m, S, pe, t, before_outputs):
        n, depth = len(self.hidden), len(self.layers)
        for e, layer in self.jobs:
            if (e, layer) == (0, depth):
                before_outputs()
            if layer < depth:
                i = self.hidden[e, layer]
                if layer == 0:
                    source = m.xt
                else:
                    pe.wait_ge(S("hidden"), t * n + self.hidden[e, layer - 1] + 1)
                    source = m.ht[:, self.hidden[e, layer - 1] % 4]
                if i >= 4:
                    pe.wait_ge(S("hidden"), t * n + i - 3)
                k_in, c_out, units, weights, _ = self.layers[layer]
                for c in range(c_out):
                    for k in range(k_in):
                        last = nc.tensor.matmul(m.hid[i % 4][0:units, c * NB:(c + 1) * NB], weights(e, k, c),
                                                source[:, k, :], start=(k == 0), stop=(k == k_in - 1))
                last.then_inc(S("hidden_sums"), 1)
            else:
                i = self.hidden[e, depth - 1]
                pe.wait_ge(S("hidden"), t * n + i + 1)
                o = 1 + e
                if o >= 2:
                    pe.wait_ge(S("added"), t * (1 + self.count) + o - 1)
                u = self.out_units
                for k in range(self.out_chunks):
                    last = nc.tensor.matmul(m.bank[6 + o % 2][0:NB, 0:D], m.ht[0:u, i % 4, k, :], self.out(e, k),
                                            start=(k == 0), stop=(k == self.out_chunks - 1))
                last.then_inc(S("outputs"), 1)

    def act(self, nc, m, S, act, t, before_outputs):
        n = len(self.hidden)
        ahead = sum(layer < len(self.layers) for _, layer in self.jobs[:self.jobs.index((0, len(self.layers)))])
        for (e, layer), i in sorted(self.hidden.items(), key=lambda kv: kv[1]):
            if i == ahead:
                before_outputs()
            act.wait_ge(S("hidden_sums"), t * n + i + 1)
            _, c_out, units, _, bias = self.layers[layer]
            for c in range(c_out):
                last = nc.scalar.activation(m.ht[0:units, i % 4, c, :], m.hid[i % 4][0:units, c * NB:(c + 1) * NB],
                                            ACT.Relu, bias=bias(e, c))
            last.then_inc(S("hidden"), 1)

    def dve(self, nc, m, S, dve, t, rows):
        total = 1 + self.count
        for o in range(total):
            if o == total - 1:
                yield
            dve.wait_ge(S("outputs"), t * total + o + 1)
            if o == 0:
                ins = nc.vector.tensor_tensor(rows, m.bank[6][0:NB, 0:D], rows, ALU.add)
            else:
                ins = nc.vector.scalar_tensor_tensor(rows, m.bank[6 + o % 2][0:NB, 0:D], m.c[:, o - 1:o], rows,
                                                     ALU.mult, ALU.add)
            ins.then_inc(S("added"), 1)
            dve.wait_ge(S("added"), t * total + o + 1)


def edge_pass(nc, m, name, table, width, kind, pe_tile, act_tile, dve_tile, weight=None, sp_loads=None, stores=0):
    ctx = ExitStack()
    with ctx:
        S = Signals(ctx, nc, name)
        scans = kind == "max"
        halves = [(0, width)] if width <= 128 else [(0, 128), (128, 256)]
        columns = {"sum": D, "degrees": GW, "max": width, "attention": GW}[kind]
        arrived, before = m.arrived, m.arrived_count
        m.arrived_count += 16 * ROUNDS
        bars_in = [S(f"bars_{k}") for k in range(RG)] if scans else []
        onehot = S("onehot")
        block = ctx.enter_context(nc.Block())

        def bounds(eng, d):
            eng.sem_inc(S(f"turn_{eng.engine.name}"), 1)
            packed = eng.value_load(m.packed[0:1, bass.ds(d, 1)], min_val=0, max_val=GROUPS * 128 - 1)
            return packed >> 7, packed & 127

        def all_visits(eng, d, visit):
            first, count = bounds(eng, d)
            with eng.Fori(first, first + count) as g:
                visit(d, inside(g))

        def visits(eng, d, found, part, visit):
            first, count = found
            at = [first, first + ((count * 3 + 4) >> 3), first + ((count + 1) >> 1), first + ((count * 7 + 4) >> 3), first + count]
            eng.sem_inc(S(f"turn_{eng.engine.name}"), 1)
            with eng.If(at[part] < at[part + 1]):
                with eng.Fori(at[part], at[part + 1]) as g:
                    visit(d, inside(g))

        def inside(g):
            return nc.s_assert_within(g, 0, GROUPS - 1, skip_runtime_bounds_check_because="a group's number")

        def gathered(slot, p):
            return m.rows[:, bass.ds((slot * GT + 2 * p) * GW, 2 * GW)].rearrange("p (s f) -> p s f", s=2)

        def slot_of(g):
            return nc.s_assert_within(g % RG, 0, RG - 1, skip_runtime_bounds_check_because="a remainder")

        @block.gpsimd
        def _(pool):
            if kind == "degrees":
                pool.memset(m.rows[:, :].rearrange("p (t w) -> p t w", w=GW)[:, :, D:GW], 1.0).then_inc(S("ones"), 1)
            with pool.Fori(0, ROUNDS) as i:
                for k in range(RG):
                    free = pool.value_load(m.fr[0:1, bass.ds(i * RG + k, 1)], min_val=0, max_val=GROUPS + BLOCKS)
                    pool.wait_ge(S("summed"), free * GT + 4)
                    pool.sem_inc(S("turn"), 1)
                    pool.tensor_copy(m.idx[:, k * GT:(k + 1) * GT], m.src_c[:, bass.ds((i * RG + k) * GT, GT)])\
                        .then_inc(S("idx"), 1)
                    pool.wait_ge(S("idx"), i * RG + (k + 1))
                    pool.sem_inc(S("turn"), 1)
                    for s in range(GT):
                        n = k * GT + s
                        pool.indirect_dma_start(
                            out=m.rows[:, n * GW:n * GW + table.shape[1]], out_offset=None, in_=table,
                            in_offset=bass.IndirectOffsetOnAxis(ap=m.idx[:, n:n + 1], axis=0)).then_inc(arrived[n], 16)

        @block.sync
        def _(sp):
            if sp_loads:
                sp_loads(sp, S)
            with sp.Fori(0, ROUNDS) as i:
                for k in range(RG):
                    if scans:
                        free = sp.value_load(m.fr[0:1, bass.ds(i * RG + k, 1)], min_val=0, max_val=GROUPS + BLOCKS)
                        sp.wait_ge(S("summed"), free * GT + 4)
                        sp.sem_inc(S("turn_sp"), 1)
                        at = (i * RG + k) * (GT * TE)
                        sp.dma_start(m.bar[:, k * GT * TE:(k + 1) * GT * TE], m.bars[bass.ds(at, GT * TE)].partition_broadcast(128))\
                            .then_inc(bars_in[k], 16)
                        sp.wait_ge(bars_in[k], i * 16 + 16)
                        sp.sem_inc(S("turn_sp"), 1)
                    for s in range(GT):
                        sp.wait_ge(arrived[k * GT + s], i * 16 + (before + 16))
                        sp.sem_inc(S("tiles_in"), 1)
            if stores:
                sp.wait_ge(S("stored"), 16 * BLOCKS * stores + 16)
            if sp_loads:
                sp.wait_ge(S("loaded"), 16 * sp_loads.count)

        @block.vector
        def _(dve):
            nc.vector.tensor_scalar(m.dloc[:, :], m.dst_c[:, :], float(NB), None, ALU.add).then_inc(S("relative"), 1)
            if scans:
                nc.vector.memset(m.run[:, 1], 0.0).then_inc(S("run0"), 1)
                dve.wait_ge(S("run0"), 1)
            def visit(d, g):
                v = g + d

                def one_hot(s):
                    dve.wait_ge(S("summed"), v * GT + (s + 1))
                    edge = bass.ds(g * GT + s, 1)
                    if weight is None:
                        nc.vector.tensor_scalar(m.sel[:, s, :], m.iota[:, 0:NB], m.dloc[:, edge], None, ALU.is_equal)\
                            .then_inc(onehot, 1)
                    else:
                        nc.vector.tensor_scalar(m.sel[:, s, :], m.iota[:, 0:NB], m.dloc[:, edge], weight[:, edge],
                                                ALU.is_equal, ALU.mult).then_inc(onehot, 1)

                if kind in ("sum", "degrees"):
                    for s in range(GT):
                        one_hot(s)
                elif kind == "max":
                    slot = slot_of(g)
                    for p in range(2):
                        one_hot(2 * p)
                        one_hot(2 * p + 1)
                        n = v * 2 + p
                        dve.wait_ge(S("turned"), n + 3)
                        dve.wait_ge(S("scanned"), n + 2)
                        dve.wait_ge(S("back"), n + 1)
                        for h, (lo, hi) in enumerate(halves):
                            w = hi - lo
                            ins = nc.vector.tensor_tensor_scan(
                                m.run[0:w, p, h, :], m.bar[0:w, bass.ds((slot * GT + 2 * p) * TE, 2 * TE)],
                                m.bank[1 + p][0:w, h * 2 * TE:(h + 1) * 2 * TE], m.run[0:w, 1 - p, h, 2 * TE - 1:2 * TE],
                                ALU.add, ALU.max)
                        ins.then_inc(S("scanned"), 1)
                else:
                    slot = slot_of(g)

                    def logit(p):
                        n = v * 2 + p
                        at = slice(2 * p, 2 * p + 2)
                        tiles = gathered(slot, p)[:, :, D:GW]
                        dve.wait_ge(S("tiles_in"), g * GT + (2 * p + 2))
                        dve.wait_ge(S("dst_values"), n + 3)
                        own = m.bank[4 + p][:, 0:4 * HEADS].rearrange("p (s f) -> p s f", s=2)
                        nc.vector.tensor_tensor(m.e0[:, at, :], tiles, own[:, :, 0:HEADS], ALU.add).then_inc(S("logit_steps"), 1)
                        dve.wait_ge(S("logit_steps"), n * 2 + 1)
                        nc.vector.scalar_tensor_tensor(m.e1[:, at, :], m.e0[:, at, :], 0.2, m.e0[:, at, :], ALU.mult, ALU.max)\
                            .then_inc(S("logit_steps"), 1)
                        dve.wait_ge(S("logit_steps"), n * 2 + 2)
                        dve.wait_ge(S("weighted"), n + 1)
                        nc.vector.tensor_tensor(m.e3[:, at, :], m.e1[:, at, :], own[:, :, HEADS:2 * HEADS], ALU.subtract)\
                            .then_inc(S("logit"), 1)

                    def message(p):
                        dve.wait_ge(S("weighted"), v * 2 + p + 3)
                        tiles = gathered(slot, p)[:, :, 0:D].rearrange("p s (h f) -> p s h f", h=HEADS)
                        out = m.msg[:, 2 * p:2 * p + 2]
                        nc.vector.tensor_tensor(out[:, :, 0:D].rearrange("p s (h f) -> p s h f", h=HEADS), tiles,
                                                out[:, :, D:GW].unsqueeze(3).to_broadcast([128, 2, HEADS, HD]), ALU.mult)\
                            .then_inc(S("message"), 1)

                    for s in range(GT):
                        one_hot(s)
                    logit(0)
                    logit(1)
                    message(0)
                    message(1)

            def begin(d):
                dve.wait_ge(S("relative"), d + 1)
                nc.vector.tensor_scalar(m.dloc[:, :], m.dloc[:, :], -float(NB), None, ALU.add).then_inc(S("relative"), 1)
                dve.wait_ge(S("relative"), d + 2)

            begin(0)
            all_visits(dve, 0, visit)
            with dve.Fori(0, BLOCKS) as d:
                found = bounds(dve, d + 1)
                for part, _ in enumerate(dve_tile(dve, S, d)):
                    if part == 0:
                        begin(d + 1)
                    visits(dve, d + 1, found, part, visit)

        @block.scalar
        def _(act):
            if stores:
                first_store(act, m, S)
            def visit(d, g):
                v = g + d
                slot = slot_of(g) if kind == "max" else None
                for p in range(2):
                    n = v * 2 + p
                    if kind == "max":
                        act.wait_ge(S("tiles_in"), g * GT + (2 * p + 2))
                        act.wait_ge(S("turned"), n + 1)
                        nc.scalar.copy(m.gt[:, 2 * p:2 * p + 2, 0:width], gathered(slot, p)[:, :, 0:width])\
                            .then_inc(S("tiles_copied"), 1)
                    else:
                        act.wait_ge(S("sel_turned"), n + 1)
                        act.wait_ge(S("dst_values"), n + 1)
                        nc.scalar.copy(m.selt[:, 2 * p:2 * p + 2, :],
                                       m.bank[1 + p][0:NB, 0:2 * TE].rearrange("p (s f) -> p s f", s=2))\
                            .then_inc(S("selt"), 1)
                for p in range(2):
                    n = v * 2 + p
                    if kind == "max":
                        act.wait_ge(S("back"), n + 3)
                        act.wait_ge(S("summed"), n * 2 + 2)
                        nc.scalar.copy(m.runt[:, 2 * p:2 * p + 2, 0:width],
                                       m.bank[4 + p][:, 0:2 * width].rearrange("p (s f) -> p s f", s=2))\
                            .then_inc(S("copied"), 1)
                    else:
                        act.wait_ge(S("logit"), n + 3)
                        act.wait_ge(S("summed"), n * 2 + 2)
                        nc.scalar.activation(m.msg[:, 2 * p:2 * p + 2, D:GW], m.e3[:, 2 * p:2 * p + 2, :], ACT.Exp)\
                            .then_inc(S("weighted"), 1)

            serves = kind in ("max", "attention")
            if serves:
                all_visits(act, 0, visit)
            with act.Fori(0, BLOCKS) as d:
                found = bounds(act, d + 1) if serves else None
                for part, _ in enumerate(act_tile(act, S, d)):
                    if serves:
                        visits(act, d + 1, found, part, visit)

        @block.tensor
        def _(pe):
            pe.sem_inc(S("summed"), 4)
            for name in ("acc_read", "stage", "done", "y"):
                pe.sem_inc(S(name), 1)
            if kind == "max":
                pe.sem_inc(S("scanned"), 2)
                pe.sem_inc(S("turned"), 2)
                pe.sem_inc(S("back"), 2)
                pe.sem_inc(S("copied"), 2)
            if kind == "attention":
                pe.sem_inc(S("selt"), 2)
                pe.sem_inc(S("dst_values"), 2)
                pe.sem_inc(S("logit"), 2)
                pe.sem_inc(S("weighted"), 2)
            if kind == "degrees":
                pe.wait_ge(S("ones"), 1)
            def visit(d, g):
                v = g + d
                slot = slot_of(g)

                def add(s, rows):
                    pe.wait_ge(onehot, v * GT + (s + 1))
                    nc.tensor.matmul(m.acc[:, 0:columns], m.sel[:, s, :], rows, start=False, stop=False).then_inc(S("summed"), 1)

                if kind in ("sum", "degrees"):
                    for s in range(GT):
                        pe.wait_ge(S("tiles_in"), g * GT + (s + 1))
                        add(s, m.rows[:, bass.ds((slot * GT + s) * GW, columns)])
                elif kind == "max":
                    for p in range(2):
                        pe.wait_ge(S("tiles_copied"), v * 2 + p + 1)
                        pe.wait_ge(S("scanned"), v * 2 + p + 1)
                        for h, (lo, hi) in enumerate(halves):
                            for s in range(2):
                                at = (2 * h + s) * TE
                                ins = nc.tensor.transpose(m.bank[1 + p][0:hi - lo, at:at + TE],
                                                          m.gt[:, 2 * p + s, lo:hi], m.ident[:, :])
                        ins.then_inc(S("turned"), 1)
                    for p in range(2):
                        pe.wait_ge(S("scanned"), v * 2 + p + 3)
                        pe.wait_ge(S("copied"), v * 2 + p + 1)
                        pe.sem_inc(S("turn_pe"), 1)
                        for s in range(2):
                            for h, (lo, hi) in enumerate(halves):
                                ins = nc.tensor.transpose(m.bank[4 + p][:, s * width + lo:s * width + hi],
                                                          m.run[0:hi - lo, p, h, s * TE:(s + 1) * TE],
                                                          m.ident[0:hi - lo, 0:hi - lo])
                        ins.then_inc(S("back"), 1)
                    for s in range(GT):
                        pe.wait_ge(S("copied"), v * 2 + s // 2 + 3)
                        add(s, m.runt[:, s, 0:width])
                else:
                    for p in range(2):
                        pe.wait_ge(onehot, v * GT + 2 * p + 2)
                        pe.wait_ge(S("selt"), v * 2 + p + 1)
                        for s in range(2):
                            ins = nc.tensor.transpose(m.bank[1 + p][0:NB, s * TE:(s + 1) * TE], m.sel[:, 2 * p + s, :],
                                                      m.ident[:, :])
                        ins.then_inc(S("sel_turned"), 1)
                    for p in range(2):
                        pe.wait_ge(S("selt"), v * 2 + p + 3)
                        pe.wait_ge(S("logit"), v * 2 + p + 1)
                        for s in range(2):
                            ins = nc.tensor.matmul(m.bank[4 + p][:, s * 2 * HEADS:(s + 1) * 2 * HEADS], m.selt[:, 2 * p + s, :],
                                                   m.own[:, bass.ds(d * 2 * HEADS, 2 * HEADS)], start=True, stop=True)
                        ins.then_inc(S("dst_values"), 1)
                    for s in range(GT):
                        pe.wait_ge(S("message"), v * 2 + s // 2 + 1)
                        add(s, m.msg[:, s, :])

            def begin(d):
                pe.wait_ge(S("acc_read"), d + 1)
                nc.tensor.matmul(m.acc[:, 0:columns], m.zeros[:, 0:NB], m.zeros[:, 0:columns], start=True, stop=False)

            def end():
                nc.tensor.matmul(m.acc[:, 0:columns], m.zeros[:, 0:NB], m.zeros[:, 0:columns], start=False, stop=True)\
                    .then_inc(S("block_summed"), 1)

            begin(0)
            all_visits(pe, 0, visit)
            end()
            with pe.Fori(0, BLOCKS) as d:
                found = bounds(pe, d + 1)
                for part, _ in enumerate(pe_tile(pe, S, d)):
                    if part == 0:
                        begin(d + 1)
                    visits(pe, d + 1, found, part, visit)
                end()
    clear(nc, S)


def load(sp, S, count, pairs):
    for out, in_ in pairs:
        sp.dma_start(out, in_).then_inc(S("loaded"), 16)


class Loads:

    def __init__(self, pairs):
        self.pairs, self.count = pairs, len(pairs)

    def __call__(self, sp, S):
        for out, in_ in self.pairs:
            sp.dma_start(out, in_, allow_slow_non_contiguous=True).then_inc(S("loaded"), 16)


def across(ap, p=NB):
    return ap.partition_broadcast(p)


def first_block(nc, m, table, w_table, w_self, bias, loads):
    ctx = ExitStack()
    with ctx:
        S = Signals(ctx, nc, "first")
        block = ctx.enter_context(nc.Block())

        @block.sync
        def _(sp):
            loads(sp, S)
            sp.wait_ge(S("loaded"), 16 * loads.count)
            sp.sem_inc(S("weights_in"), 1)
            sp.wait_ge(S("stored"), 16 * BLOCKS + 16)

        @block.vector
        def _(dve):
            dve.wait_ge(S("weights_in"), 1)
            with dve.Fori(0, BLOCKS) as t:
                dve.wait_ge(S("done"), t + 1)
                norm_dve(nc, m, S, dve, t, m.x[:, bass.ds(t * D, D)])
                own_part_dve(nc, m, S, dve, t, bias)

        @block.scalar
        def _(act):
            first_store(act, m, S)
            with act.Fori(0, BLOCKS) as t:
                norm_act(nc, m, S, act, t)
                turn_act(nc, m, S, act, t)
                store_act(nc, m, S, act, t, m.bank[6][0:NB, 0:D], D, table, "table_rows")

        @block.tensor
        def _(pe):
            pe.sem_inc(S("stage"), 1)
            pe.sem_inc(S("done"), 1)
            pe.wait_ge(S("weights_in"), 1)
            with pe.Fori(0, BLOCKS) as t:
                turn_pe(nc, m, S, pe, t)
                table_and_own_pe(nc, m, S, pe, t, w_table, w_self)
    clear(nc, S)


def table_and_own_pe(nc, m, S, pe, t, w_table, w_self):
    pe.wait_ge(S("norm_xt"), t + 1)
    product(nc, m.bank[6][0:NB, 0:D], m.xt, w_table, S("table_rows"))
    product(nc, m.bank[7][0:NB, 0:D], m.xt, w_self, S("own_rows"))


def own_part_dve(nc, m, S, dve, t, bias):
    dve.wait_ge(S("own_rows"), t + 1)
    dve.wait_ge(S("stage"), t + 2)
    nc.vector.tensor_tensor(m.y[:, bass.ds(t * D, D)], m.bank[7][0:NB, 0:D], bias, ALU.add).then_inc(S("done"), 1)


def sage_pass(nc, m, name, table, next_table, w_table, w_self, bias, degrees, loads):
    def dve_tile(dve, S, d):
        dve.wait_ge(S("block_summed"), d + 1)
        dve.wait_ge(S("done"), d + 1)
        if degrees:
            c = Chain(dve, S("degree_steps"), d, 4)
            at = bass.ds(d, 1)
            c.link(nc.vector.tensor_scalar(m.has[:, at], m.acc[:, D:D + 1], 1.0, None, ALU.min))
            c.link(nc.vector.tensor_scalar(m.deg[:, :], m.acc[:, D:D + 1], 1.0, None, ALU.max))
            c.link(nc.vector.reciprocal(m.rdeg[:, :], m.deg[:, :]))
            c.link(nc.vector.tensor_tensor(m.inv[:, at], m.has[:, at], m.rdeg[:, :], ALU.mult))
            c.end()
        nc.vector.scalar_tensor_tensor(m.h[:, :], m.acc[:, 0:D], m.inv[:, bass.ds(d, 1)], m.y[:, bass.ds(d * D, D)],
                                       ALU.mult, ALU.add).then_inc(S("acc_read"), 1)
        yield
        yield
        yield
        own_part_dve(nc, m, S, dve, d, bias)
        yield

    def act_tile(act, S, d):
        act.wait_ge(S("acc_read"), d + 2)
        nc.scalar.activation(m.xn[:, :], m.h[:, :], ACT.Relu).then_inc(S("norm_xn"), 1)
        yield
        turn_act(nc, m, S, act, d)
        yield
        yield
        store_act(nc, m, S, act, d, m.bank[6][0:NB, 0:D], D, next_table, "table_rows")
        yield

    def pe_tile(pe, S, d):
        yield
        turn_pe(nc, m, S, pe, d)
        yield
        yield
        table_and_own_pe(nc, m, S, pe, d, w_table, w_self)
        yield

    edge_pass(nc, m, name, table, D, "degrees" if degrees else "sum", pe_tile, act_tile, dve_tile, sp_loads=loads, stores=1)


def root_row(nc, m, name, table, root_idx, w, leaky, bias, out, loads):
    ctx = ExitStack()
    with ctx:
        S = Signals(ctx, nc, name)
        row, turned = m.scratch[:, 0:D], m.scratch[:, D:D + 256].rearrange("p (k n) -> p k n", k=2)
        soft = m.scratch[:, 2 * D:3 * D]
        rows_before = m.root_count
        m.root_count += 16
        block = ctx.enter_context(nc.Block())

        @block.sync
        def _(sp):
            loads(sp, S)
            sp.dma_start(m.root_in[:, :], root_idx[0:1].partition_broadcast(128)).then_inc(S("root_in"), 16)
            sp.wait_ge(S("loaded"), 16 * loads.count)
            sp.wait_ge(S("root_in"), 16)

        @block.vector
        def _(dve):
            dve.wait_ge(S("root_in"), 16)
            nc.vector.tensor_scalar(m.root[:, :], m.root_in[:, :], N - 1, None, ALU.min).then_inc(S("root"), 1)
            dve.wait_ge(m.root_arrived, rows_before + 16)
            nc.vector.scalar_tensor_tensor(soft, row, 0.01 if leaky else 1.0, row, ALU.mult, ALU.max).then_inc(S("soft"), 1)
            dve.wait_ge(S("sums"), 1)
            if bias is None:
                nc.vector.tensor_copy(out, m.bank[6][0:NB, 0:D]).then_inc(S("out"), 1)
            else:
                nc.vector.tensor_tensor(out, m.bank[6][0:NB, 0:D], bias, ALU.add).then_inc(S("out"), 1)

        @block.gpsimd
        def _(pool):
            pool.wait_ge(S("root"), 1)
            pool.indirect_dma_start(out=row, out_offset=None, in_=table,
                                    in_offset=bass.IndirectOffsetOnAxis(ap=m.root[:, 0:1], axis=0)).then_inc(m.root_arrived, 16)
            pool.wait_ge(m.root_arrived, rows_before + 16)

        @block.scalar
        def _(act):
            act.wait_ge(S("turned"), 1)
            nc.scalar.copy(turned, m.bank[3][:, 0:256].rearrange("p (k n) -> p k n", k=2)).then_inc(S("turned_in"), 1)

        @block.tensor
        def _(pe):
            pe.wait_ge(S("soft"), 1)
            nc.tensor.transpose(m.bank[3][:, 0:128], soft[:, 0:128], m.ident[:, :])
            nc.tensor.transpose(m.bank[3][:, 128:256], soft[:, 128:256], m.ident[:, :]).then_inc(S("turned"), 1)
            pe.wait_ge(S("turned_in"), 1)
            pe.wait_ge(S("loaded"), 16 * loads.count)
            product(nc, m.bank[6][0:NB, 0:D], turned[:, :, 0:NB], w, S("sums"))
    clear(nc, S)


def loaded(eng, S, loads):
    eng.wait_ge(S("loaded"), 16 * loads.count)


def experts_pe(nc, m, S, pe, t, experts, biases):
    def before_outputs():
        router_pe(nc, m, S, pe, t, experts.count)
        pe.wait_ge(S("ct"), t + 1)
        nc.tensor.matmul(m.bank[6][0:NB, 0:D], m.ct[0:experts.count, :], biases, start=True, stop=True)\
            .then_inc(S("outputs"), 1)
    experts.pe(nc, m, S, pe, t, before_outputs)


def table_act(nc, m, S, act, t, table, rows, signal, ahead=0):
    act.wait_ge(S(signal), t + (1 + ahead))
    act.dma_start(table[bass.ds(t * NB, NB), :], rows).then_inc(S("stored"), 16)


def sage_experts_pass(nc, m, a, table, next_table, norm_table):
    take, vec = m.weights.take, m.vectors.take
    m.weights.reset()
    m.vectors.reset(keep=m.sage_vectors)
    w1 = take(8 * 2 * 512).rearrange("p (e k f) -> p e k f", e=8, k=2)
    w2 = take(8 * 4 * D).rearrange("p (e k f) -> p e k f", e=8, k=4)
    wg = vec(16).rearrange("p (k e) -> p k e", k=2)
    b1 = vec(32).rearrange("p (e c) -> p e c", e=8)
    b2 = vec(D)[0:8]
    bg, bg2, rb = vec(8)[0:NB], vec(8)[0:NB], vec(8)[0:NB]
    w_next = take(2 * D).rearrange("p (k f) -> p k f", k=2)
    loads = Loads([(wg, chunks(a["L0_ffn_Wg"])), (bg, across(a["L0_ffn_bg"])), (bg2, across(a["L0_ffn_bias"])),
                   (b2, a["L0_ffn_b2"]), (w_next, chunks(a["L1_gnn_W1"]))] +
                  [(b1[:, e], a["L0_ffn_b1"][e].rearrange("(c p) -> p c", p=128)) for e in range(8)] +
                  [(w1[:, e], chunks(a["L0_ffn_W1"][e])) for e in range(8)] +
                  [(w2[:, e], chunks(a["L0_ffn_W2"][e])) for e in range(8)])
    experts = Experts(8, [(2, 4, 128, lambda e, k, c: w1[:, e, k, c * 128:(c + 1) * 128], lambda e, c: b1[:, e, c:c + 1])],
                      lambda e, k: w2[:, e, k, :], 4, 128)

    def dve_tile(dve, S, d):
        loaded(dve, S, loads)
        rows = m.x[:, bass.ds(d * D, D)]
        dve.wait_ge(S("block_summed"), d + 1)
        dve.wait_ge(S("stage"), d + 1)
        c = Chain(dve, S("entry_steps"), d, 2)
        nc.vector.scalar_tensor_tensor(m.h[:, :], m.acc[:, 0:D], m.inv[:, bass.ds(d, 1)], m.y[:, bass.ds(d * D, D)],
                                       ALU.mult, ALU.add).then_inc(S("acc_read"), 1)
        dve.wait_ge(S("acc_read"), d + 2)
        yield
        c.link(nc.vector.tensor_tensor(rows, rows, m.h[:, :], ALU.add))
        c.link(nc.vector.tensor_tensor(rb, bg, bg2, ALU.add))
        c.end()
        norm_dve(nc, m, S, dve, d, rows, stored=d * 32 + 16)
        yield
        router_dve(nc, m, S, dve, d, m.bank[6][0:NB, 0:8], rb, 8, False, 2)
        yield from experts.dve(nc, m, S, dve, d, rows)
        norm_dve(nc, m, S, dve, d, rows, "next")
        yield

    def act_tile(act, S, d):
        yield
        norm_act(nc, m, S, act, d)
        turn_act(nc, m, S, act, d)
        yield
        router_act(nc, m, S, act, d, 8, False, 2, turn=False)
        loaded(act, S, loads)
        experts.act(nc, m, S, act, d, lambda: router_turned_act(nc, m, S, act, d, 8))
        yield
        norm_act(nc, m, S, act, d, "next")
        turn_act(nc, m, S, act, d, "next")
        yield
        table_act(nc, m, S, act, d, norm_table, m.xn[:, :], "next_xn")
        store_act(nc, m, S, act, d, m.bank[6][0:NB, 0:D], D, next_table, "table_rows", per_block=2)

    def pe_tile(pe, S, d):
        loaded(pe, S, loads)
        yield
        turn_pe(nc, m, S, pe, d)
        yield
        pe.wait_ge(S("norm_xt"), d + 1)
        product(nc, m.bank[6][0:NB, 0:8], m.xt, wg, S("logits"))
        experts_pe(nc, m, S, pe, d, experts, b2)
        yield
        turn_pe(nc, m, S, pe, d, "next")
        yield
        pe.wait_ge(S("next_xt"), d + 1)
        product(nc, m.bank[6][0:NB, 0:D], m.xt, w_next, S("table_rows"))

    edge_pass(nc, m, "sage2", table, D, "sum", pe_tile, act_tile, dve_tile, sp_loads=loads, stores=2)


def conv_pass(nc, m, a, table, next_table, conv_table):
    take, vec = m.weights.take, m.vectors.take
    m.weights.reset()
    m.vectors.reset(keep=m.root_vectors)
    w2 = take(2 * D).rearrange("p (k f) -> p k f", k=2)
    b1 = vec(D)[0:NB]
    loads = Loads([(w2, chunks(a["L1_gnn_W2"][0:D])), (b1, across(a["L1_gnn_b1"]))])

    def dve_tile(dve, S, d):
        loaded(dve, S, loads)
        dve.wait_ge(S("block_summed"), d + 1)
        dve.wait_ge(S("stored"), d * 32 + 16)
        nc.vector.tensor_tensor(m.h[:, :], m.acc[:, 0:D], b1, ALU.add).then_inc(S("acc_read"), 1)
        dve.wait_ge(S("acc_read"), d + 2)
        nc.vector.scalar_tensor_tensor(m.xn[:, :], m.h[:, :], 0.01, m.h[:, :], ALU.mult, ALU.max).then_inc(S("norm_xn"), 1)
        yield
        yield
        yield
        dve.wait_ge(S("table_sums"), d + 1)
        nc.vector.tensor_tensor(m.stage[:, 0:D], m.bank[6][0:NB, 0:D], m.root_out[0:NB], ALU.add).then_inc(S("table_rows"), 1)
        yield

    def act_tile(act, S, d):
        table_act(nc, m, S, act, d, conv_table, m.h[:, :], "acc_read", ahead=1)
        turn_act(nc, m, S, act, d)
        table_act(nc, m, S, act, d, next_table, m.stage[:, 0:D], "table_rows")
        yield

    def pe_tile(pe, S, d):
        loaded(pe, S, loads)
        yield
        turn_pe(nc, m, S, pe, d)
        yield
        yield
        pe.wait_ge(S("norm_xt"), d + 1)
        product(nc, m.bank[6][0:NB, 0:D], m.xt, w2, S("table_sums"))
        yield

    edge_pass(nc, m, "conv1", table, D, "sum", pe_tile, act_tile, dve_tile, weight=m.w_c, sp_loads=loads, stores=2)


def conv_experts_pass(nc, m, a, table, next_table, logit_table):
    take, vec = m.weights.take, m.vectors.take
    m.weights.reset()
    m.vectors.reset(keep=m.root_vectors)
    square = lambda: take(6 * 2 * D).rearrange("p (e k f) -> p e k f", e=6, k=2)
    wl = take(2 * D).rearrange("p (k f) -> p k f", k=2)
    e1, e2, e3 = square(), square(), square()
    r1 = take(2 * 128).rearrange("p (k f) -> p k f", k=2)
    w_next = take(2 * D).rearrange("p (k f) -> p k f", k=2)
    r2, rb1, rb2 = vec(6), vec(1), vec(6)[0:NB]
    conv_b = vec(D)[0:NB]
    bias1 = vec(12).rearrange("p (e c) -> p e c", e=6)
    bias2 = vec(12).rearrange("p (e c) -> p e c", e=6)
    bias3 = vec(D)[0:6]
    att_s, att_d = vec(D)[0:NB], vec(D)[0:NB]
    loads = Loads([(wl, chunks(a["L1_gnn_Wl"][0:D])), (r1, chunks(a["L1_ffn_router_w1"])), (w_next, chunks(a["L2_gnn_W"])),
                   (r2, a["L1_ffn_router_w2"]), (rb1, a["L1_ffn_router_b1"].rearrange("(p c) -> p c", c=1)),
                   (rb2, across(a["L1_ffn_router_b2"])), (conv_b, across(a["L1_gnn_b2"])), (bias3, a["L1_ffn_expert_b3"]),
                   (att_s, across(a["L2_gnn_att_src"].rearrange("a h f -> (a h f)"))),
                   (att_d, across(a["L2_gnn_att_dst"].rearrange("a h f -> (a h f)")))] +
                  [(b[:, e], a[n][e].rearrange("(c p) -> p c", p=128)) for e in range(6)
                   for b, n in ((bias1, "L1_ffn_expert_b1"), (bias2, "L1_ffn_expert_b2"))] +
                  [(w[:, e], chunks(a[n][e])) for e in range(6)
                   for w, n in ((e1, "L1_ffn_expert_w1"), (e2, "L1_ffn_expert_w2"), (e3, "L1_ffn_expert_w3"))])
    layer = lambda w, b: (2, 2, 128, lambda e, k, c: w[:, e, k, c * 128:(c + 1) * 128], lambda e, c: b[:, e, c:c + 1])
    experts = Experts(6, [layer(e1, bias1), layer(e2, bias2)], lambda e, k: e3[:, e, k, :], 2, 128)
    heads = lambda ap: ap.rearrange("p (h f) -> p h f", h=HEADS)

    def dve_tile(dve, S, d):
        loaded(dve, S, loads)
        rows = m.x[:, bass.ds(d * D, D)]
        dve.wait_ge(S("block_summed"), d + 1)
        dve.wait_ge(S("stored"), d * 32 + 16)
        nc.vector.tensor_tensor(m.h[:, :], m.acc[:, 0:D], conv_b, ALU.add).then_inc(S("acc_read"), 1)
        dve.wait_ge(S("acc_read"), d + 2)
        nc.vector.scalar_tensor_tensor(m.xn[:, :], m.h[:, :], 0.01, m.h[:, :], ALU.mult, ALU.max).then_inc(S("conv_xn"), 1)
        yield
        c = Chain(dve, S("entry_steps"), d, 3)
        dve.wait_ge(S("conv_rows"), d + 1)
        c.link(nc.vector.tensor_tensor(m.h[:, :], m.bank[6][0:NB, 0:D], m.root_out[0:NB], ALU.add))
        c.link(nc.vector.scalar_tensor_tensor(m.h2[:, :], m.h[:, :], 0.01, m.h[:, :], ALU.mult, ALU.max))
        c.link(nc.vector.tensor_tensor(rows, rows, m.h2[:, :], ALU.add))
        c.end()
        norm_dve(nc, m, S, dve, d, rows)
        yield
        router_dve(nc, m, S, dve, d, m.bank[6][0:NB, 0:6], rb2, 6, True, 2)
        yield from experts.dve(nc, m, S, dve, d, rows)
        norm_dve(nc, m, S, dve, d, rows, "next")
        yield
        dve.wait_ge(S("stage"), d + 2)
        q = Chain(dve, S("logit_parts"), d, 4)
        own = m.bank[6][0:NB, 0:D]
        q.link(nc.vector.tensor_tensor(m.h[:, :], own, att_s, ALU.mult))
        q.link(nc.vector.tensor_reduce(m.as_[:, bass.ds(d * HEADS, HEADS)], heads(m.h[:, :]), AX, ALU.add))
        q.link(nc.vector.tensor_tensor(m.h2[:, :], own, att_d, ALU.mult))
        q.link(nc.vector.tensor_reduce(m.own[0:NB, bass.ds(d * 2 * HEADS, HEADS)], heads(m.h2[:, :]), AX, ALU.add))
        q.end()
        dve.sem_inc(S("turn"), 1)
        nc.vector.tensor_copy(m.stage[:, D:GW], m.as_[:, bass.ds(d * HEADS, HEADS)]).then_inc(S("stage_logits"), 1)
        nc.vector.tensor_copy(m.y[:, bass.ds(d * D, D)], own).then_inc(S("own_rows"), 1)

    def act_tile(act, S, d):
        yield
        turn_act(nc, m, S, act, d, "conv")
        norm_act(nc, m, S, act, d)
        yield
        turn_act(nc, m, S, act, d)
        loaded(act, S, loads)
        act.wait_ge(S("router_hidden"), d + 1)
        nc.scalar.activation(m.rt[:, :], m.bank[7][:, 0:NB], ACT.Relu, bias=rb1).then_inc(S("rt"), 1)
        router_act(nc, m, S, act, d, 6, True, 2, turn=False)
        experts.act(nc, m, S, act, d, lambda: router_turned_act(nc, m, S, act, d, 6))
        yield
        norm_act(nc, m, S, act, d, "next")
        turn_act(nc, m, S, act, d, "next")
        yield
        act.wait_ge(S("table_rows"), d + 1)
        nc.scalar.copy(m.stage[:, 0:D], m.bank[6][0:NB, 0:D]).then_inc(S("stage"), 1)
        act.wait_ge(S("stage"), d + 2)
        table_act(nc, m, S, act, d, next_table, m.stage[:, :], "own_rows")
        table_act(nc, m, S, act, d, logit_table, m.stage[:, D:GW], "own_rows")

    def pe_tile(pe, S, d):
        loaded(pe, S, loads)
        turn_pe(nc, m, S, pe, d, "conv")
        yield
        pe.wait_ge(S("conv_xt"), d + 1)
        product(nc, m.bank[6][0:NB, 0:D], m.xt, wl, S("conv_rows"))
        yield
        turn_pe(nc, m, S, pe, d)
        pe.wait_ge(S("norm_xt"), d + 1)
        for k in range(2):
            last = nc.tensor.matmul(m.bank[7][:, 0:NB], r1[:, k, :], m.xt[:, k, :], start=(k == 0), stop=(k == 1))
        last.then_inc(S("router_hidden"), 1)
        pe.wait_ge(S("rt"), d + 1)
        nc.tensor.matmul(m.bank[6][0:NB, 0:6], m.rt[:, :], r2, start=True, stop=True).then_inc(S("logits"), 1)
        experts_pe(nc, m, S, pe, d, experts, bias3)
        yield
        turn_pe(nc, m, S, pe, d, "next")
        yield
        pe.wait_ge(S("next_xt"), d + 1)
        product(nc, m.bank[6][0:NB, 0:D], m.xt, w_next, S("table_rows"))

    edge_pass(nc, m, "conv2", table, D, "sum", pe_tile, act_tile, dve_tile, weight=m.w_c, sp_loads=loads, stores=2)


def peak_pass(nc, m, logit_table):
    def dve_tile(dve, S, d):
        at = bass.ds(d, 1)
        as_, ad = m.as_[:, bass.ds(d * HEADS, HEADS)], m.own[0:NB, bass.ds(d * 2 * HEADS, HEADS)]
        dve.wait_ge(S("block_summed"), d + 1)
        nc.vector.tensor_tensor(m.p0[:, :], m.acc[:, 0:HEADS], ad, ALU.add).then_inc(S("acc_read"), 1)
        yield
        dve.wait_ge(S("acc_read"), d + 2)
        c = Chain(dve, S("peak_steps"), d, 6)
        c.link(nc.vector.scalar_tensor_tensor(m.p1[:, :], m.p0[:, :], 0.2, m.p0[:, :], ALU.mult, ALU.max))
        c.link(nc.vector.tensor_scalar(m.none[:, :], m.has[:, at], -1.0, -LOWEST, ALU.add, ALU.mult))
        c.link(nc.vector.tensor_scalar(m.p2[:, :], m.p1[:, :], m.has[:, at], m.none[:, :], ALU.mult, ALU.add))
        c.link(nc.vector.tensor_tensor(m.p0[:, :], as_, ad, ALU.add))
        c.link(nc.vector.scalar_tensor_tensor(m.p1[:, :], m.p0[:, :], 0.2, m.p0[:, :], ALU.mult, ALU.max))
        largest = m.own[0:NB, bass.ds(d * 2 * HEADS + HEADS, HEADS)]
        c.link(nc.vector.tensor_tensor(largest, m.p1[:, :], m.p2[:, :], ALU.max))
        c.end()
        nc.vector.tensor_tensor(m.as_[:, bass.ds(d * HEADS, HEADS)], m.p1[:, :], largest, ALU.subtract)\
            .then_inc(S("own_logit"), 1)
        dve.wait_ge(S("own_logit"), d + 1)
        for _ in range(PARTS - 1):
            yield

    def nothing(eng, S, d):
        for _ in range(PARTS):
            yield
    edge_pass(nc, m, "peak", logit_table, HEADS, "max", nothing, nothing, dve_tile, weight=m.last_c)


def attention_experts_pass(nc, m, a, table, next_table):
    take, vec = m.weights.take, m.vectors.take
    m.weights.reset()
    m.vectors.reset()
    w1 = take(2 * 2048).rearrange("p (k f) -> p k f", k=2)
    w2 = take(16 * D).rearrange("p (q f) -> p q f", q=16)
    wr = take(64).rearrange("p (k f) -> p k f", k=2)
    theta, phi, diff = (take(2 * D).rearrange("p (k f) -> p k f", k=2) for _ in range(3))
    gat_b, tb, pb = vec(D)[0:NB], vec(D)[0:NB], vec(D)[0:NB]
    rb = vec(32)[0:NB]
    b1 = vec(16)
    b2 = vec(D)[0:32]
    loads = Loads([(wr, chunks(a["L2_ffn_router_w"])), (theta, chunks(a["L3_gnn_theta_w"])), (phi, chunks(a["L3_gnn_phi_w"])),
                   (gat_b, across(a["L2_gnn_bias"])), (tb, across(a["L3_gnn_theta_b"])), (pb, across(a["L3_gnn_phi_b"])),
                   (rb, across(a["L2_ffn_router_b"])), (b2, a["L2_ffn_b2"]),
                   (b1, a["L2_ffn_b1"].rearrange("(q e) h -> (e h) q", e=2)),
                   (w2, a["L2_ffn_W2"].rearrange("(q e) h f -> (e h) q f", e=2))] +
                  [(w1[:, k, :].rearrange("p (e h) -> p e h", h=64), a["L2_ffn_W1"][:, k * 128:(k + 1) * 128, :].rearrange("e p h -> p e h"))
                   for k in range(2)])
    heads = lambda ap: ap.rearrange("p (h f) -> p h f", h=HEADS)
    wide = lambda ap: ap.unsqueeze(2).to_broadcast([NB, HEADS, HD])
    mask_bank = [m.bank[7], m.bank[3]]

    def dve_tile(dve, S, d):
        loaded(dve, S, loads)
        rows, y = m.x[:, bass.ds(d * D, D)], m.y[:, bass.ds(d * D, D)]
        dve.wait_ge(S("block_summed"), d + 1)
        dve.wait_ge(S("stage"), d + 1)
        dve.wait_ge(S("own_weight"), d + 1)
        c = Chain(dve, S("entry_steps"), d, 9)
        c.link(nc.vector.tensor_tensor(diff, phi, theta, ALU.subtract))
        c.link(nc.vector.tensor_tensor(m.h[:, :], tb, pb, ALU.add))
        c.link(nc.vector.tensor_tensor(heads(m.h2[:, :]), heads(y), wide(m.p1[:, :]), ALU.mult))
        c.link(nc.vector.tensor_tensor(m.p2[:, :], m.acc[:, D:GW], m.p1[:, :], ALU.add))
        c.link(nc.vector.reciprocal(m.p0[:, :], m.p2[:, :]))
        c.link(nc.vector.tensor_tensor(m.h2[:, :], m.acc[:, 0:D], m.h2[:, :], ALU.add))
        c.link(nc.vector.tensor_tensor(heads(m.xn[:, :]), heads(m.h2[:, :]), wide(m.p0[:, :]), ALU.mult))
        c.link(nc.vector.tensor_tensor(m.h2[:, :], m.xn[:, :], gat_b, ALU.add))
        c.link(nc.vector.tensor_tensor(rows, rows, m.h2[:, :], ALU.add))
        c.end()
        dve.sem_inc(S("acc_read"), 1)
        yield
        norm_dve(nc, m, S, dve, d, rows)
        yield
        router_dve(nc, m, S, dve, d, m.bank[6][0:NB, 0:32], rb, 32, False, 1)
        for b in range(4):
            dve.wait_ge(S("masks"), d * 4 + b + 1)
            dve.wait_ge(S("hidden"), d * 4 + b + 1)
            ht = m.ht[:, b].rearrange("p c n -> p (c n)")
            nc.vector.tensor_tensor(ht, ht, mask_bank[b % 2][:, 0:4 * NB], ALU.mult).then_inc(S("masked"), 1)
        yield
        dve.wait_ge(S("outputs"), d + 1)
        nc.vector.scalar_tensor_tensor(rows, m.bank[6][0:NB, 0:D], 0.0, rows, ALU.max, ALU.add).then_inc(S("added"), 1)
        dve.wait_ge(S("added"), d + 1)
        norm_dve(nc, m, S, dve, d, rows, "next")
        yield
        dve.wait_ge(S("own_rows"), d + 1)
        nc.vector.tensor_tensor(y, m.bank[7][0:NB, 0:D], m.h[:, :], ALU.add).then_inc(S("y"), 1)

    def act_tile(act, S, d):
        act.wait_ge(S("y"), d + 1)
        nc.scalar.activation(m.p1[:, :], m.as_[:, bass.ds(d * HEADS, HEADS)], ACT.Exp).then_inc(S("own_weight"), 1)
        yield
        norm_act(nc, m, S, act, d)
        turn_act(nc, m, S, act, d)
        yield
        loaded(act, S, loads)
        for b in range(4):
            if b == 3:
                act.wait_ge(S("weights_turned"), d + 1)
                nc.scalar.copy(m.ct[0:32, :], m.bank[3][0:32, 256:256 + NB]).then_inc(S("ct"), 1)
                nc.scalar.copy(m.ctb[:, :], m.bank[3][0:32, 256:256 + NB]).then_inc(S("ct"), 1)
            act.wait_ge(S("hidden_sums"), d * 4 + b + 1)
            for c in range(4):
                last = nc.scalar.activation(m.ht[:, b, c, :], m.hid[b][:, c * NB:(c + 1) * NB], ACT.Relu,
                                            bias=b1[:, 4 * b + c:4 * b + c + 1])
            last.then_inc(S("hidden"), 1)
        yield
        norm_act(nc, m, S, act, d, "next")
        turn_act(nc, m, S, act, d, "next")
        yield
        store_act(nc, m, S, act, d, m.bank[6][0:NB, 0:D], D, next_table, "table_rows")

    def pe_tile(pe, S, d):
        loaded(pe, S, loads)
        yield
        turn_pe(nc, m, S, pe, d)
        yield
        pe.wait_ge(S("norm_xt"), d + 1)
        product(nc, m.bank[6][0:NB, 0:32], m.xt, wr, S("logits"))
        for b in range(4):
            for c in range(4):
                q = 4 * b + c
                for k in range(2):
                    last = nc.tensor.matmul(m.hid[b][:, c * NB:(c + 1) * NB], w1[:, k, q * 128:(q + 1) * 128],
                                            m.xt[:, k, :], start=(k == 0), stop=(k == 1))
            last.then_inc(S("hidden_sums"), 1)
        router_pe(nc, m, S, pe, d, 32)
        pe.wait_ge(S("ct"), 2 * d + 2)

        def masks(b):
            if b >= 2:
                pe.wait_ge(S("masked"), d * 4 + b - 1)
            for c in range(4):
                q = 4 * b + c
                last = nc.tensor.matmul(mask_bank[b % 2][:, c * NB:(c + 1) * NB], m.spread[:, q * 128:(q + 1) * 128],
                                        m.ctb[:, :], start=True, stop=True)
            last.then_inc(S("masks"), 1)

        masks(0)
        masks(1)
        nc.tensor.matmul(m.bank[6][0:NB, 0:D], m.ct[0:32, :], b2, start=True, stop=False)
        for b in range(4):
            pe.wait_ge(S("masked"), d * 4 + b + 1)
            if b + 2 < 4:
                masks(b + 2)
            for c in range(4):
                last = nc.tensor.matmul(m.bank[6][0:NB, 0:D], m.ht[:, b, c, :], w2[:, 4 * b + c, :],
                                        start=False, stop=(4 * b + c == 15))
        last.then_inc(S("outputs"), 1)
        yield
        turn_pe(nc, m, S, pe, d, "next")
        yield
        pe.wait_ge(S("next_xt"), d + 1)
        product(nc, m.bank[6][0:NB, 0:D], m.xt, diff, S("table_rows"))
        product(nc, m.bank[7][0:NB, 0:D], m.xt, theta, S("own_rows"))

    edge_pass(nc, m, "attend", table, GW, "attention", pe_tile, act_tile, dve_tile, sp_loads=loads, stores=1)


def edge_conv_experts_pass(nc, m, a, table, out):
    take, vec = m.weights.take, m.vectors.take
    m.weights.reset()
    m.vectors.reset()
    s1 = take(2 * D).rearrange("p (k f) -> p k f", k=2)
    s2 = take(2 * 128).rearrange("p (k f) -> p k f", k=2)
    s3 = take(D)
    e1 = take(4 * 2 * 128).rearrange("p (e k f) -> p e k f", e=4, k=2)
    e2 = take(4 * 64).rearrange("p (e f) -> p e f", e=4)
    e3 = take(4 * D)[0:64].rearrange("p (e f) -> p e f", e=4)
    wg = vec(8).rearrange("p (k e) -> p k e", k=2)
    sb1, sb2 = vec(2), vec(1)
    sb3 = vec(D)[0:NB]
    eb1, eb2 = vec(4), vec(4)[0:64]
    eb3 = vec(D)[0:4]
    gb = vec(4)[0:NB]
    column = lambda v: v.rearrange("(c p) -> p c", p=128)
    loads = Loads([(s1, chunks(a["L3_ffn_sW1"])), (s2, chunks(a["L3_ffn_sW2"])), (s3, a["L3_ffn_sW3"]),
                   (wg, chunks(a["L3_ffn_gW"])), (sb1, column(a["L3_ffn_sb1"])), (sb2, column(a["L3_ffn_sb2"])),
                   (sb3, across(a["L3_ffn_sb3"])), (eb1, a["L3_ffn_eb1"].rearrange("e p -> p e")),
                   (eb2, a["L3_ffn_eb2"].rearrange("e p -> p e")), (eb3, a["L3_ffn_eb3"]), (gb, across(a["L3_ffn_gb"])),
                   (e2, a["L3_ffn_eW2"].rearrange("e p f -> p e f")), (e3, a["L3_ffn_eW3"].rearrange("e p f -> p e f"))] +
                  [(e1[:, e], chunks(a["L3_ffn_eW1"][e])) for e in range(4)])
    experts = Experts(4, [(2, 1, 128, lambda e, k, c: e1[:, e, k, :], lambda e, c: eb1[:, e:e + 1]),
                          (1, 1, 64, lambda e, k, c: e2[:, e, :], lambda e, c: eb2[:, e:e + 1])],
                      lambda e, k: e3[:, e, :], 1, 64)
    shared = m.shared

    def dve_tile(dve, S, d):
        loaded(dve, S, loads)
        rows = m.x[:, bass.ds(d * D, D)]
        dve.wait_ge(S("block_summed"), d + 1)
        nc.vector.tensor_tensor(m.h[:, :], m.acc[:, 0:D], m.y[:, bass.ds(d * D, D)], ALU.add).then_inc(S("acc_read"), 1)
        dve.wait_ge(S("acc_read"), d + 2)
        yield
        c = Chain(dve, S("entry_steps"), d, 2)
        c.link(nc.vector.tensor_scalar(m.h2[:, :], m.h[:, :], 0.0, m.has[:, bass.ds(d, 1)], ALU.max, ALU.mult))
        c.link(nc.vector.tensor_tensor(rows, rows, m.h2[:, :], ALU.add))
        c.end()
        norm_dve(nc, m, S, dve, d, rows)
        yield
        router_dve(nc, m, S, dve, d, m.bank[6][0:NB, 0:4], gb, 4, True, 2)
        yield from experts.dve(nc, m, S, dve, d, rows)
        nc.vector.tensor_tensor(rows, rows, sb3, ALU.add).then_inc(S("rows"), 1)
        yield

    def act_tile(act, S, d):
        yield
        norm_act(nc, m, S, act, d)
        turn_act(nc, m, S, act, d)
        yield
        loaded(act, S, loads)
        act.wait_ge(S("shared_sums"), 2 * d + 1)
        for c in range(2):
            last = nc.scalar.activation(shared[:, c, :], m.bank[7][:, c * NB:(c + 1) * NB], ACT.Relu, bias=sb1[:, c:c + 1])
        last.then_inc(S("shared"), 1)
        act.wait_ge(S("shared_sums"), 2 * d + 2)
        nc.scalar.activation(shared[:, 2, :], m.bank[7][:, 256:256 + NB], ACT.Relu, bias=sb2).then_inc(S("shared"), 1)
        router_act(nc, m, S, act, d, 4, True, 2, turn=False)
        experts.act(nc, m, S, act, d, lambda: router_turned_act(nc, m, S, act, d, 4))
        yield
        yield
        act.wait_ge(S("rows"), d + 1)
        act.dma_start(out[bass.ds(d * NB, NB), :], m.x[:, bass.ds(d * D, D)]).then_inc(S("stored"), 16)

    def pe_tile(pe, S, d):
        loaded(pe, S, loads)
        yield
        turn_pe(nc, m, S, pe, d)
        yield
        pe.wait_ge(S("norm_xt"), d + 1)
        product(nc, m.bank[6][0:NB, 0:4], m.xt, wg, S("logits"))
        for c in range(2):
            for k in range(2):
                last = nc.tensor.matmul(m.bank[7][:, c * NB:(c + 1) * NB], s1[:, k, c * 128:(c + 1) * 128], m.xt[:, k, :],
                                        start=(k == 0), stop=(k == 1))
        last.then_inc(S("shared_sums"), 1)
        pe.wait_ge(S("shared"), 2 * d + 1)
        for k in range(2):
            last = nc.tensor.matmul(m.bank[7][:, 256:256 + NB], s2[:, k, :], shared[:, k, :], start=(k == 0), stop=(k == 1))
        last.then_inc(S("shared_sums"), 1)

        def before_outputs():
            router_pe(nc, m, S, pe, d, 4)
            pe.wait_ge(S("ct"), d + 1)
            nc.tensor.matmul(m.bank[6][0:NB, 0:D], m.ct[0:4, :], eb3, start=True, stop=False)
            pe.wait_ge(S("shared"), 2 * d + 2)
            nc.tensor.matmul(m.bank[6][0:NB, 0:D], shared[:, 2, :], s3, start=False, stop=True).then_inc(S("outputs"), 1)
        experts.pe(nc, m, S, pe, d, before_outputs)
        yield
        yield

    edge_pass(nc, m, "peaks", table, D, "max", pe_tile, act_tile, dve_tile, weight=m.last_c, sp_loads=loads, stores=1)


class Arena:

    def __init__(self, tensor, size):
        self.tensor, self.size, self.used = tensor, size, 0

    def reset(self, keep=0):
        self.used = keep

    def take(self, columns):
        at, self.used = self.used, self.used + columns
        assert self.used <= self.size, (self.used, self.size)
        return self.tensor[:, at:at + columns]


def build(nc, a, out, stop=99):
    m = Memory()
    ctx = ExitStack()
    with ctx:
        def sb(name, shape, dt=F32):
            return ctx.enter_context(nc.sbuf_tensor(name, shape, dt))

        def small(names, widths):
            return [sb(n, [NB, w]) for n, w in zip(names.split(), widths)]

        m.arrived = [ctx.enter_context(nc.semaphore(f"rows_arrived_{k}")) for k in range(RT)]
        m.root_arrived = ctx.enter_context(nc.semaphore("root_arrived"))
        m.arrived_count = m.root_count = 0
        m.x = sb("x", [NB, BLOCKS * D])
        m.y = sb("y", [NB, BLOCKS * D])
        m.rows = sb("rows", [128, RT * GW])
        m.sel = sb("sel", [128, GT, NB])
        m.dst_c, m.w_c, m.last_c, m.dloc = (sb(n, [128, TILES]) for n in ("dst_c", "w_c", "last_c", "dloc"))
        m.src_c = sb("src_c", [128, TILES], I32)
        m.idx = sb("idx", [128, RT], I32)
        m.ident = sb("ident", [128, 128])
        m.iota = sb("iota", [128, 128])
        m.ones = sb("ones", [128, 1])
        m.zeros = sb("zeros", [1, 512], BF16)
        m.spread = sb("spread", [32, 2048], BF16)
        m.glo = sb("glo", [1, 26], I32)
        m.packed = sb("packed", [1, BLOCKS + 1], I32)
        m.fr = sb("fr", [1, GROUPS], I32)
        m.xn, m.h, m.h2 = small("xn h h2", [D, D, D])
        m.stage = sb("stage", [NB, GW])
        m.xt = sb("xt", [128, 2, NB])
        m.ht = sb("ht", [128, 4, 4, NB])
        m.rt = sb("rt", [128, NB])
        m.shared = sb("shared", [128, 3, NB])
        m.st, m.mv, m.ve, m.sd, m.rs = small("st mv ve sd rs", [6, 2, 1, 1, 1])
        m.has, m.inv, m.deg, m.rdeg, m.none = small("has inv deg rdeg none", [BLOCKS, BLOCKS, 1, 1, 1])
        m.p0, m.p1, m.p2, m.as_ = small("p0 p1 p2 as_", [HEADS, HEADS, HEADS, BLOCKS * HEADS])
        m.lg, m.ex, m.pr, m.v8, m.i8f, m.neg = small("lg ex pr v8 i8f neg", [32, 8, 8, 8, 8, 1])
        m.sm, m.sr, m.d12, m.e2, m.sm2, m.w12 = small("sm sr d12 e2 sm2 w12", [1, 1, 1, 1, 1, 2])
        m.c1, m.c2, m.c = small("c1 c2 c", [8, 8, 32])
        m.i8 = sb("i8", [NB, 8], U32)
        m.own = sb("own", [NB, (BLOCKS + 1) * 2 * HEADS])
        m.ct = sb("ct", [32, NB])
        m.ctb = sb("ctb", [32, NB], BF16)
        m.root_in = sb("root_in", [128, 1], I32)
        m.root = sb("root", [128, 1], I32)
        m.scratch = sb("scratch", [128, RT * TE // 2 + 3 * GT * D])
        at = RT * TE // 2
        m.bar = m.scratch[:, 0:at].bitcast(BF16)
        cut = lambda n, w: m.scratch[:, at + n * GT * D:at + n * GT * D + GT * w].rearrange("p (s f) -> p s f", s=GT)
        m.gt, m.runt = cut(0, D), cut(1, D)
        m.run = m.scratch[:, at + 2 * GT * D:at + 3 * GT * D].rearrange("p (s h e) -> p s h e", s=2, h=2)
        m.msg = m.scratch[:, 0:GT * GW].rearrange("p (s f) -> p s f", s=GT)
        m.selt = m.scratch[0:NB, 1100:1100 + GT * TE].rearrange("p (s f) -> p s f", s=GT)
        m.e0, m.e1, m.e3 = (m.scratch[:, 1700 + 16 * n:1716 + 16 * n].rearrange("p (s f) -> p s f", s=GT) for n in range(3))
        m.weights_t = sb("weights_t", [128, 8 * 2 * 512 + 8 * 4 * D + 2 * D])
        m.weights = Arena(m.weights_t, 8 * 2 * 512 + 8 * 4 * D + 2 * D)
        m.vectors_t = sb("vectors_t", [128, 1400])
        m.vectors = Arena(m.vectors_t, 1400)
        m.root_vectors = D
        m.root_out = m.vectors_t[:, 0:D]
        m.sage_vectors = 0
        m.bank = [ctx.enter_context(nc.psum_tensor(f"bank{i}", [128, 512], F32)) for i in range(8)]
        m.acc = m.bank[0][0:NB, :]
        m.hid = [m.bank[4], m.bank[5], m.bank[1], m.bank[2]]
        m.bars = nc.dram_tensor("bars", (1 + TILES * TE,), BF16).ap()
        dram = lambda name, width: nc.dram_tensor(name, (N, width), F32).ap()
        tables = [dram(f"table_{i}", D) for i in range(6)]
        norm_table, conv_table, attention_table, logit_table = (
            dram("norm_table", D), dram("conv_table", D), dram("attention_table", GW), dram("logit_table", HEADS))

        m.primer = dram("primer", 1)

        edge_tables(nc, m, a, None)
        m.weights.reset()
        m.vectors.reset()
        sage_w = m.weights.take(6 * 2 * D).rearrange("p (i k f) -> p i k f", i=6, k=2)
        sage_b = m.vectors.take(3 * D)[0:NB].rearrange("p (i f) -> p i f", i=3)
        loads = Loads([(m.x[:, :].rearrange("p (t f) -> p t f", f=D), a["x"].rearrange("(t p) f -> p t f", p=NB))] +
                      [(sage_w[:, i], chunks(a["L0_gnn_W_neigh"][i])) for i in range(3)] +
                      [(sage_w[:, 3 + i], chunks(a["L0_gnn_W_self"][i])) for i in range(3)] +
                      [(sage_b[:, i], across(a["L0_gnn_bias"][i])) for i in range(3)])
        first_block(nc, m, tables[0], sage_w[:, 0], sage_w[:, 3], sage_b[:, 0], loads)
        sage_pass(nc, m, "sage0", tables[0], tables[1], sage_w[:, 1], sage_w[:, 4], sage_b[:, 1], True, None)
        sage_pass(nc, m, "sage1", tables[1], tables[2], sage_w[:, 2], sage_w[:, 5], sage_b[:, 2], False, None)
        if stop > 1:
            sage_experts_pass(nc, m, a, tables[2], tables[3], norm_table)
        if stop > 2:
            m.weights.reset()
            m.vectors.reset(keep=m.root_vectors)
            w = m.weights.take(2 * D).rearrange("p (k f) -> p k f", k=2)
            root_row(nc, m, "root1", norm_table, a["L1_gnn_root_idx"], w, True, None, m.root_out[0:NB],
                     Loads([(w, chunks(a["L1_gnn_W2"][D:2 * D]))]))
            conv_pass(nc, m, a, tables[3], tables[4], conv_table)
            m.weights.reset()
            m.vectors.reset(keep=m.root_vectors)
            w = m.weights.take(2 * D).rearrange("p (k f) -> p k f", k=2)
            b = m.vectors.take(D)[0:NB]
            root_row(nc, m, "root2", conv_table, a["L1_gnn_root_idx"], w, False, b, m.root_out[0:NB],
                     Loads([(w, chunks(a["L1_gnn_Wl"][D:2 * D])), (b, across(a["L1_gnn_bl"]))]))
            conv_experts_pass(nc, m, a, tables[4], attention_table, logit_table)
        if stop > 3:
            peak_pass(nc, m, logit_table)
            attention_experts_pass(nc, m, a, attention_table, tables[5])
        if stop > 4:
            edge_conv_experts_pass(nc, m, a, tables[5], out)
        else:
            with nc.Block() as block:
                with nc.semaphore("debug") as dbg:
                    @block.sync
                    def _(sp):
                        sp.dma_start(out.rearrange("(t p) f -> p t f", p=NB), m.x[:, :].rearrange("p (t f) -> p t f", f=D)).then_inc(dbg, 16)
                        sp.wait_ge(dbg, 16)


TURNED = ("L2_ffn_router_w", "L3_gnn_theta_w", "L3_gnn_phi_w")
STOP = 99


def kernel(**inputs):
    import numpy as _np
    import concourse.bacc as _bacc
    from concourse.bass_utils import run_bass_kernel_spmd as _run

    nc = _bacc.Bacc("TRN2", target_bir_lowering=False, num_devices=1)
    arrays, a = {}, {}
    for name, value in inputs.items():
        v = _np.asarray(value)
        v = _np.ascontiguousarray(v.T if name in TURNED else v)
        arrays[f"in_{name}"] = v
        a[name] = nc.dram_tensor(f"in_{name}", v.shape, mybir.dt.from_np(v.dtype), kind="ExternalInput").ap()
    out = nc.dram_tensor("out_0_dram", (N, D), F32, kind="ExternalOutput").ap()
    build(nc, a, out, STOP)
    return _run(nc, [arrays], core_ids=[0]).results[0]["out_0_dram"]
```
